# Optimizing a Trainium2 kernel written in Bass

```python
import numpy as np
import jax
import jax.numpy as jnp

def _softmax(x, axis=-1):
    return jax.nn.softmax(x, axis=axis)

def _gelu(x):
    return jax.nn.gelu(x, approximate=True)

def _silu(x):
    return jax.nn.silu(x)

def _sigmoid(x):
    return jax.nn.sigmoid(x)

def _layernorm(x, axis=-1, eps=1e-05):
    m = jnp.mean(x, axis=axis, keepdims=True)
    v = jnp.var(x, axis=axis, keepdims=True)
    return (x - m) / jnp.sqrt(v + eps)

def _scatter_add(tgt, idx, src, axis=0):
    return tgt.at[idx].add(src)

def _segment_sum(src, seg, n):
    return jax.ops.segment_sum(src, seg, n)
kernel_name = 'mk_macaron_d1_jaxref_r8_677331'

def setup_inputs(seed: int=0):
    np.random.seed(seed)
    _w = jnp.asarray

    def _L0_attn_setup():
        import math
        import jax, jax.numpy as jnp
        import numpy as np
        B, N, D_MODEL, H = (2, 512, 256, 16)
        HEAD_DIM = D_MODEL // H
        CHUNK = 128

        def _slopes(n_heads):
            start = 2.0 ** (-2.0 ** (-(math.log2(n_heads) - 3)))
            return np.array([start ** (i + 1) for i in range(n_heads)], dtype=np.float32)

        def _lightning_attn(q, k, v):
            b, h, n, d = q.shape
            nc = n // CHUNK
            lam = jnp.exp(-jnp.asarray(_slopes(h)))
            pos = jnp.arange(CHUNK, dtype=jnp.float32)
            decay_q = lam[:, None] ** (pos + 1.0)
            decay_k = lam[:, None] ** (CHUNK - 1.0 - pos)
            diff = pos[:, None] - pos[None, :]
            causal = diff >= 0
            dmask = jnp.where(causal, lam[:, None, None] ** jnp.maximum(diff, 0.0), 0.0)
            lam_c = lam ** CHUNK

            def to_chunks(t):
                return t.reshape(b, h, nc, CHUNK, d).transpose(2, 0, 1, 3, 4)
            qc, kc, vc = (to_chunks(q), to_chunks(k), to_chunks(v))

            def step(S, inp):
                qb, kb, vb = inp
                inter = jnp.einsum('bhcd,bhde->bhce', qb * decay_q[None, :, :, None], S)
                scores = jnp.einsum('bhcd,bhed->bhce', qb, kb) * dmask[None]
                intra = jnp.einsum('bhce,bhed->bhcd', scores, vb)
                S_new = lam_c[None, :, None, None] * S + jnp.einsum('bhcd,bhce->bhde', kb * decay_k[None, :, :, None], vb)
                return (S_new, inter + intra)
            S0 = jnp.zeros((b, h, d, d), dtype=q.dtype)
            _, out = jax.lax.scan(step, S0, (qc, kc, vc))
            return out.transpose(1, 2, 0, 3, 4).reshape(b, h, n, d)
        key = jax.random.key(seed)
        kx, k1, k2, k3, k4 = jax.random.split(key, 5)
        scale = 1.0 / math.sqrt(D_MODEL)
        x = jax.random.normal(kx, (B, N, D_MODEL), dtype=jnp.float32)
        w_qkv = jax.random.normal(k1, (3 * D_MODEL, D_MODEL), dtype=jnp.float32) * scale
        b_qkv = jax.random.normal(k2, (3 * D_MODEL,), dtype=jnp.float32) * 0.01
        w_out = jax.random.normal(k3, (D_MODEL, D_MODEL), dtype=jnp.float32) * scale
        b_out = jax.random.normal(k4, (D_MODEL,), dtype=jnp.float32) * 0.01
        return {'x': x, 'w_qkv': w_qkv, 'b_qkv': b_qkv, 'w_out': w_out, 'b_out': b_out}
    _L0_attn_in = _L0_attn_setup()

    def _L0_ffn_setup():
        import jax, jax.numpy as jnp
        import numpy as np
        E, K = (12, 3)
        B, S, H, I = (2, 256, 256, 640)

        def _forward(x, Wr, br, w1, b1, w2, b2, Wp1, bp1, Wp2, bp2):
            logits = jnp.einsum('bsh,he->bse', x, Wr) + br
            probs = jax.nn.softmax(logits, axis=-1)
            top_vals, top_idx = jax.lax.top_k(probs, K)
            ew = jax.nn.softmax(top_vals, axis=-1)
            out = jnp.zeros_like(x)
            for e in range(E):
                sel = top_idx == e
                mask = sel.any(axis=-1)
                cnt = sel.sum()
                w_e = jnp.sum(jnp.where(sel, ew, 0.0)) / jnp.maximum(cnt, 1).astype(ew.dtype)
                h = jax.nn.relu(jnp.einsum('bsh,hi->bsi', x, w1[e]) + b1[e])
                h = jnp.einsum('bsi,ih->bsh', h, w2[e]) + b2[e]
                out = out + mask[..., None].astype(x.dtype) * (w_e * h)
            pooled = out.mean(axis=1)
            phi = jax.nn.sigmoid(jax.nn.relu(pooled @ Wp1 + bp1) @ Wp2 + bp2)
            phi_mask = (phi > 0.7).astype(out.dtype)[:, :, None]
            return out * (1.0 - phi_mask * 0.8)
        key = jax.random.key(seed)
        ks = jax.random.split(key, 8)
        sH = np.float32(1.0 / np.sqrt(H))
        sI = np.float32(1.0 / np.sqrt(I))
        sH2 = np.float32(1.0 / np.sqrt(H // 2))
        return {'hidden_states': jax.random.normal(ks[0], (B, S, H), jnp.float32), 'Wr': jax.random.normal(ks[1], (H, E), jnp.float32) * sH, 'br': jnp.zeros((E,), jnp.float32), 'w1': jax.random.normal(ks[2], (E, H, I), jnp.float32) * sH, 'b1': jnp.zeros((E, I), jnp.float32), 'w2': jax.random.normal(ks[3], (E, I, H), jnp.float32) * sI, 'b2': jnp.zeros((E, H), jnp.float32), 'Wp1': jax.random.normal(ks[4], (H, H // 2), jnp.float32) * sH, 'bp1': jnp.zeros((H // 2,), jnp.float32), 'Wp2': jax.random.normal(ks[5], (H // 2, 1), jnp.float32) * sH2, 'bp2': jnp.zeros((1,), jnp.float32)}
    _L0_ffn_in = _L0_ffn_setup()
    _d = {'L0_attn_x': _L0_attn_in['x'], 'L0_attn_w_qkv': _L0_attn_in['w_qkv'], 'L0_attn_b_qkv': _L0_attn_in['b_qkv'], 'L0_attn_w_out': _L0_attn_in['w_out'], 'L0_attn_b_out': _L0_attn_in['b_out'], 'L0_ffn_Wr': _L0_ffn_in['Wr'], 'L0_ffn_br': _L0_ffn_in['br'], 'L0_ffn_w1': _L0_ffn_in['w1'], 'L0_ffn_b1': _L0_ffn_in['b1'], 'L0_ffn_w2': _L0_ffn_in['w2'], 'L0_ffn_b2': _L0_ffn_in['b2'], 'L0_ffn_Wp1': _L0_ffn_in['Wp1'], 'L0_ffn_bp1': _L0_ffn_in['bp1'], 'L0_ffn_Wp2': _L0_ffn_in['Wp2'], 'L0_ffn_bp2': _L0_ffn_in['bp2']}
    _x0 = _d['L0_attn_x']
    _d['L0_attn_x'] = jax.random.normal(jax.random.fold_in(jax.random.key(seed), 1), (4, 512, 256), dtype=_x0.dtype)
    del _x0
    return _d

def reference(L0_attn_x, L0_attn_w_qkv, L0_attn_b_qkv, L0_attn_w_out, L0_attn_b_out, L0_ffn_Wr, L0_ffn_br, L0_ffn_w1, L0_ffn_b1, L0_ffn_w2, L0_ffn_b2, L0_ffn_Wp1, L0_ffn_bp1, L0_ffn_Wp2, L0_ffn_bp2):

    def _L0_attn_ref(x, w_qkv, b_qkv, w_out, b_out):
        import math
        import jax, jax.numpy as jnp
        import numpy as np
        B, N, D_MODEL, H = (2, 512, 256, 16)
        HEAD_DIM = D_MODEL // H
        CHUNK = 128

        def _slopes(n_heads):
            start = 2.0 ** (-2.0 ** (-(math.log2(n_heads) - 3)))
            return np.array([start ** (i + 1) for i in range(n_heads)], dtype=np.float32)

        def _lightning_attn(q, k, v):
            b, h, n, d = q.shape
            nc = n // CHUNK
            lam = jnp.exp(-jnp.asarray(_slopes(h)))
            pos = jnp.arange(CHUNK, dtype=jnp.float32)
            decay_q = lam[:, None] ** (pos + 1.0)
            decay_k = lam[:, None] ** (CHUNK - 1.0 - pos)
            diff = pos[:, None] - pos[None, :]
            causal = diff >= 0
            dmask = jnp.where(causal, lam[:, None, None] ** jnp.maximum(diff, 0.0), 0.0)
            lam_c = lam ** CHUNK

            def to_chunks(t):
                return t.reshape(b, h, nc, CHUNK, d).transpose(2, 0, 1, 3, 4)
            qc, kc, vc = (to_chunks(q), to_chunks(k), to_chunks(v))

            def step(S, inp):
                qb, kb, vb = inp
                inter = jnp.einsum('bhcd,bhde->bhce', qb * decay_q[None, :, :, None], S)
                scores = jnp.einsum('bhcd,bhed->bhce', qb, kb) * dmask[None]
                intra = jnp.einsum('bhce,bhed->bhcd', scores, vb)
                S_new = lam_c[None, :, None, None] * S + jnp.einsum('bhcd,bhce->bhde', kb * decay_k[None, :, :, None], vb)
                return (S_new, inter + intra)
            S0 = jnp.zeros((b, h, d, d), dtype=q.dtype)
            _, out = jax.lax.scan(step, S0, (qc, kc, vc))
            return out.transpose(1, 2, 0, 3, 4).reshape(b, h, n, d)
        b, n, dm = x.shape
        qkv = x @ w_qkv.T + b_qkv
        q, k, v = jnp.split(qkv, 3, axis=-1)

        def heads(t):
            return t.reshape(b, n, H, HEAD_DIM).transpose(0, 2, 1, 3)
        attn = _lightning_attn(heads(q), heads(k), heads(v))
        attn = attn.transpose(0, 2, 1, 3).reshape(b, n, dm)
        return attn @ w_out.T + b_out

    def _L0_ffn_ref(hidden_states, Wr, br, w1, b1, w2, b2, Wp1, bp1, Wp2, bp2):
        import jax, jax.numpy as jnp
        import numpy as np
        E, K = (12, 3)
        B, S, H, I = (2, 256, 256, 640)

        def _forward(x, Wr, br, w1, b1, w2, b2, Wp1, bp1, Wp2, bp2):
            logits = jnp.einsum('bsh,he->bse', x, Wr) + br
            probs = jax.nn.softmax(logits, axis=-1)
            top_vals, top_idx = jax.lax.top_k(probs, K)
            ew = jax.nn.softmax(top_vals, axis=-1)
            out = jnp.zeros_like(x)
            for e in range(E):
                sel = top_idx == e
                mask = sel.any(axis=-1)
                cnt = sel.sum()
                w_e = jnp.sum(jnp.where(sel, ew, 0.0)) / jnp.maximum(cnt, 1).astype(ew.dtype)
                h = jax.nn.relu(jnp.einsum('bsh,hi->bsi', x, w1[e]) + b1[e])
                h = jnp.einsum('bsi,ih->bsh', h, w2[e]) + b2[e]
                out = out + mask[..., None].astype(x.dtype) * (w_e * h)
            pooled = out.mean(axis=1)
            phi = jax.nn.sigmoid(jax.nn.relu(pooled @ Wp1 + bp1) @ Wp2 + bp2)
            phi_mask = (phi > 0.7).astype(out.dtype)[:, :, None]
            return out * (1.0 - phi_mask * 0.8)
        return _forward(hidden_states, Wr, br, w1, b1, w2, b2, Wp1, bp1, Wp2, bp2)
    x = L0_attn_x
    x = x + 0.5 * _L0_ffn_ref(_layernorm(x, axis=-1), L0_ffn_Wr, L0_ffn_br, L0_ffn_w1, L0_ffn_b1, L0_ffn_w2, L0_ffn_b2, L0_ffn_Wp1, L0_ffn_bp1, L0_ffn_Wp2, L0_ffn_bp2)
    x = x + _L0_attn_ref(_layernorm(x, axis=-1), L0_attn_w_qkv, L0_attn_b_qkv, L0_attn_w_out, L0_attn_b_out)
    x = x + 0.5 * _L0_ffn_ref(_layernorm(x, axis=-1), L0_ffn_Wr, L0_ffn_br, L0_ffn_w1, L0_ffn_b1, L0_ffn_w2, L0_ffn_b2, L0_ffn_Wp1, L0_ffn_bp1, L0_ffn_Wp2, L0_ffn_bp2)
    return x

_drawn_inputs = setup_inputs


def setup_inputs(seed=0):
    import zlib

    import numpy as np

    out = dict(_drawn_inputs(seed))
    spreads = {'L0_ffn_br': (0.0, 0.1),
     'L0_ffn_b1': (0.0, 0.1),
     'L0_ffn_b2': (0.0, 0.1),
     'L0_ffn_bp1': (0.0, 0.1)}
    factors = {'L0_attn_b_qkv': 3.662, 'L0_attn_b_out': 173.584}
    for name, (base, spread) in spreads.items():
        noise = np.random.default_rng([zlib.crc32(name.encode()), seed]).standard_normal(out[name].shape)
        drawn = base * np.exp(spread * noise) if base else spread * noise
        out[name] = jnp.asarray(drawn.astype(out[name].dtype))
    for name, factor in factors.items():
        out[name] = (out[name] * factor).astype(out[name].dtype)
    return out
```

```python
from contextlib import ExitStack

import numpy as np

import concourse.bass as bass
from concourse import mybir

ALU = mybir.AluOpType
ACT = mybir.ActivationFunctionType
AX = mybir.AxisListType
F32 = mybir.dt.float32
F16 = mybir.dt.float16
BF16 = mybir.dt.bfloat16
I32 = mybir.dt.int32
U32 = mybir.dt.uint32

P = 128
B, N, D = 4, 512, 256
T = B * N // P
NC = N // P
E, K, I = 12, 3, 640
KC, IC = D // P, I // P
NB = 60
ASSIGN = T * K
DUMP = 1 << 16
H, HD = 16, 16
RC = B * P
G = 2
EPS = 1e-5
SLOT = 2 * IC * P
X_SCALE = 1024.0
H_SHIFT = 2.0 ** -14

_COLS = [("ident", P), ("tri", P), ("iota_p", P), ("iota_e", E), ("steps", T), ("iota_b", NB),
         ("row", 1), ("reset", E * T), ("even", 1), ("odd", 1), ("decay_chunk", G), ("diag", P),
         ("decay_q", G * P), ("decay_k", D)]
CONST = {}
_at = 0
for _name, _n in _COLS:
    CONST[_name] = (_at, _n)
    _at += _n
CONST_N = _at


def constants():
    c = np.zeros((P, CONST_N), np.float32)

    def put(name, v):
        o, n = CONST[name]
        c[:, o:o + n] = v

    p = np.arange(P)
    put("ident", np.eye(P))
    put("tri", p[:, None] < p[None, :])
    put("iota_p", p[None, :])
    put("iota_e", np.arange(E)[None, :])
    put("steps", P * np.arange(T)[None, :])
    put("iota_b", np.arange(NB)[None, :])
    put("row", p[:, None])
    put("reset", (np.arange(E * T) % T != 0)[None, :])
    put("even", (p // HD % 2 == 0)[:, None])
    put("odd", (p // HD % 2 == 1)[:, None])
    start = 2.0 ** -0.5
    slopes = np.array([start ** (i + 1) for i in range(H)], np.float32)
    lam = np.exp(-slopes.astype(np.float64))
    lg = lam.reshape(G, H // G).repeat(HD, axis=1).T
    put("decay_chunk", lg ** P)
    put("diag", p[:, None] // HD == p[None, :] // HD)
    put("decay_q", (lg[:, :, None] ** (p + 1.0)[None, None, :]).reshape(P, G * P))
    put("decay_k", lam.repeat(HD)[None, :] ** (P - 1.0 - p)[:, None])
    diff = p[None, :] - p[:, None]
    mask = np.where(diff[:, None, :] >= 0, lam[None, :, None] ** np.maximum(diff, 0)[:, None, :], 0.0)
    return c, mask.reshape(P, H * P).astype(np.float32)


class Chain:

    def __init__(self, eng, sem):
        self.eng, self.sem, self.n = eng, sem, 0

    def __call__(self, ins):
        ins.then_inc(self.sem, 1)
        self.n += 1

    def settle(self):
        self.eng.wait_ge(self.sem, self.n)


def build(nc, x, w_qkvT, b_qkv, b_qkT, w_outT, b_out, Wr, br, w1, b1T, w2, b2, Wp1, bp1, Wp2, bp2, cst, dmask,
          xn_dram, rows_dram, out, stop=None):
    ctx = ExitStack()
    with ctx:
        def sb(name, shape, dt=F32):
            return ctx.enter_context(nc.sbuf_tensor(name, shape, dt))

        def sem(name):
            return ctx.enter_context(nc.semaphore(name))

        W1 = sb("W1", [P, (E + 1) * SLOT])
        W2 = sb("W2", [P, (E + 1) * SLOT])
        w1h = W1[:, :].bitcast(F16)
        w2h = W2[:, :].bitcast(F16)
        X = sb("X", [P, T, D])
        C = sb("C", [P, CONST_N])
        Wr_s = sb("Wr_s", [P, KC, E])
        br_s = sb("br_s", [P, E])
        b1_s = sb("b1_s", [P, E * IC])
        b1s = sb("b1s", [P, E * IC])
        Wp1_s = sb("Wp1_s", [P, KC, P])
        bp1_s = sb("bp1_s", [P, 1])
        Wp2_s = sb("Wp2_s", [P, 1])
        Wp2_b = sb("Wp2_b", [P, P])
        bp2_s = sb("bp2_s", [P, 1])
        tri_h = sb("tri_h", [P, P], BF16)
        ones_h = sb("ones_h", [P, P], BF16)
        iota_h = sb("iota_h", [P, P], BF16)
        ones = sb("ones", [P, P])
        eps = sb("eps", [P, 1])
        ss = sb("ss", [P, E * 2])
        ssb = sb("ssb", [P, E])
        dsc = sb("dsc", [P, E])
        n2 = sb("n2", [P, 2])
        ibits = sb("ibits", [P, 2], I32)
        ihalf = sb("ihalf", [P, 2], I32)
        iscl = sb("iscl", [P, 4], I32)
        wscale = sb("wscale", [P, E, 4])
        wsc = sb("wsc", [P, E])
        wexp = sb("wexp", [P, E])
        cntm = sb("cntm", [P, E])[:, :]
        eob = sb("eob", [P, NB], I32)
        token = sb("token", [P, NB], I32)
        place = sb("place", [P, NB], I32)
        tok_q = sb("tok_q", [P, 2], I32)
        place_q = sb("place_q", [P, 2], I32)
        mv = sb("mv", [P, T, 2])
        rstd = sb("rstd", [P, T])
        nmr = sb("nmr", [P, T])
        gate = sb("gate", [P, B])
        pooled = sb("pooled", [P, KC * B])
        phid = sb("phid", [P, B])

        def const(name):
            o, n = CONST[name]
            return C[:, o:o + n]

        ident = const("ident")

        AR = 12832
        A = sb("A", [P, AR])
        top = {"at": 0}

        def carve(n, dt=F32, at=None):
            if at is not None:
                top["at"] = at
            words = n if dt in (F32, I32, U32) else (n + 1) // 2
            o = top["at"]
            top["at"] = o + words
            assert o + words <= AR, (o + words, AR)
            ap = A[:, o:o + words]
            return ap if dt == F32 else ap.bitcast(dt)

        b2w = carve(E * D, at=0)
        bufs_at = top["at"]
        XG = [carve(D) for _ in range(2)]
        XH = [carve(D, F16) for _ in range(2)]
        XL = [carve(D, F16) for _ in range(2)]
        HF = [carve(I) for _ in range(2)]
        HH = [carve(I, F16) for _ in range(2)]
        HL = [carve(I, F16) for _ in range(2)]
        YO = [carve(D) for _ in range(2)]
        blocks_end = top["at"]
        XN = carve(T * D).rearrange("p (i d) -> p i d", i=T)
        O = XN
        xn_at = blocks_end
        XT = [carve(D) for _ in range(2)]
        junk = carve(SLOT, BF16)
        YL = [carve(K * D, at=(bufs_at if q == 0 else None)).rearrange("p (k d) -> p k d", k=K)
              for q in range(2)]
        OHB = carve(ASSIGN * 2 * NB, BF16, at=0).rearrange("p (a n) -> p a n", a=ASSIGN)
        OHA = carve(ASSIGN * P, BF16, at=xn_at).rearrange("p (a n) -> p a n", a=ASSIGN)
        r3 = "p (i e) -> p i e"
        stats = carve(T * 6, at=bufs_at).rearrange("p (i s) -> p i s", i=T)
        CB = A[:, top["at"]:top["at"] + NB * E]
        LG = carve(T * E).rearrange(r3, i=T)
        V8 = carve(T * 8).rearrange(r3, i=T)
        I8 = carve(T * 8, U32).rearrange(r3, i=T)
        DX = carve(T * (E + K)).rearrange(r3, i=T)
        EX = carve(T * (E + K)).rearrange(r3, i=T)
        Z = carve(T)
        RZ = carve(T)
        P3 = carve(T * K).rearrange(r3, i=T)
        D3 = carve(T * K).rearrange(r3, i=T)
        E3 = carve(T * K).rearrange(r3, i=T)
        S3 = carve(T)
        RS3 = carve(T)
        EW = carve(T * K).rearrange(r3, i=T)
        IF = carve(T * K).rearrange(r3, i=T)
        OH = carve(ASSIGN * E)
        OHv = OH.rearrange("p (i k e) -> p i k e", i=T, k=K)
        OW = carve(ASSIGN * E)
        OWv = OW.rearrange("p (i k e) -> p i k e", i=T, k=K)
        M = carve(T * E, BF16)
        EWS = carve(T * E)
        TOT = carve(E * T)
        INC = carve(E * T)
        EXC = carve(E * T)
        POS = carve(T * E)
        CMP = OW[:, 0:E * T]
        NBK = sb("NBK", [P, E])[:, :]
        BINC = carve(E)
        BEX = carve(E)
        DF = carve(ASSIGN)
        DI = carve(ASSIGN, I32)
        DBI = carve(ASSIGN, I32)
        DMI = carve(ASSIGN, I32)
        DB = carve(ASSIGN)
        DM = carve(ASSIGN)
        EOF = carve(NB)
        RF = carve(NB)
        BIG = carve(NB)
        PF = carve(NB)
        assert top["at"] <= blocks_end, (top["at"], blocks_end)

        dmask_s = carve(H * P, at=0).rearrange("p (g r s c) -> p g r s c", g=G, r=4, s=2)
        XNa = carve(B * D).rearrange("p (b d) -> p b d", b=B)
        XTa = carve(KC * RC).rearrange("p (k c) -> p k c", k=KC)
        QE = carve(G * RC).rearrange("p (g c) -> p g c", g=G)
        QO = carve(G * RC).rearrange("p (g c) -> p g c", g=G)
        QD = carve(G * RC).rearrange("p (g c) -> p g c", g=G)
        KT = carve(G * RC).rearrange("p (g c) -> p g c", g=G)
        V = [carve(D) for _ in range(2)]
        KD = [carve(D) for _ in range(2)]
        PM = [carve(D * 4).rearrange("p (r s c) -> p r s c", r=4, s=2) for _ in range(G)]
        S = carve(B * G * P).rearrange("p (b g e) -> p b g e", b=B, g=G)
        TMP = carve(G * P).rearrange("p (g e) -> p g e", g=G)
        AN = carve(D)
        AT = XNa[:, B - 1, :]
        extra1 = W1[:, E * SLOT:(E + 1) * SLOT]
        extra2 = W2[:, E * SLOT:(E + 1) * SLOT]
        wqk_s = extra1[:, 0:KC * 2 * D].rearrange("p (k n) -> p k n", k=KC)
        bo_s = extra1[:, KC * 2 * D:KC * 2 * D + D]
        wv_s = extra2[:, 0:KC * D].rearrange("p (k n) -> p k n", k=KC)
        wo_s = extra2[:, KC * D:2 * KC * D].rearrange("p (k n) -> p k n", k=KC)
        bv_s = extra2[:, 2 * KC * D:2 * KC * D + D]
        bqk_s = sb("bqk_s", [P, 2 * G])
        bk_s = sb("bk_s", [P, D])

        PS = ctx.enter_context(nc.psum_tensor("PS", [P, 8, 512], F32))
        bank = [PS[:, i, :] for i in range(8)]

        x_in = [sem(f"x_in{j}") for j in range(NC)]
        small_in = sem("small_in")
        w_in = [sem(f"w_in{e}") for e in range(E)]
        set_up = sem("set_up")
        squares = sem("squares")
        normed = sem("normed")
        scaled = sem("scaled")
        scale_steps = sem("scale_steps")
        w_hi = sem("w_hi")
        w_lo = sem("w_lo")
        dve_steps = sem("dve_steps")
        var_ready = sem("var_ready")
        sd_ready = sem("sd_ready")
        rstd_ready = sem("rstd_ready")
        xn_dve = sem("xn_dve")
        xn_act = sem("xn_act")
        xn_stored = sem("xn_stored")
        xt_psum = sem("xt_psum")
        xt_copied = sem("xt_copied")
        logits_ready = sem("logits_ready")
        diffs_ready = sem("diffs_ready")
        exps_ready = sem("exps_ready")
        member_ready = sem("member_ready")
        weight_ready = sem("weight_ready")
        counted = sem("counted")
        onehot_ready = sem("onehot_ready")
        table_psum = sem("table_psum")
        table_ready = sem("table_ready")
        b2_in = sem("b2_in")
        w_ready = sem("w_ready")
        b2w_ready = sem("b2w_ready")
        gathered = [sem(f"gathered{q}") for q in range(2)]
        idx_copied = sem("idx_copied")
        pool_held = sem("pool_held")
        transposed = sem("transposed")
        xh_ready = sem("xh_ready")
        xl_ready = sem("xl_ready")
        layer1 = sem("layer1")
        relu_done = sem("relu_done")
        hh_ready = sem("hh_ready")
        hl_ready = sem("hl_ready")
        layer2 = sem("layer2")
        y_ready = sem("y_ready")
        y_sent = [sem(f"y_sent{q}") for q in range(2)]
        y_back = [sem(f"y_back{q}") for q in range(2)]
        o_half = sem("o_half")
        o_ready = sem("o_ready")
        pool_psum = sem("pool_psum")
        pool_ready = sem("pool_ready")
        hid_psum = sem("hid_psum")
        hid_ready = sem("hid_ready")
        phi_psum = sem("phi_psum")
        phi_exp = sem("phi_exp")
        x_out = sem("x_out")
        x_new = sem("x_new")

        attn_w_in = sem("attn_w_in")
        dmask_in = sem("dmask_in")
        a_xn = sem("a_xn")
        a_xb = sem("a_xb")
        a_tp = sem("a_tp")
        a_xt = sem("a_xt")
        a_proj = sem("a_proj")
        a_qk = sem("a_qk")
        a_q = sem("a_q")
        a_qsteps = sem("a_qsteps")
        a_kv = sem("a_kv")
        a_ve = sem("a_ve")
        a_kd = sem("a_kd")
        a_sc = sem("a_sc")
        a_p = sem("a_p")
        a_in = sem("a_in")
        a_st = sem("a_st")
        a_s = sem("a_s")
        a_tmp = sem("a_tmp")
        a_pv = sem("a_pv")
        a_an = sem("a_an")
        a_at = sem("a_at")
        a_atc = sem("a_atc")
        a_out = sem("a_out")
        a_x = sem("a_x")

        FREE = 2
        SMALLS = 10
        DO_ATTN = stop is None

        block = ctx.enter_context(nc.Block())
        x_t = x.rearrange("b (c p) d -> p c b d", p=P)
        out_t = out.rearrange("b (c p) d -> p c b d", p=P)
        Xc = X[:, :, :].rearrange("p (c b) d -> p c b d", b=B)
        xn_t = xn_dram.rearrange("(i p) d -> p i d", p=P)
        rows_t = rows_dram.rearrange("(k i p) d -> p i k d", k=K, p=P)
        calls = (0,) if stop else (0, 1)

        def bcast_row(ap, n):
            return ap.rearrange("(a n) -> a n", a=1).to_broadcast([P, n])

        @block.sync
        def _(sp):
            for j in range(NC):
                sp.dma_start(Xc[:, j], x_t[:, j]).then_inc(x_in[j], 16)
                if j == 0:
                    sp.dma_start(C[:, :], cst).then_inc(small_in, 16)
                    sp.dma_start(Wr_s[:, :, :], Wr.rearrange("(k p) e -> p k e", p=P)).then_inc(small_in, 16)
                    sp.dma_start(br_s[:, :], bcast_row(br, E)).then_inc(small_in, 16)
                    sp.dma_start(b1_s[:, :], b1T).then_inc(small_in, 16)
            for e in range(E):
                sp.dma_start(W1[:, (e + 1) * SLOT:(e + 2) * SLOT].rearrange("p (k i) -> p k i", k=KC),
                             w1[e].rearrange("(k p) i -> p k i", p=P)).then_inc(w_in[e], 16)
                sp.dma_start(W2[:, (e + 1) * SLOT:(e + 2) * SLOT].rearrange("p (c h) -> p c h", c=IC),
                             w2[e].rearrange("(c p) h -> p c h", p=P)).then_inc(w_in[e], 16)
                if e == 0:
                    sp.dma_start(Wp1_s[:, :, :], Wp1.rearrange("(k p) j -> p k j", p=P)).then_inc(small_in, 16)
                    sp.dma_start(bp1_s[:, :], bp1.rearrange("(p a) -> p a", a=1)).then_inc(small_in, 16)
                    sp.dma_start(Wp2_s[:, :], Wp2).then_inc(small_in, 16)
                    sp.dma_start(bp2_s[:, :], bcast_row(bp2, 1)).then_inc(small_in, 16)
            def load_attention():
                sp.wait_ge(w_lo, 2 + 2 * E)
                for k in range(KC):
                    rows = w_qkvT[k * P:(k + 1) * P, :]
                    sp.dma_start(wqk_s[:, k, :], rows[:, 0:2 * D]).then_inc(attn_w_in, 16)
                    sp.dma_start(wv_s[:, k, :], rows[:, 2 * D:3 * D]).then_inc(attn_w_in, 16)
                    sp.dma_start(wo_s[:, k, :], w_outT[k * P:(k + 1) * P, :]).then_inc(attn_w_in, 16)
                sp.dma_start(bo_s, bcast_row(b_out, D)).then_inc(attn_w_in, 16)
                sp.dma_start(bk_s[:, :], bcast_row(b_qkv[D:2 * D], D)).then_inc(attn_w_in, 16)
                sp.dma_start(bv_s, bcast_row(b_qkv[2 * D:3 * D], D)).then_inc(attn_w_in, 16)
                sp.dma_start(bqk_s[:, :], b_qkT).then_inc(attn_w_in, 16)

            for f in calls:
                for g in range(4):
                    sp.wait_ge(xn_dve, 8 * f + 2 * (g + 1))
                    sp.wait_ge(xn_act, 8 * f + 2 * (g + 1))
                    sp.dma_start(xn_t[:, 4 * g:4 * g + 4, :], XN[:, 4 * g:4 * g + 4, :]).then_inc(xn_stored, 16)
                sp.wait_ge(table_psum, f + 1)
                sp.dma_start(b2w, b2.rearrange("(a e) h -> a (e h)", a=1).to_broadcast([P, E * D])).then_inc(b2_in, 16)
                for q in range(2):
                    sp.wait_ge(y_sent[q], 16 * (NB // 2) * (f + 1))
                if f == 0 and stop != "ffn":
                    load_attention()
                for i in range(T):
                    if i >= 2:
                        sp.wait_ge(o_ready, T * f + i - 1)
                    sp.dma_start(YL[i % 2], rows_t[:, i]).then_inc(y_back[i % 2], 16)
                if f == 0 and stop != "ffn":
                    sp.wait_ge(x_new, T)
                    sp.dma_start(dmask_s, dmask).then_inc(dmask_in, 16)
            for c in range(NC):
                if stop == "attn":
                    sp.wait_ge(a_x, 1 + T)
                sp.wait_ge(x_new, T * (len(calls) - 1) + B * (c + 1))
                sp.dma_start(out_t[:, c], Xc[:, c]).then_inc(x_out, 16)
            sp.wait_ge(x_out, 16 * NC)

        def scale_of(e, n):
            return wscale[:, bass.ds(e, 1), n:n + 1].rearrange("p a b -> p (a b)")

        @block.gpsimd
        def _(pool):
            for e in range(E):
                pool.wait_ge(scaled, e + 2)
                for n, (raw, half) in enumerate(((W1, w1h), (W2, w2h))):
                    pool.wait_ge(w_lo, 2 * e + n + 1)
                    nc.gpsimd.tensor_scalar(half[:, e * 2 * SLOT:e * 2 * SLOT + SLOT],
                                            raw[:, (e + 1) * SLOT:(e + 2) * SLOT],
                                            wscale[:, e, n:n + 1], None, ALU.mult).then_inc(w_hi, 1)

            def gather(f, b, q):
                pool.wait_ge(transposed, f * NB + b + 1)
                pool.sem_inc(pool_held, 1)
                nc.gpsimd.tensor_copy(tok_q[:, q:q + 1], token[:, bass.ds(b, 1)]).then_inc(idx_copied, 1)
                pool.wait_ge(idx_copied, idx(f, b, 0))
                pool.sem_inc(pool_held, 1)
                nc.gpsimd.indirect_dma_start(XG[q], None, xn_dram[:, :],
                                             bass.IndirectOffsetOnAxis(ap=tok_q[:, q:q + 1], axis=0)
                                             ).then_inc(gathered[q], 16)

            def scatter(f, b, q):
                pool.wait_ge(y_ready, FREE + f * NB + b + 1)
                pool.sem_inc(pool_held, 1)
                nc.gpsimd.tensor_copy(place_q[:, q:q + 1], place[:, bass.ds(b, 1)]).then_inc(idx_copied, 1)
                pool.wait_ge(idx_copied, idx(f, b, 1))
                pool.sem_inc(pool_held, 1)
                nc.gpsimd.indirect_dma_start(rows_dram[:, :],
                                             bass.IndirectOffsetOnAxis(ap=place_q[:, q:q + 1], axis=0),
                                             YO[q], None, bounds_check=K * T * P - 1, oob_is_err=False,
                                             ).then_inc(y_sent[q], 16)

            LAG = 4

            def idx(f, b, kind):
                if kind == 0:
                    if isinstance(b, int) and b < LAG:
                        return 2 * NB * f + b + 1
                    return b * 2 + (2 * NB * f - LAG + 1)
                if isinstance(b, int) and b >= NB - LAG:
                    return 2 * NB * f + NB + b + 1
                return b * 2 + (2 * NB * f + LAG + 2)

            for f in calls:
                pool.wait_ge(table_ready, f + 1)
                pool.wait_ge(xn_stored, 64 * (f + 1))
                for b in range(LAG):
                    if b == 2:
                        pool.wait_ge(b2_in, 16 * (f + 1))
                        pool.wait_ge(w_ready, f + 1)
                        v = b2w.rearrange("p (e h) -> p e h", e=E)
                        nc.gpsimd.tensor_tensor(v, v, wexp[:, :].unsqueeze(2).to_broadcast([P, E, D]),
                                                ALU.mult).then_inc(b2w_ready, 1)
                    gather(f, b, b % 2)
                with pool.Fori(0, (NB - LAG) // 2) as j:
                    for q in range(2):
                        gather(f, j * 2 + (LAG + q), q)
                        scatter(f, j * 2 + q, q)
                for b in range(NB - LAG, NB):
                    scatter(f, b, b % 2)
                if f == 0 and stop != "ffn":
                    pool.wait_ge(attn_w_in, 16 * 10)
                    with pool.Fori(0, T) as t:
                        pool.wait_ge(a_xn, t + 1)
                        pool.sem_inc(pool_held, 1)
                        xi = X[:, bass.ds(t, 1), :].rearrange("p a d -> p (a d)")
                        nc.gpsimd.tensor_tensor(xi, xi, bo_s, ALU.add).then_inc(a_xb, 1)

        @block.scalar
        def _(act):
            def square_sums():
                for e in range(E):
                    act.wait_ge(w_in[e], 32)
                    for n, raw in enumerate((W1, W2)):
                        if e or n:
                            act.wait_ge(squares, 2 * e + n)
                        ins = nc.scalar.activation(junk, raw[:, (e + 1) * SLOT:(e + 2) * SLOT], ACT.Square,
                                                   accum_out=ss[:, 2 * e + n:2 * e + n + 1])
                        ins.then_inc(squares, 1)

            def deviation(n):
                act.wait_ge(var_ready, n + 1)
                nc.scalar.activation(rstd[:, :], nmr[:, :], ACT.Sqrt).then_inc(sd_ready, 1)
                act.wait_ge(rstd_ready, n + 1)

            def attention():
                deviation(1)
                act.wait_ge(attn_w_in, 16 * 10)
                with act.Fori(0, NC) as c:
                    for b in range(B):
                        t = c * B + b
                        act.wait_ge(a_tp, t + 1)
                        if b == B - 1:
                            act.wait_ge(a_out, c * B + 1)
                        nc.scalar.activation(XNa[:, b, :], X[:, bass.ds(t, 1), :].rearrange("p a d -> p (a d)"),
                                             ACT.Identity, bias=nmr[:, bass.ds(t, 1)],
                                             scale=rstd[:, bass.ds(t, 1)]).then_inc(a_xn, 1)
                    act.wait_ge(a_kv, c * B + 1)
                    for b in range(B):
                        t = c * B + b
                        act.wait_ge(a_tp, t + 5)
                        nc.scalar.copy(XTa[:, :, b * P:(b + 1) * P],
                                       bank[b][:, 0:D].rearrange("p (k c) -> p k c", k=KC)).then_inc(a_xt, 1)
                    act.wait_ge(a_sc, c * (2 * B) + 1)
                    for n, dst in enumerate((QE[:, 0], QE[:, 1], KT[:, 0], KT[:, 1])):
                        act.wait_ge(a_proj, c * 4 + (n + 1))
                        nc.scalar.activation(dst, bank[n], ACT.Identity, bias=bqk_s[:, n:n + 1]).then_inc(a_qk, 1)

                    def rows_out(b):
                        t = c * B + b
                        act.wait_ge(a_pv, t * 2 + 6)
                        act.wait_ge(a_at, t + 1)
                        nc.scalar.copy(AN, bank[6][:, 0:D]).then_inc(a_an, 1)
                        act.wait_ge(a_at, t + 2)
                        act.wait_ge(a_out, t + 1)
                        nc.scalar.copy(AT, bank[7][:, 0:D]).then_inc(a_atc, 1)

                    for b in range(B):
                        rows_out(b)

            def routing(f):
                deviation(2 * f)
                for i in range(1, T, 2):
                    nc.scalar.activation(XN[:, i, :], X[:, i, :], ACT.Identity, bias=nmr[:, i:i + 1],
                                         scale=rstd[:, i:i + 1]).then_inc(xn_act, 1)
                for i in range(T):
                    act.wait_ge(xt_psum, T * f + i + 1)
                    if i >= 2:
                        act.wait_ge(logits_ready, T * f + i - 1)
                    nc.scalar.copy(XT[i % 2], bank[4 + i % 2][:, 0:D]).then_inc(xt_copied, 1)
                for n in range(2):
                    act.wait_ge(diffs_ready, 2 * f + n + 1)
                    src, dst = ((DX, EX), (D3, E3))[n]
                    nc.scalar.activation(dst, src, ACT.Exp).then_inc(exps_ready, 1)

            def blocks(f):
                def high(b, q):
                    act.wait_ge(transposed, FREE + f * NB + b + 1)
                    act.wait_ge(layer1, f * NB + b + 1)
                    nc.scalar.mul(XH[q], bank[6 + q][:, 0:D], X_SCALE).then_inc(xh_ready, 1)

                def relu(b, q):
                    e = act.value_load(eob[0:1, bass.ds(b, 1)], min_val=0, max_val=E - 1)
                    act.wait_ge(layer1, FREE + f * NB + b + 1)
                    act.wait_ge(hl_ready, f * NB + b + 1)
                    for c in range(IC):
                        ins = nc.scalar.activation(HF[q][:, c * P:(c + 1) * P],
                                                   bank[2 * q + c // 4][:, c % 4 * P:(c % 4 + 1) * P],
                                                   ACT.Relu, bias=b1s[:, bass.ds(e * IC + c, 1)],
                                                   scale=H_SHIFT)
                    ins.then_inc(relu_done, 1)

                high(0, 0)
                with act.Fori(0, (NB - 2) // 2) as j:
                    for q in range(2):
                        high(j * 2 + (q + 1), 1 - q)
                        relu(j * 2 + q, q)
                high(NB - 1, 1)
                relu(NB - 2, 0)
                relu(NB - 1, 1)

            def combine(f):
                act.wait_ge(hid_psum, f + 1)
                nc.scalar.activation(phid[:, :], bank[2][:, 0:B], ACT.Relu, bias=bp1_s[:, :]).then_inc(hid_ready, 1)
                act.wait_ge(phi_psum, f + 1)
                nc.scalar.activation(gate[:, :], bank[3][:, 0:B], ACT.Exp, bias=bp2_s[:, :],
                                     scale=-1.0).then_inc(phi_exp, 1)

            act.sem_inc(relu_done, FREE)
            act.sem_inc(a_an, 1)
            act.wait_ge(small_in, 16 * 8)
            for f in calls:
                routing(f)
                if f == 0:
                    square_sums()
                blocks(f)
                combine(f)
                if f == 0 and stop != "ffn":
                    attention()

        @block.tensor
        def _(pe):
            def matmul(out_, l, r, start, stop_):
                return nc.tensor.matmul(out_, l, r, start=start, stop=stop_, skip_group_check=True)

            def norms():
                with pe.Fori(0, E) as e:
                    pe.wait_ge(squares, e * 2 + 2)
                    pe.wait_ge(scaled, e + 1)
                    matmul(bank[6][:, 0:2], ones[:, :], ss[:, bass.ds(e * 2, 2)], True, False)
                    matmul(bank[6][:, 0:1], ones[:, :], ssb[:, bass.ds(e, 1)], False, True).then_inc(normed, 1)

            def routing(f):
                for i in range(T + 1):
                    if i < T:
                        if i % 2 == 0:
                            pe.wait_ge(xn_dve, 8 * f + i // 2 + 1)
                        else:
                            pe.wait_ge(xn_act, 8 * f + i // 2 + 1)
                        if i >= 2:
                            pe.wait_ge(xt_copied, T * f + i - 1)
                        for k in range(KC):
                            ins = nc.tensor.transpose(bank[4 + i % 2][:, k * P:(k + 1) * P],
                                                      XN[:, i, k * P:(k + 1) * P], ident)
                        ins.then_inc(xt_psum, 1)
                    if i >= 1:
                        pe.wait_ge(xt_copied, T * f + i)
                        for k in range(KC):
                            ins = matmul(bank[0][:, (i - 1) * E:i * E], XT[(i - 1) % 2][:, k * P:(k + 1) * P],
                                         Wr_s[:, k, :], k == 0, k == KC - 1)
                        ins.then_inc(logits_ready, 1)
                pe.wait_ge(member_ready, f + 1)
                matmul(bank[1][:, 0:T * E], tri_h[:, :], M, True, True)
                matmul(bank[1][:, 256:256 + T * E], ones_h[:, :], M, True, True).then_inc(counted, 1)
                pe.wait_ge(weight_ready, f + 1)
                matmul(bank[2][:, 0:T * E], ones[:, :], EWS, True, True).then_inc(counted, 1)
                for g in range(4):
                    pe.wait_ge(onehot_ready, 4 * f + g + 1)
                    for a in range(12 * g, 12 * g + 12):
                        ins = matmul(bank[3][:, 0:2 * NB], OHA[:, a, :], OHB[:, a, :], a == 0, a == ASSIGN - 1)
                ins.then_inc(table_psum, 1)

            def blocks(f):
                def transposes(b, q):
                    pe.wait_ge(gathered[q], gcount(f, b, q))
                    pe.wait_ge(xl_ready, f * NB + b + 1)
                    for k in range(KC):
                        ins = nc.tensor.transpose(bank[6 + q][:, k * P:(k + 1) * P], XG[q][:, k * P:(k + 1) * P], ident)
                    ins.then_inc(transposed, 1)

                def first(b, q):
                    e = pe.value_load(eob[0:1, bass.ds(b, 1)], min_val=0, max_val=E - 1)
                    pe.wait_ge(xl_ready, FREE + f * NB + b + 1)
                    pe.wait_ge(relu_done, f * NB + b + 1)
                    for c in range(IC):
                        dst = bank[2 * q + c // 4][:, c % 4 * P:(c % 4 + 1) * P]
                        n = 0
                        for k in range(KC):
                            for part, src in ((0, XH), (0, XL), (1, XH)):
                                w = w1h[:, bass.ds(e * (2 * SLOT) + (part * SLOT + k * I + c * P), P)]
                                ins = matmul(dst, w, src[q][:, k * P:(k + 1) * P], n == 0, n == 5)
                                n += 1
                    ins.then_inc(layer1, 1)

                def second(b, q):
                    e = pe.value_load(eob[0:1, bass.ds(b, 1)], min_val=0, max_val=E - 1)
                    pe.wait_ge(hl_ready, FREE + f * NB + b + 1)
                    pe.wait_ge(y_ready, f * NB + b + 1)
                    n = 0
                    for c in range(IC):
                        for part, src in ((0, HH), (0, HL), (1, HH)):
                            w = w2h[:, bass.ds(e * (2 * SLOT) + (part * SLOT + c * D), D)]
                            ins = matmul(bank[4 + q][:, 0:D], src[q][:, c * P:(c + 1) * P], w, n == 0, n == 14)
                            n += 1
                    ins.then_inc(layer2, 1)

                if f == 0:
                    pe.wait_ge(w_lo, 2 + 2 * E)
                transposes(0, 0)
                transposes(1, 1)
                first(0, 0)
                with pe.Fori(0, (NB - 2) // 2) as j:
                    for u in range(2):
                        transposes(j * 2 + (u + 2), u)
                        first(j * 2 + (u + 1), 1 - u)
                        second(j * 2 + u, u)
                first(NB - 1, 1)
                second(NB - 2, 0)
                second(NB - 1, 1)

            def gcount(f, b, q):
                base = 16 * (f * NB // 2 + 1)
                return (b - q) // 2 * 16 + base if isinstance(b, int) else (b - q) * 8 + base

            def combine(f):
                pe.wait_ge(o_ready, T * (f + 1))
                n = 0
                for k in range(KC):
                    for b in range(B):
                        for c in range(NC):
                            col = k * B + b
                            ins = matmul(bank[1][:, col:col + 1], O[:, c * B + b, k * P:(k + 1) * P],
                                         ones[:, 0:1], c == 0, c == NC - 1)
                ins.then_inc(pool_psum, 1)
                pe.wait_ge(pool_ready, f + 1)
                for k in range(KC):
                    ins = matmul(bank[2][:, 0:B], Wp1_s[:, k, :], pooled[:, k * B:(k + 1) * B], k == 0, k == KC - 1)
                ins.then_inc(hid_psum, 1)
                pe.wait_ge(hid_ready, f + 1)
                matmul(bank[3][:, 0:B], Wp2_b[:, :], phid[:, :], True, True).then_inc(phi_psum, 1)

            def attention():
                pe.wait_ge(attn_w_in, 16 * 10)
                with pe.Fori(0, NC) as c:
                    pe.wait_ge(a_p, c * (2 * B) + 1)
                    for b in range(B):
                        pe.wait_ge(a_xn, c * B + (b + 1))
                        for k in range(KC):
                            ins = nc.tensor.transpose(bank[b][:, k * P:(k + 1) * P],
                                                      XNa[:, b, k * P:(k + 1) * P], ident)
                        ins.then_inc(a_tp, 1)
                    pe.wait_ge(a_xt, c * B + B)
                    for n in range(4):
                        for k in range(KC):
                            ins = matmul(bank[n], wqk_s[:, k, n * P:(n + 1) * P], XTa[:, k, :], k == 0, k == KC - 1)
                        ins.then_inc(a_proj, 1)

                    def keys_values(b):
                        pe.wait_ge(a_ve, c * B + (b + 1))
                        for k in range(KC):
                            matmul(bank[4][:, 0:D], XTa[:, k, b * P:(b + 1) * P], wqk_s[:, k, D:2 * D],
                                   k == 0, k == KC - 1)
                        for k in range(KC):
                            ins = matmul(bank[4][:, D:2 * D], XTa[:, k, b * P:(b + 1) * P], wv_s[:, k, :],
                                         k == 0, k == KC - 1)
                        ins.then_inc(a_kv, 1)

                    def scores(b, g):
                        pe.wait_ge(a_p, c * (2 * B) + (2 * b + g + 1))
                        for s in range(2):
                            q = (QE, QO)[s]
                            for r in range(4):
                                rows = slice(32 * r, 32 * r + 32)
                                ins = matmul(bank[r][:, s * P:(s + 1) * P], KT[rows, g, b * P:(b + 1) * P],
                                             q[rows, g, b * P:(b + 1) * P], True, True)
                        ins.then_inc(a_sc, 1)

                    def from_state(b):
                        pe.wait_ge(a_s, c * B + (b + 1))
                        pe.wait_ge(a_an, c * B + (b + 1))
                        for g in range(G):
                            ins = matmul(bank[6][:, g * P:(g + 1) * P], QD[:, g, b * P:(b + 1) * P], S[:, b, g, :],
                                         g == 0, False)
                        ins.then_inc(a_in, 1)

                    def from_chunk(b, g):
                        pe.wait_ge(a_p, c * (2 * B) + (2 * b + g + 2))
                        for r in range(4):
                            for s in range(2):
                                h = 8 * g + 2 * r + s
                                ins = matmul(bank[6][:, h * HD:(h + 1) * HD], PM[g][:, r, s, :],
                                             V[b % 2][:, h * HD:(h + 1) * HD], False, h == H - 1)
                        ins.then_inc(a_pv, 1)

                    def state(b):
                        pe.wait_ge(a_kd, c * B + (b + 1))
                        pe.wait_ge(a_s, c * B + (b + 4))
                        for g in range(G):
                            ins = matmul(bank[5][:, g * P:(g + 1) * P], KD[b % 2][:, g * P:(g + 1) * P],
                                         V[b % 2][:, g * P:(g + 1) * P], True, True)
                        ins.then_inc(a_st, 1)

                    def rows_transposed(b):
                        pe.wait_ge(a_an, c * B + (b + 2))
                        pe.wait_ge(a_x, c * B + (b + 1))
                        for k in range(KC):
                            ins = nc.tensor.transpose(bank[7][:, k * P:(k + 1) * P], AN[:, k * P:(k + 1) * P], ident)
                        ins.then_inc(a_at, 1)

                    def out_proj(b):
                        pe.wait_ge(a_atc, c * B + (b + 1))
                        for k in range(KC):
                            ins = matmul(bank[7][:, D:2 * D], AT[:, k * P:(k + 1) * P], wo_s[:, k, :],
                                         k == 0, k == KC - 1)
                        ins.then_inc(a_out, 1)

                    pe.wait_ge(a_q, c + 1)
                    pe.wait_ge(a_qk, c * 4 + 4)
                    for b in range(B):
                        keys_values(b)
                        scores(b, 0)
                        if b:
                            rows_transposed(b - 1)
                        from_state(b)
                        scores(b, 1)
                        if b:
                            out_proj(b - 1)
                        state(b)
                        from_chunk(b, 0)
                        from_chunk(b, 1)
                    rows_transposed(B - 1)
                    out_proj(B - 1)

            pe.sem_inc(a_tp, 4)
            pe.sem_inc(a_kv, 1)
            pe.sem_inc(a_sc, 1)
            pe.sem_inc(a_pv, 4)
            pe.sem_inc(a_at, 1)
            pe.sem_inc(a_out, 1)
            pe.sem_inc(a_in, 1)
            pe.sem_inc(transposed, FREE)
            pe.sem_inc(layer1, FREE)
            pe.sem_inc(layer2, FREE)
            pe.wait_ge(set_up, 1)
            for f in calls:
                routing(f)
                if f == 0:
                    norms()
                blocks(f)
                combine(f)
                if f == 0 and stop != "ffn":
                    attention()

        @block.vector
        def _(dve):
            step = Chain(dve, dve_steps)

            def set_up_tables():
                dve.wait_ge(small_in, 16 * 8)
                v = nc.vector
                v.memset(ones[:, :], 1.0)
                v.memset(ones_h[:, :], 1.0)
                v.tensor_copy(tri_h[:, :], const("tri"))
                v.tensor_copy(iota_h[:, :], const("iota_p"))
                v.memset(eps[:, :], EPS)
                v.tensor_scalar(bp2_s[:, :], bp2_s[:, :], -1.0, None, ALU.mult)
                step(v.tensor_tensor(b1s[:, :], b1_s[:, :], b1_s[:, :], ALU.mult))
                step(v.tensor_copy(Wp2_b[:, :], Wp2_s[:, :].to_broadcast([P, P])))
                step.settle()
                v.tensor_reduce(ssb[:, :], b1s[:, :].rearrange("p (e c) -> p e c", c=IC), AX.X,
                                ALU.add).then_inc(set_up, 1)

            def scales():
                v = nc.vector
                with dve.Fori(0, E) as e:
                    base = e * 6
                    dve.wait_ge(normed, e + 1)
                    v.tensor_scalar(n2[:, :], bank[6][:, 0:2], 1e-30, None, ALU.max).then_inc(scale_steps, 1)
                    dve.wait_ge(scale_steps, base + 1)
                    v.tensor_scalar(ibits[:, :], n2[:, :].bitcast(I32), 23, None,
                                    ALU.logical_shift_right).then_inc(scale_steps, 1)
                    dve.wait_ge(scale_steps, base + 2)
                    v.tensor_scalar(ihalf[:, :], ibits[:, :], 1.0, None, ALU.add).then_inc(scale_steps, 1)
                    dve.wait_ge(scale_steps, base + 3)
                    v.tensor_scalar(ibits[:, :], ihalf[:, :], 1, None,
                                    ALU.logical_shift_right).then_inc(scale_steps, 1)
                    dve.wait_ge(scale_steps, base + 4)
                    v.tensor_scalar(iscl[:, 0:2], ibits[:, :], -1.0, 205.0, ALU.mult, ALU.add)
                    v.tensor_scalar(iscl[:, 2:4], ibits[:, :], 49.0, None, ALU.add).then_inc(scale_steps, 1)
                    dve.wait_ge(scale_steps, base + 5)
                    ws = wscale[:, bass.ds(e, 1), :].rearrange("p a n -> p (a n)")
                    v.tensor_scalar(ws.bitcast(I32), iscl[:, :], 23, None,
                                    ALU.logical_shift_left).then_inc(scaled, 1)
                    dve.wait_ge(scaled, e + 2)
                    w0 = wscale[:, bass.ds(e, 1), 0:1].rearrange("p a n -> p (a n)")
                    v.tensor_scalar(b1s[:, bass.ds(e * IC, IC)], b1_s[:, bass.ds(e * IC, IC)], w0,
                                    X_SCALE * H_SHIFT, ALU.mult, ALU.mult)
                    v.scalar_tensor_tensor(dsc[:, bass.ds(e, 1)],
                                           wscale[:, bass.ds(e, 1), 2:3].rearrange("p a n -> p (a n)"),
                                           1.0 / (X_SCALE * H_SHIFT),
                                           wscale[:, bass.ds(e, 1), 3:4].rearrange("p a n -> p (a n)"),
                                           ALU.mult, ALU.mult).then_inc(scale_steps, 1)
                    for n, (raw, half) in enumerate(((W1, w1h), (W2, w2h))):
                        dve.wait_ge(w_hi, 2 * e + n + 1)
                        v.scalar_tensor_tensor(half[:, bass.ds(e * (2 * SLOT) + SLOT, SLOT)],
                                               raw[:, bass.ds(e * SLOT + SLOT, SLOT)],
                                               wscale[:, bass.ds(e, 1), n:n + 1].rearrange("p a n -> p (a n)"),
                                               half[:, bass.ds(e * (2 * SLOT), SLOT)],
                                               ALU.mult, ALU.subtract).then_inc(w_lo, 1)
                dve.wait_ge(scale_steps, 6 * E)
                dve.wait_ge(w_lo, 2 + 2 * E)

            def row_stats(n):
                v = nc.vector
                for i in range(T):
                    if n == 0 and i % B == 0:
                        dve.wait_ge(x_in[i // B], 16)
                    step(v.bn_stats(stats[:, i, :], X[:, i, :]))
                step.settle()
                for i in range(T):
                    step(v.bn_aggr(mv[:, i, :], stats[:, i, :]))
                step.settle()
                v.tensor_scalar(nmr[:, :], mv[:, :, 1], EPS, None, ALU.add).then_inc(var_ready, 1)
                dve.wait_ge(sd_ready, n + 1)
                step(v.reciprocal(rstd[:, :], rstd[:, :]))
                step.settle()
                v.scalar_tensor_tensor(nmr[:, :], mv[:, :, 0], -1.0, rstd[:, :], ALU.mult,
                                       ALU.mult).then_inc(rstd_ready, 1)
                dve.wait_ge(rstd_ready, n + 1)

            def routing(f):
                v = nc.vector
                row_stats(2 * f)
                for i in range(0, T, 2):
                    v.tensor_scalar(XN[:, i, :], X[:, i, :], rstd[:, i:i + 1], nmr[:, i:i + 1],
                                    ALU.mult, ALU.add).then_inc(xn_dve, 1)
                dve.wait_ge(logits_ready, T * (f + 1))
                step(v.tensor_tensor(LG, bank[0][:, 0:T * E].rearrange(r3, i=T),
                                     br_s[:, :].unsqueeze(1).to_broadcast([P, T, E]), ALU.add))
                step.settle()
                for i in range(T):
                    step(v.max(V8[:, i, :], LG[:, i, :]))
                step.settle()
                for i in range(T):
                    step(v.max_index(I8[:, i, :], V8[:, i, :], LG[:, i, :]))
                top1 = V8[:, :, 0:1]
                v.tensor_tensor(DX[:, :, E:E + K], V8[:, :, 0:K], top1.to_broadcast([P, T, K]), ALU.subtract)
                v.tensor_tensor(DX[:, :, 0:E], LG, top1.to_broadcast([P, T, E]),
                                ALU.subtract).then_inc(diffs_ready, 1)
                step.settle()
                step(v.tensor_copy(IF, I8[:, :, 0:K]))
                step.settle()
                step(v.tensor_tensor(OHv, IF.unsqueeze(3).to_broadcast([P, T, K, E]),
                                     const("iota_e").unsqueeze(1).unsqueeze(1).to_broadcast([P, T, K, E]),
                                     ALU.is_equal))
                step.settle()
                with nc.allow_low_precision(reason="sums of zeros and at most one one"):
                    v.tensor_reduce(M, OHv.rearrange("p i k e -> p i e k"), AX.X, ALU.add).then_inc(member_ready, 1)
                dve.wait_ge(exps_ready, 2 * f + 1)
                step(v.tensor_reduce(Z, EX[:, :, 0:E], AX.X, ALU.add))
                step.settle()
                step(v.reciprocal(RZ, Z))
                step.settle()
                step(v.tensor_tensor(P3, EX[:, :, E:E + K], RZ.unsqueeze(2).to_broadcast([P, T, K]), ALU.mult))
                step.settle()
                v.tensor_tensor(D3, P3, P3[:, :, 0:1].to_broadcast([P, T, K]),
                                ALU.subtract).then_inc(diffs_ready, 1)
                dve.wait_ge(counted, 2 * f + 1)
                step(v.tensor_copy(TOT.rearrange("p (e i) -> p e i", e=E),
                                   bank[1][:, 256:256 + T * E].rearrange("p (i e) -> p e i", e=E)))
                step.settle()
                step(v.tensor_tensor_scan(INC, const("reset"), TOT, 0.0, ALU.mult, ALU.add))
                step.settle()
                cnt = INC.rearrange("p (e i) -> p e i", e=E)[:, :, T - 1:T]
                step(v.tensor_tensor(EXC, INC, TOT, ALU.subtract))
                step(v.tensor_tensor(CMP.rearrange("p (e i) -> p e i", e=E), cnt.to_broadcast([P, E, T]),
                                     const("steps").unsqueeze(1).to_broadcast([P, E, T]), ALU.is_gt))
                step.settle()
                step(v.tensor_reduce(NBK, CMP.rearrange("p (e i) -> p e i", e=E), AX.X, ALU.add))
                step.settle()
                step(v.tensor_tensor_scan(BINC, ones[:, 0:E], NBK, 0.0, ALU.mult, ALU.add))
                step.settle()
                step(v.tensor_tensor(BEX, BINC, NBK, ALU.subtract))
                step.settle()
                e3 = EXC.rearrange("p (e i) -> p e i", e=E)
                step(v.scalar_tensor_tensor(e3, BEX.unsqueeze(2).to_broadcast([P, E, T]), float(P), e3,
                                            ALU.mult, ALU.add))
                step.settle()
                step(v.tensor_tensor(POS.rearrange(r3, i=T), bank[1][:, 0:T * E].rearrange(r3, i=T),
                                     EXC.rearrange("p (e i) -> p i e", e=E), ALU.add))
                step.settle()
                step(v.tensor_tensor(OWv, OHv, POS.rearrange(r3, i=T).unsqueeze(2).to_broadcast([P, T, K, E]),
                                     ALU.mult))
                step.settle()
                step(v.tensor_reduce(DF, OW.rearrange("p (a e) -> p a e", e=E), AX.X, ALU.add))
                step.settle()
                step(v.tensor_copy(DI, DF))
                step.settle()
                step(v.tensor_scalar(DBI, DI, 7, None, ALU.logical_shift_right))
                step(v.tensor_scalar(DMI, DI, P - 1, None, ALU.bitwise_and))
                step.settle()
                step(v.tensor_copy(DB, DBI))
                step(v.tensor_copy(DM, DMI))
                step.settle()
                dve.wait_ge(xn_stored, 64 * (f + 1))
                dve.wait_ge(xt_psum, T * (f + 1))
                for a in range(ASSIGN):
                    i, k = a // K, a % K
                    v.tensor_scalar(OHA[:, a, :], iota_h[:, :], DM[:, a:a + 1], None, ALU.is_equal)
                    v.tensor_scalar(OHB[:, a, 0:NB], const("iota_b"), DB[:, a:a + 1], const("row"),
                                    ALU.is_equal, ALU.mult)
                    ins = v.tensor_scalar(OHB[:, a, NB:2 * NB], const("iota_b"), DB[:, a:a + 1],
                                          float(T * k + i + 1), ALU.is_equal, ALU.mult)
                    if a % 12 == 11:
                        ins.then_inc(onehot_ready, 1)
                dve.wait_ge(exps_ready, 2 * f + 2)
                step(v.tensor_reduce(S3, E3, AX.X, ALU.add))
                step.settle()
                step(v.reciprocal(RS3, S3))
                step.settle()
                step(v.tensor_tensor(EW, E3, RS3.unsqueeze(2).to_broadcast([P, T, K]), ALU.mult))
                step.settle()
                step(v.tensor_tensor(OWv, OHv, EW.unsqueeze(3).to_broadcast([P, T, K, E]), ALU.mult))
                step.settle()
                v.tensor_reduce(EWS.rearrange(r3, i=T), OWv.rearrange("p i k e -> p i e k"), AX.X,
                                ALU.add).then_inc(weight_ready, 1)
                step(v.tensor_tensor(CB.rearrange("p (b e) -> p b e", e=E),
                                     const("iota_b").unsqueeze(2).to_broadcast([P, NB, E]),
                                     BINC.unsqueeze(1).to_broadcast([P, NB, E]), ALU.is_ge))
                step.settle()
                step(v.tensor_reduce(EOF, CB.rearrange("p (b e) -> p b e", e=E), AX.X, ALU.add))
                step.settle()
                step(v.tensor_scalar(eob[:, :], EOF, float(E - 1), None, ALU.min))
                dve.wait_ge(table_psum, f + 1)
                step(v.tensor_copy(RF, bank[3][:, NB:2 * NB]))
                step.settle()
                step(v.tensor_scalar(BIG, RF, 0.0, float(DUMP - P), ALU.is_equal, ALU.mult))
                step(v.scalar_tensor_tensor(PF, RF, float(P), bank[3][:, 0:NB], ALU.mult, ALU.add))
                step.settle()
                step(v.scalar_tensor_tensor(place[:, :], PF, float(-P), BIG, ALU.add, ALU.add))
                step.settle()
                v.tensor_scalar(token[:, :], place[:, :], T * P - 1, None, ALU.bitwise_and).then_inc(table_ready, 1)
                dve.wait_ge(counted, 2 * f + 2)
                step(v.tensor_reduce(wexp[:, :], bank[2][:, 0:T * E].rearrange("p (i e) -> p e i", e=E), AX.X,
                                     ALU.add))
                step(v.tensor_scalar(cntm, cnt.rearrange("p e i -> p (e i)"), 1.0, None, ALU.max))
                step.settle()
                step(v.reciprocal(cntm, cntm))
                step.settle()
                v.tensor_tensor(wexp[:, :], wexp[:, :], cntm, ALU.mult).then_inc(w_ready, 1)

            def blocks(f):
                v = nc.vector
                dve.wait_ge(w_ready, f + 1)
                step(v.tensor_tensor(wsc[:, :], wexp[:, :], dsc[:, :], ALU.mult))
                step.settle()
                dve.wait_ge(b2w_ready, f + 1)

                def low(b, q):
                    dve.wait_ge(xh_ready, f * NB + b + 1)
                    v.scalar_tensor_tensor(XL[q], bank[6 + q][:, 0:D], X_SCALE, XH[q], ALU.mult,
                                           ALU.subtract).then_inc(xl_ready, 1)

                def split(b, q):
                    dve.wait_ge(relu_done, FREE + f * NB + b + 1)
                    dve.wait_ge(layer2, f * NB + b + 1)
                    v.tensor_copy(HH[q], HF[q]).then_inc(hh_ready, 1)
                    dve.wait_ge(hh_ready, f * NB + b + 1)
                    v.tensor_tensor(HL[q], HF[q], HH[q], ALU.subtract).then_inc(hl_ready, 1)

                def weigh(b, q, j):
                    e = dve.value_load(eob[0:1, bass.ds(b, 1)], min_val=0, max_val=E - 1)
                    dve.wait_ge(layer2, FREE + f * NB + b + 1)
                    if not isinstance(b, int) or b >= 2:
                        dve.wait_ge(y_sent[q], sent(f, b, q))
                    v.scalar_tensor_tensor(YO[q], bank[4 + q][:, 0:D], wsc[:, bass.ds(e, 1)],
                                           b2w[:, bass.ds(e * D, D)], ALU.mult, ALU.add).then_inc(y_ready, 1)

                low(0, 0)
                low(1, 1)
                split(0, 0)
                for u in range(2):
                    low(u + 2, u)
                    split(u + 1, 1 - u)
                    weigh(u, u, None)
                with dve.Fori(1, (NB - 2) // 2) as j:
                    for u in range(2):
                        low(j * 2 + (u + 2), u)
                        split(j * 2 + (u + 1), 1 - u)
                        weigh(j * 2 + u, u, j)
                split(NB - 1, 1)
                weigh(NB - 2, 0, None)
                weigh(NB - 1, 1, None)

            def sent(f, b, q):
                base = 16 * (f * NB // 2)
                return (b - q) // 2 * 16 + base if isinstance(b, int) else (b - q) * 8 + base

            def combine(f):
                v = nc.vector
                for i in range(T):
                    dve.wait_ge(y_back[i % 2], 16 * (f * T // 2 + i // 2 + 1))
                    y = YL[i % 2]
                    v.tensor_tensor(O[:, i, :], y[:, 0, :], y[:, 1, :], ALU.add).then_inc(o_half, 1)
                    dve.wait_ge(o_half, f * T + i + 1)
                    v.tensor_tensor(O[:, i, :], O[:, i, :], y[:, 2, :], ALU.add).then_inc(o_ready, 1)
                dve.wait_ge(pool_psum, f + 1)
                v.tensor_scalar(pooled[:, :], bank[1][:, 0:KC * B], 1.0 / N, None, ALU.mult).then_inc(pool_ready, 1)
                dve.wait_ge(phi_exp, f + 1)
                step(v.tensor_scalar(gate[:, :], gate[:, :], 1.0, None, ALU.add))
                step.settle()
                step(v.reciprocal(gate[:, :], gate[:, :]))
                step.settle()
                step(v.tensor_scalar(gate[:, :], gate[:, :], 0.7, None, ALU.is_gt))
                step.settle()
                step(v.tensor_scalar(gate[:, :], gate[:, :], -0.4, 0.5, ALU.mult, ALU.add))
                step.settle()
                for i in range(T):
                    v.scalar_tensor_tensor(X[:, i, :], O[:, i, :], gate[:, i % B:i % B + 1], X[:, i, :],
                                           ALU.mult, ALU.add).then_inc(x_new, 1)
                dve.wait_ge(x_new, T * (f + 1))

            def attention():
                v = nc.vector
                row_stats(1)
                v.memset(S, 0.0).then_inc(a_s, 4)
                dve.wait_ge(dmask_in, 16)
                with dve.Fori(0, NC) as c:
                    dve.wait_ge(a_qk, c * 4 + 2)
                    dve.wait_ge(a_in, c * B + 1)
                    for g in range(G):
                        v.tensor_tensor(QD[:, g].rearrange("p (b c) -> p b c", b=B),
                                        QE[:, g].rearrange("p (b c) -> p b c", b=B),
                                        const("decay_q")[:, g * P:(g + 1) * P].unsqueeze(1).to_broadcast([P, B, P]),
                                        ALU.mult)
                    v.tensor_scalar(QO, QE, const("odd"), None, ALU.mult).then_inc(a_qsteps, 1)
                    dve.wait_ge(a_qsteps, c + 1)
                    v.tensor_scalar(QE, QE, const("even"), None, ALU.mult).then_inc(a_q, 1)

                    def masked(b, g):
                        n = c * (2 * B) + (2 * b + g)
                        dve.wait_ge(a_sc, n + 2)
                        dve.wait_ge(a_pv, n + 3)
                        v.tensor_tensor(PM[g].rearrange("p r s c -> p r (s c)"), PS[:, 0:4, 0:2 * P],
                                        dmask_s[:, g].rearrange("p r s c -> p r (s c)"), ALU.mult).then_inc(a_p, 1)

                    def residual(b):
                        t = c * B + b
                        dve.wait_ge(a_xb, t + 1)
                        dve.wait_ge(a_out, t + 2)
                        xi = X[:, bass.ds(t, 1), :].rearrange("p a d -> p (a d)")
                        v.tensor_tensor(xi, bank[7][:, D:2 * D], xi, ALU.add).then_inc(a_x, 1)

                    for b in range(B):
                        t = c * B + b
                        dve.wait_ge(a_kv, t + 2)
                        dve.wait_ge(a_pv, t * 2 + 2)
                        v.tensor_tensor(KD[b % 2], bank[4][:, 0:D], bk_s[:, :], ALU.add)
                        v.tensor_tensor(V[b % 2], bank[4][:, D:2 * D], bv_s, ALU.add).then_inc(a_ve, 1)
                        masked(b, 0)
                        dve.wait_ge(a_ve, t + 2)
                        v.tensor_tensor(KD[b % 2], KD[b % 2], const("decay_k"), ALU.mult).then_inc(a_kd, 1)
                        masked(b, 1)
                        if b:
                            residual(b - 1)
                        dve.wait_ge(a_st, t + 1)
                        dve.wait_ge(a_in, t + 2)
                        v.tensor_tensor(TMP, bank[5][:, 0:G * P].rearrange("p (g e) -> p g e", g=G),
                                        const("diag").unsqueeze(1).to_broadcast([P, G, P]), ALU.mult).then_inc(a_tmp, 1)
                        dve.wait_ge(a_tmp, t + 1)
                        for g in range(G):
                            ins = v.scalar_tensor_tensor(S[:, b, g, :], S[:, b, g, :],
                                                         const("decay_chunk")[:, g:g + 1], TMP[:, g, :],
                                                         ALU.mult, ALU.add)
                        ins.then_inc(a_s, 1)
                    residual(B - 1)
                dve.wait_ge(a_x, T + 1)

            dve.sem_inc(a_p, 1)
            dve.sem_inc(a_ve, 1)
            dve.sem_inc(a_x, 1)
            dve.sem_inc(w_lo, 2)
            dve.sem_inc(scaled, 1)
            dve.sem_inc(xl_ready, FREE)
            dve.sem_inc(hl_ready, FREE)
            dve.sem_inc(y_ready, FREE)
            set_up_tables()
            for f in calls:
                routing(f)
                if f == 0:
                    scales()
                blocks(f)
                combine(f)
                if f == 0 and stop != "ffn":
                    attention()


def kernel(L0_attn_x, L0_attn_w_qkv, L0_attn_b_qkv, L0_attn_w_out, L0_attn_b_out, L0_ffn_Wr, L0_ffn_br,
           L0_ffn_w1, L0_ffn_b1, L0_ffn_w2, L0_ffn_b2, L0_ffn_Wp1, L0_ffn_bp1, L0_ffn_Wp2, L0_ffn_bp2):
    import concourse.bacc as bacc
    from concourse.bass_utils import run_bass_kernel_spmd

    nc, arrays = program(dict(
        x=L0_attn_x, w_qkv=L0_attn_w_qkv, b_qkv=L0_attn_b_qkv, w_out=L0_attn_w_out, b_out=L0_attn_b_out,
        Wr=L0_ffn_Wr, br=L0_ffn_br, w1=L0_ffn_w1, b1=L0_ffn_b1, w2=L0_ffn_w2, b2=L0_ffn_b2,
        Wp1=L0_ffn_Wp1, bp1=L0_ffn_bp1, Wp2=L0_ffn_Wp2, bp2=L0_ffn_bp2), bacc)
    r = run_bass_kernel_spmd(nc, [arrays], core_ids=[0])
    return r.results[0]["out"]


def program(a, bacc, stop=None):
    a = {k: np.asarray(v) for k, v in a.items()}
    cst, dmask = constants()
    arrays = {
        "x": a["x"], "w_qkvT": a["w_qkv"].T, "b_qkv": a["b_qkv"],
        "b_qkT": a["b_qkv"][:2 * D].reshape(2 * G, P).T, "w_outT": a["w_out"].T, "b_out": a["b_out"],
        "Wr": a["Wr"], "br": a["br"], "w1": a["w1"],
        "b1T": a["b1"].reshape(E, IC, P).transpose(2, 0, 1).reshape(P, E * IC),
        "w2": a["w2"], "b2": a["b2"], "Wp1": a["Wp1"], "bp1": a["bp1"], "Wp2": a["Wp2"], "bp2": a["bp2"],
        "cst": cst, "dmask": dmask,
    }
    arrays = {k: np.ascontiguousarray(v) for k, v in arrays.items()}
    nc = bacc.Bacc("TRN2", target_bir_lowering=False, num_devices=1)
    args = [nc.dram_tensor(k, v.shape, mybir.dt.from_np(v.dtype), kind="ExternalInput").ap()
            for k, v in arrays.items()]
    xn_dram = nc.dram_tensor("xn_rows", (T * P, D), F32, kind="Internal").ap()
    rows_dram = nc.dram_tensor("expert_rows", (K * T * P, D), F32, kind="Internal").ap()
    out = nc.dram_tensor("out", (B, N, D), F32, kind="ExternalOutput").ap()
    build(nc, *args, xn_dram, rows_dram, out, stop=stop)
    return nc, arrays
```

```python
from contextlib import ExitStack

import numpy as np

import concourse.bass as bass
from concourse import mybir

ALU = mybir.AluOpType
ACT = mybir.ActivationFunctionType
AX = mybir.AxisListType
F32 = mybir.dt.float32
F16 = mybir.dt.float16
BF16 = mybir.dt.bfloat16
I32 = mybir.dt.int32
U32 = mybir.dt.uint32

P = 128
B, N, D = 4, 512, 256
T = B * N // P
NC = N // P
E, K, I = 12, 3, 640
KC, IC = D // P, I // P
W = 2
NB = 36
NT = NB * W
ASSIGN = T * K
TOKENS = T * P
SPARE = W * P
GROUP = 12
H, HD = 16, 16
G = 2
EPS = 1e-5
SLOT = 2 * IC * P
X_SCALE = 1024.0
H_SHIFT = 2.0 ** -14

_COLS = [("ident", P), ("tri", P), ("iota_p", P), ("iota_e", E), ("steps", T // W), ("iota_b", NT),
         ("row", 1), ("pad_place", NT), ("tile_mark", ASSIGN), ("reset", E * T), ("even", 1), ("odd", 1), ("decay_chunk", G), ("diag", P),
         ("decay_q", G * P), ("decay_k", D)]
CONST = {}
_at = 0
for _name, _n in _COLS:
    CONST[_name] = (_at, _n)
    _at += _n
CONST_N = _at


def constants():
    c = np.zeros((P, CONST_N), np.float32)

    def put(name, v):
        o, n = CONST[name]
        c[:, o:o + n] = v

    p = np.arange(P)
    put("ident", np.eye(P))
    put("tri", p[:, None] < p[None, :])
    put("iota_p", p[None, :])
    put("iota_e", np.arange(E)[None, :])
    put("steps", W * P * np.arange(T // W)[None, :])
    put("iota_b", np.arange(NT)[None, :])
    put("row", p[:, None])
    put("pad_place", P + T * P + np.arange(NT)[None, :] % W * P + p[:, None])
    put("tile_mark", np.arange(ASSIGN)[None, :] // K + 1)
    put("reset", (np.arange(E * T) % T != 0)[None, :])
    put("even", (p // HD % 2 == 0)[:, None])
    put("odd", (p // HD % 2 == 1)[:, None])
    start = 2.0 ** -0.5
    slopes = np.array([start ** (i + 1) for i in range(H)], np.float32)
    lam = np.exp(-slopes.astype(np.float64)).astype(np.float32).astype(np.float64)
    lg = lam.reshape(G, H // G).repeat(HD, axis=1).T
    put("decay_chunk", lg ** P)
    put("diag", p[:, None] // HD == p[None, :] // HD)
    put("decay_q", (lg[:, :, None] ** (p + 1.0)[None, None, :]).reshape(P, G * P))
    put("decay_k", lam.repeat(HD)[None, :] ** (P - 1.0 - p)[:, None])
    diff = p[None, :] - p[:, None]
    mask = np.where(diff[:, None, :] >= 0, lam[None, :, None] ** np.maximum(diff, 0)[:, None, :], 0.0)
    return c, mask.reshape(P, H * P).astype(np.float32)


class Chain:

    def __init__(self, eng, sem):
        self.eng, self.sem, self.n = eng, sem, 0

    def __call__(self, ins):
        ins.then_inc(self.sem, 1)
        self.n += 1

    def settle(self):
        self.eng.wait_ge(self.sem, self.n)


def build(nc, x, w_qkvT, b_qkv, b_qkT, w_outT, b_out, Wr, br, w1, b1T, w2, b2, Wp1, bp1, Wp2, bp2, cst, dmask,
          xn_dram, sums_dram, out, stop=None):
    ctx = ExitStack()
    with ctx:
        def sb(name, shape, dt=F32):
            return ctx.enter_context(nc.sbuf_tensor(name, shape, dt))

        def sem(name):
            return ctx.enter_context(nc.semaphore(name))

        W1 = sb("W1", [P, (E + 1) * SLOT])
        W2 = sb("W2", [P, (E + 1) * SLOT])
        w1h = W1[:, :].bitcast(F16)
        w2h = W2[:, :].bitcast(F16)
        X = sb("X", [P, T, D])
        C = sb("C", [P, CONST_N])
        Wr_s = sb("Wr_s", [P, KC, E])
        br_s = sb("br_s", [P, E])
        b1_s = sb("b1_s", [P, E * IC])
        b1s = sb("b1s", [P, E * IC])
        Wp1_s = sb("Wp1_s", [P, KC, P])
        bp1_s = sb("bp1_s", [P, 1])
        Wp2_s = sb("Wp2_s", [P, 1])
        Wp2_b = sb("Wp2_b", [P, P])
        bp2_s = sb("bp2_s", [P, 1])
        tri_h = sb("tri_h", [P, P], BF16)
        ones_h = sb("ones_h", [P, P], BF16)
        iota_h = sb("iota_h", [P, P], BF16)
        ones = sb("ones", [P, P])
        eps = sb("eps", [P, 1])
        ss = sb("ss", [P, E * 2])
        ssb = sb("ssb", [P, E * 2])
        dsc = sb("dsc", [P, E])
        n2 = sb("n2", [P, E * 2])
        ibits = sb("ibits", [P, E * 2], I32)
        ihalf = sb("ihalf", [P, E * 2], I32)
        iscl = sb("iscl", [P, E, 4], I32)
        zeros = sb("zeros", [P, P])
        wscale = sb("wscale", [P, E, 4])
        wsc = sb("wsc", [P, E])
        wexp = sb("wexp", [P, E])
        cntm = sb("cntm", [P, E])[:, :]
        eob = sb("eob", [P, NB], I32)
        token = sb("token", [P, NT], I32)
        place = sb("place", [P, NT], I32)
        tok_q = sb("tok_q", [P, 2 * W], I32)
        place_q = sb("place_q", [P, 2 * W], I32)
        mv = sb("mv", [P, T, 2])
        rstd = sb("rstd", [P, T])
        nmr = sb("nmr", [P, T])
        gate = sb("gate", [P, B])
        pooled = sb("pooled", [P, KC * B])
        phid = sb("phid", [P, B])

        def const(name):
            o, n = CONST[name]
            return C[:, o:o + n]

        ident = const("ident")

        AR = 12672
        A = sb("A", [P, AR])
        top = {"at": 0}

        def carve(n, dt=F32, at=None):
            if at is not None:
                top["at"] = at
            words = n if dt in (F32, I32, U32) else (n + 1) // 2
            o = top["at"]
            top["at"] = o + words
            assert o + words <= AR, (o + words, AR)
            ap = A[:, o:o + words]
            return ap if dt == F32 else ap.bitcast(dt)

        b2w = carve(E * D, at=0)
        bufs_at = top["at"]
        XG = [carve(W * D) for _ in range(2)]
        XH = [carve(W * D, F16).rearrange("p (k t) -> p k t", k=KC) for _ in range(2)]
        XL = [carve(W * D, F16).rearrange("p (k t) -> p k t", k=KC) for _ in range(2)]
        HF = [carve(W * I) for _ in range(2)]
        HH = [carve(W * I, F16) for _ in range(2)]
        HL = [carve(W * I, F16) for _ in range(2)]
        YO = [carve(W * D) for _ in range(2)]
        temps_at = ASSIGN * NT
        xn_at = temps_at + T * D
        XN = carve(T * D, at=xn_at).rearrange("p (i d) -> p i d", i=T)
        O = XN
        XT = [carve(2 * D) for _ in range(2)]
        junk = W1[:, 0:SLOT // 2].bitcast(BF16)
        OHB = carve(ASSIGN * 2 * NT, BF16, at=0).rearrange("p (a n) -> p a n", a=ASSIGN)
        OHA = carve(ASSIGN * P, BF16, at=xn_at).rearrange("p (a n) -> p a n", a=ASSIGN)
        OHR = [carve(GROUP * NT, BF16).rearrange("p (a n) -> p a n", a=GROUP) for _ in range(2)]
        r3 = "p (i e) -> p i e"
        stats = carve(T * 6, at=temps_at).rearrange("p (i s) -> p i s", i=T)
        CB = A[:, top["at"]:top["at"] + NB * E]
        LG = carve(T * E).rearrange(r3, i=T)
        V8 = carve(T * 8).rearrange(r3, i=T)
        I8 = carve(T * 8, U32).rearrange(r3, i=T)
        DX = carve(T * (E + K)).rearrange(r3, i=T)
        EX = carve(T * (E + K)).rearrange(r3, i=T)
        Z = carve(T)
        RZ = carve(T)
        P3 = carve(T * K).rearrange(r3, i=T)
        D3 = carve(T * K).rearrange(r3, i=T)
        E3 = carve(T * K).rearrange(r3, i=T)
        S3 = Z
        RS3 = RZ
        EW = carve(T * K).rearrange(r3, i=T)
        IF = carve(T * K).rearrange(r3, i=T)
        OH = carve(ASSIGN * E)
        OHv = OH.rearrange("p (i k e) -> p i k e", i=T, k=K)
        OW = carve(ASSIGN * E)
        OWv = OW.rearrange("p (i k e) -> p i k e", i=T, k=K)
        M = carve(T * E, BF16)
        EWS = carve(T * E)
        TOT = carve(E * T)
        INC = carve(E * T)
        EXC = carve(E * T)
        POS = carve(T * E)
        CMP = OW[:, 0:E * (T // W)]
        NBK = sb("NBK", [P, E])[:, :]
        BINC = carve(E)
        BEX = carve(E)
        DF = carve(ASSIGN)
        DI = carve(ASSIGN, I32)
        DBI = carve(ASSIGN, I32)
        DMI = carve(ASSIGN, I32)
        DB = carve(ASSIGN)
        DM = carve(ASSIGN)
        EOF = carve(NB)
        RF = carve(NT)
        BIG = carve(NT)
        PF = carve(NT)
        assert top["at"] <= xn_at, (top["at"], xn_at)

        dmask_s = carve(H * P, at=0).rearrange("p (g r s c) -> p g r s c", g=G, r=4, s=2)
        XNa = [carve(D) for _ in range(2)]
        XTa = [carve(D).rearrange("p (k c) -> p k c", k=KC) for _ in range(2)]
        QE = carve(D).rearrange("p (g c) -> p g c", g=G)
        QO = carve(D).rearrange("p (g c) -> p g c", g=G)
        QD = carve(D).rearrange("p (g c) -> p g c", g=G)
        KT = carve(D).rearrange("p (g c) -> p g c", g=G)
        KD = carve(D)
        V2 = carve(H * 2 * HD)
        V2w = V2.rearrange("p (q s n) -> p q s n", s=2, n=2 * HD)
        V2m = V2.rearrange("p (q m d) -> p q m d", m=4, d=HD)
        PM = [carve(D * 4).rearrange("p (r s c) -> p r s c", r=4, s=2) for _ in range(G)]
        S = carve(B * G * P).rearrange("p (b g e) -> p b g e", b=B, g=G)
        TMP = carve(G * P).rearrange("p (g e) -> p g e", g=G)
        AT = carve(D)
        extra1 = W1[:, E * SLOT:(E + 1) * SLOT]
        extra2 = W2[:, E * SLOT:(E + 1) * SLOT]
        wqk_s = extra1[:, 0:KC * 2 * D].rearrange("p (k n) -> p k n", k=KC)
        bo_s = extra1[:, KC * 2 * D:KC * 2 * D + D]
        wv_s = extra2[:, 0:KC * D].rearrange("p (k n) -> p k n", k=KC)
        wo_s = extra2[:, KC * D:2 * KC * D].rearrange("p (k n) -> p k n", k=KC)
        bv_s = extra2[:, 2 * KC * D:2 * KC * D + D]
        bqk_s = sb("bqk_s", [P, 2 * G])

        PS = ctx.enter_context(nc.psum_tensor("PS", [P, 8, 512], F32))
        bank = [PS[:, i, :] for i in range(8)]

        x_in = [sem(f"x_in{j}") for j in range(NC)]
        small_in = sem("small_in")
        w_in = [sem(f"w_in{e}") for e in range(E)]
        set_up = sem("set_up")
        squares = sem("squares")
        normed = sem("normed")
        scaled = sem("scaled")
        scale_steps = sem("scale_steps")
        w_hi = sem("w_hi")
        w_lo = sem("w_lo")
        dve_steps = sem("dve_steps")
        var_ready = sem("var_ready")
        sd_ready = sem("sd_ready")
        rstd_ready = sem("rstd_ready")
        xn_dve = sem("xn_dve")
        xn_act = sem("xn_act")
        xn_stored = sem("xn_stored")
        xt_psum = sem("xt_psum")
        xt_copied = sem("xt_copied")
        logits_ready = sem("logits_ready")
        diffs_ready = sem("diffs_ready")
        exps_ready = sem("exps_ready")
        member_ready = sem("member_ready")
        weight_ready = sem("weight_ready")
        counted = sem("counted")
        onehot_ready = sem("onehot_ready")
        table_psum = sem("table_psum")
        table_ready = sem("table_ready")
        b2_in = sem("b2_in")
        w_ready = sem("w_ready")
        b2w_ready = sem("b2w_ready")
        gathered = [sem(f"gathered{q}") for q in range(2)]
        idx_copied = sem("idx_copied")
        pool_held = sem("pool_held")
        transposed = sem("transposed")
        xh_ready = sem("xh_ready")
        xl_ready = sem("xl_ready")
        layer1 = sem("layer1")
        relu_done = sem("relu_done")
        hh_ready = sem("hh_ready")
        hl_ready = sem("hl_ready")
        layer2 = sem("layer2")
        y_ready = sem("y_ready")
        y_sent = [sem(f"y_sent{q}") for q in range(2)]
        sums_in = [sem(f"sums_in{c}") for c in range(NC)]
        zeros_ready = sem("zeros_ready")
        sums_cleared = sem("sums_cleared")
        raw_ready = sem("raw_ready")
        rows_marked = sem("rows_marked")
        tiles_marked = sem("tiles_marked")
        pool_psum = sem("pool_psum")
        pool_ready = sem("pool_ready")
        hid_psum = sem("hid_psum")
        hid_ready = sem("hid_ready")
        phi_psum = sem("phi_psum")
        phi_exp = sem("phi_exp")
        x_out = sem("x_out")
        x_new = sem("x_new")

        attn_w_in = sem("attn_w_in")
        dmask_in = sem("dmask_in")
        a_xn = sem("a_xn")
        a_xb = sem("a_xb")
        a_tp = sem("a_tp")
        a_xt = sem("a_xt")
        a_proj = sem("a_proj")
        a_qk = sem("a_qk")
        a_q = sem("a_q")
        a_qsteps = sem("a_qsteps")
        a_kv = sem("a_kv")
        a_ve = sem("a_ve")
        a_kd = sem("a_kd")
        a_sc = sem("a_sc")
        a_p = sem("a_p")
        a_st = sem("a_st")
        a_s = sem("a_s")
        a_tmp = sem("a_tmp")
        a_pv = sem("a_pv")
        a_at = sem("a_at")
        a_out = sem("a_out")
        a_x = sem("a_x")

        FREE = 2
        SMALLS = 10
        DO_ATTN = stop is None

        block = ctx.enter_context(nc.Block())
        x_t = x.rearrange("b (c p) d -> p c b d", p=P)
        out_t = out.rearrange("b (c p) d -> p c b d", p=P)
        Xc = X[:, :, :].rearrange("p (c b) d -> p c b d", b=B)
        xn_t = xn_dram.rearrange("(i p) d -> p i d", p=P)
        sums_t = [s[0:TOKENS, :].rearrange("(i p) d -> p i d", p=P) for s in sums_dram]
        calls = (0,) if stop else (0, 1)

        def bcast_row(ap, n):
            return ap.rearrange("(a n) -> a n", a=1).to_broadcast([P, n])

        @block.sync
        def _(sp):
            for j in range(NC):
                sp.dma_start(Xc[:, j], x_t[:, j]).then_inc(x_in[j], 16)
            sp.dma_start(C[:, :], cst).then_inc(small_in, 16)
            sp.dma_start(Wr_s[:, :, :], Wr.rearrange("(k p) e -> p k e", p=P)).then_inc(small_in, 16)
            sp.dma_start(br_s[:, :], bcast_row(br, E)).then_inc(small_in, 16)
            sp.dma_start(b1_s[:, :], b1T).then_inc(small_in, 16)
            for e in range(E):
                sp.dma_start(W1[:, (e + 1) * SLOT:(e + 2) * SLOT].rearrange("p (k i) -> p k i", k=KC),
                             w1[e].rearrange("(k p) i -> p k i", p=P)).then_inc(w_in[e], 16)
                sp.dma_start(W2[:, (e + 1) * SLOT:(e + 2) * SLOT].rearrange("p (c h) -> p c h", c=IC),
                             w2[e].rearrange("(c p) h -> p c h", p=P)).then_inc(w_in[e], 16)
                if e == 0:
                    sp.dma_start(Wp1_s[:, :, :], Wp1.rearrange("(k p) j -> p k j", p=P)).then_inc(small_in, 16)
                    sp.dma_start(bp1_s[:, :], bp1.rearrange("(p a) -> p a", a=1)).then_inc(small_in, 16)
                    sp.dma_start(Wp2_s[:, :], Wp2).then_inc(small_in, 16)
                    sp.dma_start(bp2_s[:, :], bcast_row(bp2, 1)).then_inc(small_in, 16)
            def load_attention():
                sp.wait_ge(w_lo, 2 + 2 * E)
                for k in range(KC):
                    rows = w_qkvT[k * P:(k + 1) * P, :]
                    sp.dma_start(wqk_s[:, k, :], rows[:, 0:2 * D]).then_inc(attn_w_in, 16)
                    sp.dma_start(wv_s[:, k, :], rows[:, 2 * D:3 * D]).then_inc(attn_w_in, 16)
                    sp.dma_start(wo_s[:, k, :], w_outT[k * P:(k + 1) * P, :]).then_inc(attn_w_in, 16)
                sp.dma_start(bo_s, bcast_row(b_out, D)).then_inc(attn_w_in, 16)
                sp.dma_start(bv_s, bcast_row(b_qkv[2 * D:3 * D], D)).then_inc(attn_w_in, 16)
                sp.dma_start(bqk_s[:, :], b_qkT).then_inc(attn_w_in, 16)

            def clear_sums(f):
                rows = sums_dram[f].rearrange("(p r) (h d) -> p (r h) d", p=P, d=P)
                sp.dma_start(rows, zeros[:, :].unsqueeze(1).to_broadcast([P, rows.shape[1], P])
                             ).then_inc(sums_cleared, 16)

            sp.wait_ge(zeros_ready, 1)
            clear_sums(0)
            for f in calls:
                for g in range(4):
                    sp.wait_ge(xn_dve, 8 * f + 2 * (g + 1))
                    sp.wait_ge(xn_act, 8 * f + 2 * (g + 1))
                    sp.dma_start(xn_t[:, 4 * g:4 * g + 4, :], XN[:, 4 * g:4 * g + 4, :]).then_inc(xn_stored, 16)
                sp.wait_ge(table_psum, f + 1)
                sp.dma_start(b2w, b2.rearrange("(a e) h -> a (e h)", a=1).to_broadcast([P, E * D])).then_inc(b2_in, 16)
                if f == 0 and stop != "ffn":
                    load_attention()
                    clear_sums(1)
                for q in range(2):
                    sp.wait_ge(y_sent[q], 16 * W * (NB // 2) * (f + 1))
                for c in range(NC):
                    sp.dma_start(O[:, c * B:(c + 1) * B, :], sums_t[f][:, c * B:(c + 1) * B, :]).then_inc(sums_in[c], 16)
                if f == 0 and stop != "ffn":
                    sp.wait_ge(x_new, T)
                    sp.dma_start(dmask_s, dmask).then_inc(dmask_in, 16)
            for c in range(NC):
                if stop == "attn":
                    sp.wait_ge(a_x, 1 + T)
                sp.wait_ge(x_new, T * (len(calls) - 1) + B * (c + 1))
                sp.dma_start(out_t[:, c], Xc[:, c]).then_inc(x_out, 16)
            sp.wait_ge(x_out, 16 * NC)

        def scale_of(e, n):
            return wscale[:, bass.ds(e, 1), n:n + 1].rearrange("p a b -> p (a b)")

        @block.gpsimd
        def _(pool):
            def gather(f, b, q):
                pool.wait_ge(transposed, f * NB + b + 1)
                pool.sem_inc(pool_held, 1)
                nc.gpsimd.tensor_copy(tok_q[:, W * q:W * q + W], token[:, bass.ds(b * W, W)]).then_inc(idx_copied, 1)
                pool.wait_ge(idx_copied, idx(f, b, 0))
                pool.sem_inc(pool_held, 1)
                for u in range(W):
                    nc.gpsimd.indirect_dma_start(
                        XG[q][:, u * D:(u + 1) * D], None, xn_dram[:, :],
                        bass.IndirectOffsetOnAxis(ap=tok_q[:, W * q + u:W * q + u + 1], axis=0)
                    ).then_inc(gathered[q], 16)

            def scatter(f, b, q):
                if not isinstance(b, int) or b >= 1:
                    pool.wait_ge(y_sent[1 - q], landed(f, b, q))
                    pool.sem_inc(pool_held, 1)
                pool.wait_ge(y_ready, FREE + f * NB + b + 1)
                pool.sem_inc(pool_held, 1)
                nc.gpsimd.tensor_copy(place_q[:, W * q:W * q + W], place[:, bass.ds(b * W, W)]).then_inc(idx_copied, 1)
                pool.wait_ge(idx_copied, idx(f, b, 1))
                pool.sem_inc(pool_held, 1)
                for u in range(W):
                    nc.gpsimd.indirect_dma_start(
                        sums_dram[f][:, :],
                        bass.IndirectOffsetOnAxis(ap=place_q[:, W * q + u:W * q + u + 1], axis=0),
                        YO[q][:, u * D:(u + 1) * D], None, compute_op=ALU.add).then_inc(y_sent[q], 16)

            def landed(f, b, q):
                base = 16 * W * (f * NB // 2)
                return (b + q) // 2 * 16 * W + base if isinstance(b, int) else (b + q) * (8 * W) + base

            LAG = 4

            def idx(f, b, kind):
                if kind == 0:
                    if isinstance(b, int) and b < LAG:
                        return 2 * NB * f + b + 1
                    return b * 2 + (2 * NB * f - LAG + 1)
                if isinstance(b, int) and b >= NB - LAG:
                    return 2 * NB * f + NB + b + 1
                return b * 2 + (2 * NB * f + LAG + 2)

            pool.wait_ge(small_in, 16 * 8)
            for f in calls:
                for g in range(ASSIGN // GROUP):
                    pool.wait_ge(raw_ready, 4 * f + g + 1)
                    nc.gpsimd.tensor_tensor(
                        OHB[:, g * GROUP:(g + 1) * GROUP, NT:2 * NT], OHR[g % 2],
                        const("tile_mark")[:, g * GROUP:(g + 1) * GROUP].unsqueeze(2).to_broadcast([P, GROUP, NT]),
                        ALU.mult).then_inc(tiles_marked, 1)
                if f == 0:
                    pool.wait_ge(sums_cleared, 16)
                else:
                    pool.wait_ge(sums_cleared, 32)
                pool.wait_ge(table_ready, f + 1)
                pool.wait_ge(xn_stored, 64 * (f + 1))
                for b in range(LAG):
                    if b == 2:
                        pool.wait_ge(b2_in, 16 * (f + 1))
                        pool.wait_ge(w_ready, f + 1)
                        v = b2w.rearrange("p (e h) -> p e h", e=E)
                        nc.gpsimd.tensor_tensor(v, v, wexp[:, :].unsqueeze(2).to_broadcast([P, E, D]),
                                                ALU.mult).then_inc(b2w_ready, 1)
                    gather(f, b, b % 2)
                for q in range(2):
                    gather(f, LAG + q, q)
                    scatter(f, q, q)
                with pool.Fori(1, (NB - LAG) // 2) as j:
                    for q in range(2):
                        gather(f, j * 2 + (LAG + q), q)
                        scatter(f, j * 2 + q, q)
                for b in range(NB - LAG, NB):
                    scatter(f, b, b % 2)
                if f == 0 and stop != "ffn":
                    pool.wait_ge(attn_w_in, 16 * 9)
                    with pool.Fori(0, T) as t:
                        pool.wait_ge(a_xn, t + 1)
                        pool.sem_inc(pool_held, 1)
                        xi = X[:, bass.ds(t, 1), :].rearrange("p a d -> p (a d)")
                        nc.gpsimd.tensor_tensor(xi, xi, bo_s, ALU.add).then_inc(a_xb, 1)

        TB = bank[6].rearrange("p (k t) -> p k t", k=KC)

        def hidden(q, c):
            return bank[3 * q + c // 2][:, c % 2 * W * P:(c % 2 + 1) * W * P]

        @block.scalar
        def _(act):
            def square_sums(e):
                act.wait_ge(w_in[e], 32)
                for n, raw in enumerate((W1, W2)):
                    if e or n:
                        act.wait_ge(squares, 2 * e + n)
                    nc.scalar.activation(junk, raw[:, (e + 1) * SLOT:(e + 2) * SLOT], ACT.Square,
                                         accum_out=ss[:, 2 * e + n:2 * e + n + 1]).then_inc(squares, 1)

            def high_parts():
                act.wait_ge(scaled, 1)
                with act.Fori(0, E) as e:
                    for n, (raw, half) in enumerate(((W1, w1h), (W2, w2h))):
                        act.wait_ge(w_lo, e * 2 + (n + 1))
                        nc.scalar.mul(half[:, bass.ds(e * (2 * SLOT), SLOT)], raw[:, bass.ds(e * SLOT + SLOT, SLOT)],
                                      scale_of(e, n)).then_inc(w_hi, 1)

            def deviation(n):
                act.wait_ge(var_ready, n + 1)
                nc.scalar.activation(rstd[:, :], nmr[:, :], ACT.Sqrt).then_inc(sd_ready, 1)
                act.wait_ge(rstd_ready, n + 1)

            def attention():
                deviation(1)
                act.wait_ge(attn_w_in, 16 * 9)

                def normalise(t, b):
                    act.wait_ge(a_tp, t + 1)
                    nc.scalar.activation(XNa[b % 2], X[:, bass.ds(t, 1), :].rearrange("p a d -> p (a d)"),
                                         ACT.Identity, bias=nmr[:, bass.ds(t, 1)],
                                         scale=rstd[:, bass.ds(t, 1)]).then_inc(a_xn, 1)

                def columns(t, b):
                    act.wait_ge(a_tp, t + 3)
                    act.wait_ge(a_kv, t + 1)
                    nc.scalar.copy(XTa[b % 2], bank[4][:, 0:D].rearrange("p (k c) -> p k c", k=KC)).then_inc(a_xt, 1)

                def queries_keys(t):
                    act.wait_ge(a_proj, t + 1)
                    act.wait_ge(a_sc, t * 2 + 1)
                    for n, dst in enumerate((QE[:, 0], QE[:, 1], KT[:, 0], KT[:, 1])):
                        nc.scalar.activation(dst, bank[4][:, n * P:(n + 1) * P], ACT.Identity,
                                             bias=bqk_s[:, n:n + 1]).then_inc(a_qk, 1)

                def rows_out(t):
                    act.wait_ge(a_pv, t * 2 + 4)
                    act.wait_ge(a_out, t + 1)
                    nc.scalar.copy(AT, bank[6][:, 0:D]).then_inc(a_at, 1)

                def tile(t, b, last=False):
                    if not (last and b == B - 1):
                        columns(t + 1, b + 1)
                    if not (last and b >= B - 2):
                        normalise(t + 2, b)
                    if not (last and b == B - 1):
                        queries_keys(t + 1)
                    rows_out(t)

                normalise(0, 0)
                normalise(1, 1)
                columns(0, 0)
                queries_keys(0)
                with act.Fori(0, NC - 1) as c:
                    for b in range(B):
                        tile(c * B + b, b)
                for b in range(B):
                    tile((NC - 1) * B + b, b, last=True)

            def routing(f):
                deviation(2 * f)
                for i in range(1, T, 2):
                    nc.scalar.activation(XN[:, i, :], X[:, i, :], ACT.Identity, bias=nmr[:, i:i + 1],
                                         scale=rstd[:, i:i + 1]).then_inc(xn_act, 1)
                if f == 0:
                    for e in range(E // 2):
                        square_sums(e)
                for n in range(2):
                    act.wait_ge(diffs_ready, 2 * f + n + 1)
                    src, dst = ((DX, EX), (D3, E3))[n]
                    nc.scalar.activation(dst, src, ACT.Exp).then_inc(exps_ready, 1)
                for g in range(ASSIGN // GROUP):
                    act.wait_ge(raw_ready, 4 * f + g + 1)
                    nc.scalar.activation(OHB[:, g * GROUP:(g + 1) * GROUP, 0:NT], OHR[g % 2], ACT.Identity,
                                         scale=const("row")).then_inc(rows_marked, 1)
                if f == 0:
                    for e in range(E // 2, E):
                        square_sums(e)
                    high_parts()

            def blocks(f):
                def high(b, q):
                    act.wait_ge(transposed, FREE + f * NB + b + 1)
                    act.wait_ge(layer1, f * NB + b + 1)
                    nc.scalar.mul(XH[q], TB, X_SCALE).then_inc(xh_ready, 1)

                def relu(b, q):
                    e = act.value_load(eob[0:1, bass.ds(b, 1)], min_val=0, max_val=E - 1)
                    act.wait_ge(layer1, FREE + f * NB + b + 1)
                    act.wait_ge(hl_ready, f * NB + b + 1)
                    for c in range(IC):
                        ins = nc.scalar.activation(HF[q][:, c * W * P:(c + 1) * W * P], hidden(q, c),
                                                   ACT.Relu, bias=b1s[:, bass.ds(e * IC + c, 1)],
                                                   scale=H_SHIFT)
                    ins.then_inc(relu_done, 1)

                high(0, 0)
                with act.Fori(0, (NB - 2) // 2) as j:
                    for q in range(2):
                        high(j * 2 + (q + 1), 1 - q)
                        relu(j * 2 + q, q)
                high(NB - 1, 1)
                relu(NB - 2, 0)
                relu(NB - 1, 1)

            def combine(f):
                act.wait_ge(hid_psum, f + 1)
                nc.scalar.activation(phid[:, :], bank[2][:, 0:B], ACT.Relu, bias=bp1_s[:, :]).then_inc(hid_ready, 1)
                act.wait_ge(phi_psum, f + 1)
                nc.scalar.activation(gate[:, :], bank[3][:, 0:B], ACT.Exp, bias=bp2_s[:, :],
                                     scale=-1.0).then_inc(phi_exp, 1)

            act.sem_inc(relu_done, FREE)
            act.sem_inc(a_at, 1)
            act.sem_inc(a_qk, 1)
            act.wait_ge(small_in, 16 * 8)
            for f in calls:
                routing(f)
                blocks(f)
                combine(f)
                if f == 0 and stop != "ffn":
                    attention()

        @block.tensor
        def _(pe):
            def matmul(out_, l, r, start, stop_):
                return nc.tensor.matmul(out_, l, r, start=start, stop=stop_, skip_group_check=True)

            def norms():
                pe.wait_ge(squares, 2 * E)
                matmul(bank[6][:, 0:2 * E], ones[:, :], ss[:, :], True, False)
                matmul(bank[6][:, 0:2 * E], ones[:, :], ssb[:, :], False, True).then_inc(normed, 1)

            def routing(f):
                for j in range(T // 2 + 1):
                    if j < T // 2:
                        pe.wait_ge(xn_dve, 8 * f + j + 1)
                        pe.wait_ge(xn_act, 8 * f + j + 1)
                        if j >= 2:
                            pe.wait_ge(xt_copied, T // 2 * f + j - 1)
                        for u in range(2):
                            for k in range(KC):
                                ins = nc.tensor.transpose(bank[4 + j % 2][:, (u * KC + k) * P:(u * KC + k + 1) * P],
                                                          XN[:, 2 * j + u, k * P:(k + 1) * P], ident)
                        ins.then_inc(xt_psum, 1)
                    if j >= 1:
                        pe.wait_ge(xt_copied, T // 2 * f + j)
                        for u in range(2):
                            i = 2 * j - 2 + u
                            for k in range(KC):
                                ins = matmul(bank[0][:, i * E:(i + 1) * E],
                                             XT[(j - 1) % 2][:, (u * KC + k) * P:(u * KC + k + 1) * P],
                                             Wr_s[:, k, :], k == 0, k == KC - 1)
                        ins.then_inc(logits_ready, 1)
                pe.wait_ge(member_ready, f + 1)
                matmul(bank[1][:, 0:T * E], tri_h[:, :], M, True, True)
                matmul(bank[1][:, 256:256 + T * E], ones_h[:, :], M, True, True).then_inc(counted, 1)
                pe.wait_ge(weight_ready, f + 1)
                matmul(bank[2][:, 0:T * E], ones[:, :], EWS, True, True).then_inc(counted, 1)
                for g in range(4):
                    pe.wait_ge(onehot_ready, 4 * f + g + 1)
                    pe.wait_ge(rows_marked, 4 * f + g + 1)
                    pe.wait_ge(tiles_marked, 4 * f + g + 1)
                    for a in range(GROUP * g, GROUP * (g + 1)):
                        ins = matmul(bank[3][:, 0:2 * NT], OHA[:, a, :], OHB[:, a, :], a == 0, a == ASSIGN - 1)
                ins.then_inc(table_psum, 1)

            def blocks(f):
                def transposes(b, q):
                    pe.wait_ge(gathered[q], gcount(f, b, q))
                    pe.wait_ge(xl_ready, f * NB + b + 2)
                    for u in range(W):
                        for k in range(KC):
                            ins = nc.tensor.transpose(TB[:, k, u * P:(u + 1) * P],
                                                      XG[q][:, u * D + k * P:u * D + (k + 1) * P], ident)
                    ins.then_inc(transposed, 1)

                def first(b, q):
                    e = pe.value_load(eob[0:1, bass.ds(b, 1)], min_val=0, max_val=E - 1)
                    pe.wait_ge(xl_ready, FREE + f * NB + b + 1)
                    pe.wait_ge(relu_done, f * NB + b + 1)
                    for c in range(IC):
                        dst = hidden(q, c)
                        n = 0
                        for k in range(KC):
                            for part, src in ((0, XH), (0, XL), (1, XH)):
                                w = w1h[:, bass.ds(e * (2 * SLOT) + (part * SLOT + k * I + c * P), P)]
                                ins = matmul(dst, w, src[q][:, k, :], n == 0, n == 5)
                                n += 1
                    ins.then_inc(layer1, 1)

                def second(b, q):
                    e = pe.value_load(eob[0:1, bass.ds(b, 1)], min_val=0, max_val=E - 1)
                    pe.wait_ge(hl_ready, FREE + f * NB + b + 1)
                    pe.wait_ge(y_ready, f * NB + b + 2)
                    n = 0
                    for c in range(IC):
                        for part, src in ((0, HH), (0, HL), (1, HH)):
                            w = w2h[:, bass.ds(e * (2 * SLOT) + (part * SLOT + c * D), D)]
                            for u in range(W):
                                ins = matmul(bank[7][:, u * D:(u + 1) * D],
                                             src[q][:, (c * W + u) * P:(c * W + u + 1) * P], w,
                                             n == 0 and u == 0, n == 14)
                            n += 1
                    ins.then_inc(layer2, 1)

                if f == 0:
                    pe.wait_ge(w_lo, 2 + 2 * E)
                transposes(0, 0)
                transposes(1, 1)
                first(0, 0)
                with pe.Fori(0, (NB - 2) // 2) as j:
                    for u in range(2):
                        transposes(j * 2 + (u + 2), u)
                        first(j * 2 + (u + 1), 1 - u)
                        second(j * 2 + u, u)
                first(NB - 1, 1)
                second(NB - 2, 0)
                second(NB - 1, 1)

            def gcount(f, b, q):
                base = 16 * W * (f * NB // 2 + 1)
                return (b - q) // 2 * 16 * W + base if isinstance(b, int) else (b - q) * (8 * W) + base

            def combine(f):
                for c in range(NC):
                    pe.wait_ge(sums_in[c], 16 * (f + 1))
                for k in range(KC):
                    for b in range(B):
                        for c in range(NC):
                            col = k * B + b
                            ins = matmul(bank[1][:, col:col + 1], O[:, c * B + b, k * P:(k + 1) * P],
                                         ones[:, 0:1], c == 0, c == NC - 1)
                ins.then_inc(pool_psum, 1)
                pe.wait_ge(pool_ready, f + 1)
                for k in range(KC):
                    ins = matmul(bank[2][:, 0:B], Wp1_s[:, k, :], pooled[:, k * B:(k + 1) * B], k == 0, k == KC - 1)
                ins.then_inc(hid_psum, 1)
                pe.wait_ge(hid_ready, f + 1)
                matmul(bank[3][:, 0:B], Wp2_b[:, :], phid[:, :], True, True).then_inc(phi_psum, 1)

            def attention():
                pe.wait_ge(attn_w_in, 16 * 9)

                def columns(t, b):
                    pe.wait_ge(a_xn, t + 1)
                    pe.wait_ge(a_qk, t * 4 + 1)
                    for k in range(KC):
                        ins = nc.tensor.transpose(bank[4][:, k * P:(k + 1) * P], XNa[b % 2][:, k * P:(k + 1) * P],
                                                  ident)
                    ins.then_inc(a_tp, 1)

                def queries_keys(t, b):
                    pe.wait_ge(a_xt, t + 1)
                    for n in range(4):
                        for k in range(KC):
                            ins = matmul(bank[4][:, n * P:(n + 1) * P], wqk_s[:, k, n * P:(n + 1) * P],
                                         XTa[b % 2][:, k, :], k == 0, k == KC - 1)
                    ins.then_inc(a_proj, 1)

                def values_keys(t, b):
                    pe.wait_ge(a_qk, t * 4 + 5)
                    pe.wait_ge(a_kd, t + 1)
                    for k in range(KC):
                        matmul(bank[5][:, 0:D], XTa[b % 2][:, k, :], wv_s[:, k, :], k == 0, k == KC - 1)
                    for g in range(G):
                        ins = nc.tensor.transpose(bank[5][:, D + g * P:D + (g + 1) * P], KT[:, g, :], ident)
                    ins.then_inc(a_kv, 1)

                def scores(t, g):
                    pe.wait_ge(a_qk, t * 4 + 5)
                    pe.wait_ge(a_q, t + 1)
                    pe.wait_ge(a_p, t * 2 + (g + 1))
                    for s in range(2):
                        q = (QE, QO)[s]
                        for r in range(4):
                            rows = slice(32 * r, 32 * r + 32)
                            ins = matmul(bank[r][:, s * P:(s + 1) * P], KT[rows, g, :], q[rows, g, :], True, True)
                    ins.then_inc(a_sc, 1)

                def from_state(t, b):
                    pe.wait_ge(a_s, t + 1)
                    pe.wait_ge(a_at, t + 1)
                    for g in range(G):
                        matmul(bank[6][:, g * P:(g + 1) * P], S[:, b, g, :], QD[:, g, :], g == 0, False)

                def from_chunk(t, g):
                    pe.wait_ge(a_p, t * 2 + (g + 2))
                    if g == 0:
                        pe.wait_ge(a_ve, t + 1)
                    for s in range(2):
                        for r in range(4):
                            ins = matmul(bank[6][32 * r:32 * r + 32, g * P:(g + 1) * P], V2w[:, 4 * g + r, s, :],
                                         PM[g][:, r, s, :], False, g == G - 1 and s == 1)
                    ins.then_inc(a_pv, 1)

                def state(t):
                    pe.wait_ge(a_kd, t + 2)
                    pe.wait_ge(a_x, t + 1)
                    for g in range(G):
                        ins = matmul(bank[7][:, g * P:(g + 1) * P], KD[:, g * P:(g + 1) * P],
                                     V2m[:, 4 * g:4 * g + 4, 0:4:3, :], True, True)
                    ins.then_inc(a_st, 1)

                def out_proj(t):
                    pe.wait_ge(a_at, t + 2)
                    pe.wait_ge(a_s, t + 5)
                    for k in range(KC):
                        ins = matmul(bank[7][:, D:2 * D], AT[:, k * P:(k + 1) * P], wo_s[:, k, :],
                                     k == 0, k == KC - 1)
                    ins.then_inc(a_out, 1)

                def tile(t, b, last=False):
                    more = not (last and b == B - 1)
                    if more:
                        columns(t + 1, b + 1)
                    values_keys(t, b)
                    from_state(t, b)
                    scores(t, 1)
                    from_chunk(t, 0)
                    state(t)
                    if more:
                        queries_keys(t + 1, b + 1)
                    from_chunk(t, 1)
                    if more:
                        scores(t + 1, 0)
                    out_proj(t)

                columns(0, 0)
                queries_keys(0, 0)
                scores(0, 0)
                with pe.Fori(0, NC - 1) as c:
                    for b in range(B):
                        tile(c * B + b, b)
                for b in range(B):
                    tile((NC - 1) * B + b, b, last=True)

            pe.sem_inc(a_tp, 2)
            pe.sem_inc(a_kv, 2)
            pe.sem_inc(a_sc, 1)
            pe.sem_inc(a_pv, 2)
            pe.sem_inc(a_out, 1)
            pe.sem_inc(transposed, FREE)
            pe.sem_inc(layer1, FREE)
            pe.sem_inc(layer2, FREE)
            pe.wait_ge(set_up, 1)
            for f in calls:
                routing(f)
                if f == 0:
                    norms()
                blocks(f)
                combine(f)
                if f == 0 and stop != "ffn":
                    attention()

        @block.vector
        def _(dve):
            step = Chain(dve, dve_steps)

            def set_up_tables():
                v = nc.vector
                v.memset(zeros[:, :], 0.0).then_inc(zeros_ready, 1)
                v.memset(ssb[:, :], 0.0).then_inc(zeros_ready, 1)
                dve.wait_ge(zeros_ready, 2)
                dve.wait_ge(small_in, 16 * 8)
                v.memset(ones[:, :], 1.0)
                v.memset(ones_h[:, :], 1.0)
                v.tensor_copy(tri_h[:, :], const("tri"))
                v.tensor_copy(iota_h[:, :], const("iota_p"))
                v.memset(eps[:, :], EPS)
                v.tensor_scalar(bp2_s[:, :], bp2_s[:, :], -1.0, None, ALU.mult)
                step(v.tensor_tensor(b1s[:, :], b1_s[:, :], b1_s[:, :], ALU.mult))
                step(v.tensor_copy(Wp2_b[:, :], Wp2_s[:, :].to_broadcast([P, P])))
                step.settle()
                v.tensor_reduce(ssb[:, :].rearrange("p (e n) -> p e n", n=2)[:, :, 0],
                                b1s[:, :].rearrange("p (e c) -> p e c", c=IC), AX.X, ALU.add).then_inc(set_up, 1)

            def scales():
                v = nc.vector
                dve.wait_ge(normed, 1)
                step(v.tensor_scalar(n2[:, :], bank[6][:, 0:2 * E], 1e-30, None, ALU.max))
                step.settle()
                step(v.tensor_scalar(ibits[:, :], n2[:, :].bitcast(I32), 23, None, ALU.logical_shift_right))
                step.settle()
                step(v.tensor_scalar(ihalf[:, :], ibits[:, :], 1.0, None, ALU.add))
                step.settle()
                step(v.tensor_scalar(ibits[:, :], ihalf[:, :], 1, None, ALU.logical_shift_right))
                step.settle()
                pairs = ibits[:, :].rearrange("p (e n) -> p e n", n=2)
                step(v.tensor_scalar(iscl[:, :, 0:2], pairs, -1.0, 205.0, ALU.mult, ALU.add))
                step(v.tensor_scalar(iscl[:, :, 2:4], pairs, 49.0, None, ALU.add))
                step.settle()
                v.tensor_scalar(wscale[:, :, :].bitcast(I32), iscl[:, :, :], 23, None,
                                ALU.logical_shift_left).then_inc(scaled, 1)
                dve.wait_ge(scaled, 1)
                b3 = "p (e c) -> p e c"
                step(v.scalar_tensor_tensor(b1s[:, :].rearrange(b3, c=IC), b1_s[:, :].rearrange(b3, c=IC),
                                            X_SCALE * H_SHIFT, wscale[:, :, 0:1].to_broadcast([P, E, IC]),
                                            ALU.mult, ALU.mult))
                step(v.scalar_tensor_tensor(dsc[:, :], wscale[:, :, 2], 1.0 / (X_SCALE * H_SHIFT),
                                            wscale[:, :, 3], ALU.mult, ALU.mult))
                with dve.Fori(0, E) as e:
                    for n, (raw, half) in enumerate(((W1, w1h), (W2, w2h))):
                        dve.wait_ge(w_hi, e * 2 + (n + 1))
                        v.scalar_tensor_tensor(half[:, bass.ds(e * (2 * SLOT) + SLOT, SLOT)],
                                               raw[:, bass.ds(e * SLOT + SLOT, SLOT)], scale_of(e, n),
                                               half[:, bass.ds(e * (2 * SLOT), SLOT)],
                                               ALU.mult, ALU.subtract).then_inc(w_lo, 1)
                dve.wait_ge(w_lo, 2 + 2 * E)
                step.settle()

            def row_stats(n):
                v = nc.vector
                for i in range(T):
                    if n == 0 and i % B == 0:
                        dve.wait_ge(x_in[i // B], 16)
                    step(v.bn_stats(stats[:, i, :], X[:, i, :]))
                step.settle()
                for i in range(T):
                    step(v.bn_aggr(mv[:, i, :], stats[:, i, :]))
                step.settle()
                v.tensor_scalar(nmr[:, :], mv[:, :, 1], EPS, None, ALU.add).then_inc(var_ready, 1)
                dve.wait_ge(sd_ready, n + 1)
                step(v.reciprocal(rstd[:, :], rstd[:, :]))
                step.settle()
                v.scalar_tensor_tensor(nmr[:, :], mv[:, :, 0], -1.0, rstd[:, :], ALU.mult,
                                       ALU.mult).then_inc(rstd_ready, 1)
                dve.wait_ge(rstd_ready, n + 1)

            def routing(f):
                v = nc.vector
                row_stats(2 * f)
                for i in range(0, T, 2):
                    v.tensor_scalar(XN[:, i, :], X[:, i, :], rstd[:, i:i + 1], nmr[:, i:i + 1],
                                    ALU.mult, ALU.add).then_inc(xn_dve, 1)
                for j in range(T // 2):
                    if f == 0 and j == 0:
                        set_up_tables()
                    dve.wait_ge(xt_psum, T // 2 * f + j + 1)
                    if j >= 2:
                        dve.wait_ge(logits_ready, T // 2 * f + j - 1)
                    v.tensor_copy(XT[j % 2], bank[4 + j % 2][:, :]).then_inc(xt_copied, 1)
                dve.wait_ge(logits_ready, T // 2 * (f + 1))
                step(v.tensor_tensor(LG, bank[0][:, 0:T * E].rearrange(r3, i=T),
                                     br_s[:, :].unsqueeze(1).to_broadcast([P, T, E]), ALU.add))
                step.settle()
                for i in range(T):
                    step(v.max(V8[:, i, :], LG[:, i, :]))
                step.settle()
                for i in range(T):
                    step(v.max_index(I8[:, i, :], V8[:, i, :], LG[:, i, :]))
                top1 = V8[:, :, 0:1]
                v.tensor_tensor(DX[:, :, E:E + K], V8[:, :, 0:K], top1.to_broadcast([P, T, K]), ALU.subtract)
                v.tensor_tensor(DX[:, :, 0:E], LG, top1.to_broadcast([P, T, E]),
                                ALU.subtract).then_inc(diffs_ready, 1)
                step.settle()
                step(v.tensor_copy(IF, I8[:, :, 0:K]))
                step.settle()
                step(v.tensor_tensor(OHv, IF.unsqueeze(3).to_broadcast([P, T, K, E]),
                                     const("iota_e").unsqueeze(1).unsqueeze(1).to_broadcast([P, T, K, E]),
                                     ALU.is_equal))
                step.settle()
                with nc.allow_low_precision(reason="sums of zeros and at most one one"):
                    v.tensor_reduce(M, OHv.rearrange("p i k e -> p i e k"), AX.X, ALU.add).then_inc(member_ready, 1)
                dve.wait_ge(exps_ready, 2 * f + 1)
                step(v.tensor_reduce(Z, EX[:, :, 0:E], AX.X, ALU.add))
                step.settle()
                step(v.reciprocal(RZ, Z))
                step.settle()
                step(v.tensor_tensor(P3, EX[:, :, E:E + K], RZ.unsqueeze(2).to_broadcast([P, T, K]), ALU.mult))
                step.settle()
                v.tensor_tensor(D3, P3, P3[:, :, 0:1].to_broadcast([P, T, K]),
                                ALU.subtract).then_inc(diffs_ready, 1)
                dve.wait_ge(counted, 2 * f + 1)
                step(v.tensor_copy(TOT.rearrange("p (e i) -> p e i", e=E),
                                   bank[1][:, 256:256 + T * E].rearrange("p (i e) -> p e i", e=E)))
                step.settle()
                step(v.tensor_tensor_scan(INC, const("reset"), TOT, 0.0, ALU.mult, ALU.add))
                step.settle()
                cnt = INC.rearrange("p (e i) -> p e i", e=E)[:, :, T - 1:T]
                step(v.tensor_tensor(EXC, INC, TOT, ALU.subtract))
                step(v.tensor_tensor(CMP.rearrange("p (e i) -> p e i", e=E), cnt.to_broadcast([P, E, T // W]),
                                     const("steps").unsqueeze(1).to_broadcast([P, E, T // W]), ALU.is_gt))
                step.settle()
                step(v.tensor_reduce(NBK, CMP.rearrange("p (e i) -> p e i", e=E), AX.X, ALU.add))
                step.settle()
                step(v.tensor_tensor_scan(BINC, ones[:, 0:E], NBK, 0.0, ALU.mult, ALU.add))
                step.settle()
                step(v.tensor_tensor(BEX, BINC, NBK, ALU.subtract))
                step.settle()
                e3 = EXC.rearrange("p (e i) -> p e i", e=E)
                step(v.scalar_tensor_tensor(e3, BEX.unsqueeze(2).to_broadcast([P, E, T]), float(W * P), e3,
                                            ALU.mult, ALU.add))
                step.settle()
                step(v.tensor_tensor(POS.rearrange(r3, i=T), bank[1][:, 0:T * E].rearrange(r3, i=T),
                                     EXC.rearrange("p (e i) -> p i e", e=E), ALU.add))
                step.settle()
                step(v.tensor_tensor(OWv, OHv, POS.rearrange(r3, i=T).unsqueeze(2).to_broadcast([P, T, K, E]),
                                     ALU.mult))
                step.settle()
                step(v.tensor_reduce(DF, OW.rearrange("p (a e) -> p a e", e=E), AX.X, ALU.add))
                step.settle()
                step(v.tensor_copy(DI, DF))
                step.settle()
                step(v.tensor_scalar(DBI, DI, 7, None, ALU.logical_shift_right))
                step(v.tensor_scalar(DMI, DI, P - 1, None, ALU.bitwise_and))
                step.settle()
                step(v.tensor_copy(DB, DBI))
                step(v.tensor_copy(DM, DMI))
                step.settle()
                dve.wait_ge(xn_stored, 64 * (f + 1))
                dve.wait_ge(xt_psum, T // 2 * (f + 1))
                for g in range(ASSIGN // GROUP):
                    pairs = slice(g * GROUP, (g + 1) * GROUP)
                    if g >= 2:
                        dve.wait_ge(rows_marked, 4 * f + g - 1)
                        dve.wait_ge(tiles_marked, 4 * f + g - 1)
                    v.tensor_tensor(OHR[g % 2], const("iota_b").unsqueeze(1).to_broadcast([P, GROUP, NT]),
                                    DB[:, pairs].unsqueeze(2).to_broadcast([P, GROUP, NT]),
                                    ALU.is_equal).then_inc(raw_ready, 1)
                    v.tensor_tensor(OHA[:, pairs, :], iota_h[:, :].unsqueeze(1).to_broadcast([P, GROUP, P]),
                                    DM[:, pairs].unsqueeze(2).to_broadcast([P, GROUP, P]),
                                    ALU.is_equal).then_inc(onehot_ready, 1)
                dve.wait_ge(exps_ready, 2 * f + 2)
                step(v.tensor_reduce(S3, E3, AX.X, ALU.add))
                step.settle()
                step(v.reciprocal(RS3, S3))
                step.settle()
                step(v.tensor_tensor(EW, E3, RS3.unsqueeze(2).to_broadcast([P, T, K]), ALU.mult))
                step.settle()
                step(v.tensor_tensor(OWv, OHv, EW.unsqueeze(3).to_broadcast([P, T, K, E]), ALU.mult))
                step.settle()
                v.tensor_reduce(EWS.rearrange(r3, i=T), OWv.rearrange("p i k e -> p i e k"), AX.X,
                                ALU.add).then_inc(weight_ready, 1)
                step(v.tensor_tensor(CB.rearrange("p (b e) -> p b e", e=E),
                                     const("iota_b")[:, 0:NB].unsqueeze(2).to_broadcast([P, NB, E]),
                                     BINC.unsqueeze(1).to_broadcast([P, NB, E]), ALU.is_ge))
                step.settle()
                step(v.tensor_reduce(EOF, CB.rearrange("p (b e) -> p b e", e=E), AX.X, ALU.add))
                step.settle()
                step(v.tensor_scalar(eob[:, :], EOF, float(E - 1), None, ALU.min))
                dve.wait_ge(table_psum, f + 1)
                step(v.tensor_copy(RF, bank[3][:, NT:2 * NT]))
                step.settle()
                step(v.scalar_tensor_tensor(BIG, RF, 0.0, const("pad_place"), ALU.is_equal, ALU.mult))
                step(v.scalar_tensor_tensor(PF, RF, float(P), bank[3][:, 0:NT], ALU.mult, ALU.add))
                step.settle()
                step(v.scalar_tensor_tensor(place[:, :], PF, float(-P), BIG, ALU.add, ALU.add))
                step.settle()
                v.tensor_scalar(token[:, :], place[:, :], T * P - 1, None, ALU.bitwise_and).then_inc(table_ready, 1)
                dve.wait_ge(counted, 2 * f + 2)
                step(v.tensor_reduce(wexp[:, :], bank[2][:, 0:T * E].rearrange("p (i e) -> p e i", e=E), AX.X,
                                     ALU.add))
                step(v.tensor_scalar(cntm, cnt.rearrange("p e i -> p (e i)"), 1.0, None, ALU.max))
                step.settle()
                step(v.reciprocal(cntm, cntm))
                step.settle()
                v.tensor_tensor(wexp[:, :], wexp[:, :], cntm, ALU.mult).then_inc(w_ready, 1)

            def blocks(f):
                v = nc.vector
                dve.wait_ge(w_ready, f + 1)
                step(v.tensor_tensor(wsc[:, :], wexp[:, :], dsc[:, :], ALU.mult))
                step.settle()
                dve.wait_ge(b2w_ready, f + 1)

                def low(b, q):
                    dve.wait_ge(xh_ready, f * NB + b + 1)
                    v.scalar_tensor_tensor(XL[q], TB, X_SCALE, XH[q], ALU.mult,
                                           ALU.subtract).then_inc(xl_ready, 1)

                def split(b, q):
                    dve.wait_ge(relu_done, FREE + f * NB + b + 1)
                    dve.wait_ge(layer2, f * NB + b + 1)
                    v.tensor_copy(HH[q], HF[q]).then_inc(hh_ready, 1)
                    dve.wait_ge(hh_ready, f * NB + b + 1)
                    v.tensor_tensor(HL[q], HF[q], HH[q], ALU.subtract).then_inc(hl_ready, 1)

                def weigh(b, q, j):
                    e = dve.value_load(eob[0:1, bass.ds(b, 1)], min_val=0, max_val=E - 1)
                    dve.wait_ge(layer2, FREE + f * NB + b + 1)
                    if not isinstance(b, int) or b >= 2:
                        dve.wait_ge(y_sent[q], sent(f, b, q))
                    for u in range(W):
                        ins = v.scalar_tensor_tensor(YO[q][:, u * D:(u + 1) * D], bank[7][:, u * D:(u + 1) * D],
                                                     wsc[:, bass.ds(e, 1)], b2w[:, bass.ds(e * D, D)],
                                                     ALU.mult, ALU.add)
                    ins.then_inc(y_ready, 1)

                low(0, 0)
                low(1, 1)
                split(0, 0)
                for u in range(2):
                    low(u + 2, u)
                    split(u + 1, 1 - u)
                    weigh(u, u, None)
                with dve.Fori(1, (NB - 2) // 2) as j:
                    for u in range(2):
                        low(j * 2 + (u + 2), u)
                        split(j * 2 + (u + 1), 1 - u)
                        weigh(j * 2 + u, u, j)
                split(NB - 1, 1)
                weigh(NB - 2, 0, None)
                weigh(NB - 1, 1, None)

            def sent(f, b, q):
                base = 16 * W * (f * NB // 2)
                return (b - q) // 2 * 16 * W + base if isinstance(b, int) else (b - q) * (8 * W) + base

            def combine(f):
                v = nc.vector
                dve.wait_ge(pool_psum, f + 1)
                v.tensor_scalar(pooled[:, :], bank[1][:, 0:KC * B], 1.0 / N, None, ALU.mult).then_inc(pool_ready, 1)
                dve.wait_ge(phi_exp, f + 1)
                step(v.tensor_scalar(gate[:, :], gate[:, :], 1.0, None, ALU.add))
                step.settle()
                step(v.reciprocal(gate[:, :], gate[:, :]))
                step.settle()
                step(v.tensor_scalar(gate[:, :], gate[:, :], 0.7, None, ALU.is_gt))
                step.settle()
                step(v.tensor_scalar(gate[:, :], gate[:, :], -0.4, 0.5, ALU.mult, ALU.add))
                step.settle()
                for c in range(NC):
                    dve.wait_ge(sums_in[c], 16 * (f + 1))
                for i in range(T):
                    v.scalar_tensor_tensor(X[:, i, :], O[:, i, :], gate[:, i % B:i % B + 1], X[:, i, :],
                                           ALU.mult, ALU.add).then_inc(x_new, 1)
                dve.wait_ge(x_new, T * (f + 1))

            def attention():
                v = nc.vector
                row_stats(1)
                v.memset(V2, 0.0)
                v.memset(S, 0.0).then_inc(a_s, 4)
                dve.wait_ge(dmask_in, 16)

                def queries(t):
                    dve.wait_ge(a_qk, t * 4 + 3)
                    v.tensor_tensor(QD, QE, const("decay_q").rearrange("p (g c) -> p g c", g=G), ALU.mult)
                    v.tensor_scalar(QO, QE, const("odd"), None, ALU.mult).then_inc(a_qsteps, 1)
                    dve.wait_ge(a_qsteps, t + 1)
                    v.tensor_scalar(QE, QE, const("even"), None, ALU.mult).then_inc(a_q, 1)

                def masked(t, g):
                    dve.wait_ge(a_sc, t * 2 + (g + 2))
                    dve.wait_ge(a_pv, t * 2 + (g + 1))
                    v.tensor_tensor(PM[g].rearrange("p r s c -> p r (s c)"), PS[:, 0:4, 0:2 * P],
                                    dmask_s[:, g].rearrange("p r s c -> p r (s c)"), ALU.mult).then_inc(a_p, 1)

                def values_keys(t):
                    dve.wait_ge(a_kv, t + 3)
                    dve.wait_ge(a_pv, t * 2 + 2)
                    v.tensor_tensor(V2m[:, :, 0:4:3, :], bank[5][:, 0:D].rearrange("p (q s d) -> p q s d", s=2, d=HD),
                                    bv_s.rearrange("p (q s d) -> p q s d", s=2, d=HD), ALU.add).then_inc(a_ve, 1)
                    v.tensor_tensor(KD, bank[5][:, D:2 * D], const("decay_k"), ALU.mult).then_inc(a_kd, 1)

                def state(t, b):
                    dve.wait_ge(a_st, t + 1)
                    v.tensor_tensor(TMP, bank[7][:, 0:G * P].rearrange("p (g e) -> p g e", g=G),
                                    const("diag").unsqueeze(1).to_broadcast([P, G, P]), ALU.mult).then_inc(a_tmp, 1)
                    dve.wait_ge(a_tmp, t + 1)
                    for g in range(G):
                        ins = v.scalar_tensor_tensor(S[:, b, g, :], S[:, b, g, :], const("decay_chunk")[:, g:g + 1],
                                                     TMP[:, g, :], ALU.mult, ALU.add)
                    ins.then_inc(a_s, 1)

                def residual(t):
                    dve.wait_ge(a_xb, t + 1)
                    dve.wait_ge(a_out, t + 2)
                    xi = X[:, bass.ds(t, 1), :].rearrange("p a d -> p (a d)")
                    v.tensor_tensor(xi, bank[7][:, D:2 * D], xi, ALU.add).then_inc(a_x, 1)

                def tile(t, b, last=False):
                    masked(t, 0)
                    values_keys(t)
                    masked(t, 1)
                    state(t, b)
                    if not (last and b == B - 1):
                        queries(t + 1)
                    residual(t)

                queries(0)
                with dve.Fori(0, NC - 1) as c:
                    for b in range(B):
                        tile(c * B + b, b)
                for b in range(B):
                    tile((NC - 1) * B + b, b, last=True)
                dve.wait_ge(a_x, T + 1)

            dve.sem_inc(a_p, 1)
            dve.sem_inc(a_kd, 1)
            dve.sem_inc(a_x, 1)
            dve.sem_inc(w_lo, 2)
            dve.sem_inc(xl_ready, FREE)
            dve.sem_inc(hl_ready, FREE)
            dve.sem_inc(y_ready, FREE)
            for f in calls:
                routing(f)
                if f == 0:
                    scales()
                blocks(f)
                combine(f)
                if f == 0 and stop != "ffn":
                    attention()


def kernel(L0_attn_x, L0_attn_w_qkv, L0_attn_b_qkv, L0_attn_w_out, L0_attn_b_out, L0_ffn_Wr, L0_ffn_br,
           L0_ffn_w1, L0_ffn_b1, L0_ffn_w2, L0_ffn_b2, L0_ffn_Wp1, L0_ffn_bp1, L0_ffn_Wp2, L0_ffn_bp2):
    import concourse.bacc as bacc
    from concourse.bass_utils import run_bass_kernel_spmd

    nc, arrays = program(dict(
        x=L0_attn_x, w_qkv=L0_attn_w_qkv, b_qkv=L0_attn_b_qkv, w_out=L0_attn_w_out, b_out=L0_attn_b_out,
        Wr=L0_ffn_Wr, br=L0_ffn_br, w1=L0_ffn_w1, b1=L0_ffn_b1, w2=L0_ffn_w2, b2=L0_ffn_b2,
        Wp1=L0_ffn_Wp1, bp1=L0_ffn_bp1, Wp2=L0_ffn_Wp2, bp2=L0_ffn_bp2), bacc)
    r = run_bass_kernel_spmd(nc, [arrays], core_ids=[0])
    return r.results[0]["out"]


def program(a, bacc, stop=None):
    a = {k: np.asarray(v) for k, v in a.items()}
    cst, dmask = constants()
    arrays = {
        "x": a["x"], "w_qkvT": a["w_qkv"].T, "b_qkv": a["b_qkv"],
        "b_qkT": a["b_qkv"][:2 * D].reshape(2 * G, P).T, "w_outT": a["w_out"].T, "b_out": a["b_out"],
        "Wr": a["Wr"], "br": a["br"], "w1": a["w1"],
        "b1T": a["b1"].reshape(E, IC, P).transpose(2, 0, 1).reshape(P, E * IC),
        "w2": a["w2"], "b2": a["b2"], "Wp1": a["Wp1"], "bp1": a["bp1"], "Wp2": a["Wp2"], "bp2": a["bp2"],
        "cst": cst, "dmask": dmask,
    }
    arrays = {k: np.ascontiguousarray(v) for k, v in arrays.items()}
    nc = bacc.Bacc("TRN2", target_bir_lowering=False, num_devices=1)
    args = [nc.dram_tensor(k, v.shape, mybir.dt.from_np(v.dtype), kind="ExternalInput").ap()
            for k, v in arrays.items()]
    xn_dram = nc.dram_tensor("xn_rows", (T * P, D), F32, kind="Internal").ap()
    sums_dram = [nc.dram_tensor(f"expert_sums{f}", (TOKENS + SPARE, D), F32, kind="Internal").ap() for f in range(2)]
    out = nc.dram_tensor("out", (B, N, D), F32, kind="ExternalOutput").ap()
    build(nc, *args, xn_dram, sums_dram, out, stop=stop)
    return nc, arrays
```

```python
from contextlib import ExitStack

import numpy as np

import concourse.bass as bass
from concourse import mybir

ALU = mybir.AluOpType
ACT = mybir.ActivationFunctionType
AX = mybir.AxisListType
F32 = mybir.dt.float32
F16 = mybir.dt.float16
BF16 = mybir.dt.bfloat16
I32 = mybir.dt.int32
U32 = mybir.dt.uint32

P = 128
B, N, D = 4, 512, 256
T = B * N // P
NC = N // P
E, K, I = 12, 3, 640
KC, IC = D // P, I // P
W = 2
NB = 35
assert NB == (T * P * K - E) // (W * P) + E and NB % 2 == 1
NT = NB * W
ASSIGN = T * K
TOKENS = T * P
SPARE = W * P
AHEAD = 4
GROUP = 12
H, HD = 16, 16
G = 2
EPS = 1e-5
SLOT = 2 * IC * P
X_SCALE = 1024.0
H_SHIFT = 2.0 ** -14

_COLS = [("ident", P), ("tri", P), ("iota_p", P), ("iota_e", E), ("steps", T // W), ("iota_b", NT),
         ("row", 1), ("pad_place", NT), ("tile_mark", ASSIGN), ("reset", E * T), ("even", 1), ("odd", 1),
         ("decay_chunk", G), ("diag", P), ("decay_q", G * P), ("decay_k", D)]
CONST = {}
_at = 0
for _name, _n in _COLS:
    CONST[_name] = (_at, _n)
    _at += _n
CONST_N = _at


def constants():
    c = np.zeros((P, CONST_N), np.float32)

    def put(name, v):
        o, n = CONST[name]
        c[:, o:o + n] = v

    p = np.arange(P)
    put("ident", np.eye(P))
    put("tri", p[:, None] < p[None, :])
    put("iota_p", p[None, :])
    put("iota_e", np.arange(E)[None, :])
    put("steps", W * P * np.arange(T // W)[None, :])
    put("iota_b", np.arange(NT)[None, :])
    put("row", p[:, None])
    put("pad_place", P + T * P + np.arange(NT)[None, :] % W * P + p[:, None])
    put("tile_mark", np.arange(ASSIGN)[None, :] // K + 1)
    put("reset", (np.arange(E * T) % T != 0)[None, :])
    put("even", (p // HD % 2 == 0)[:, None])
    put("odd", (p // HD % 2 == 1)[:, None])
    start = 2.0 ** -0.5
    slopes = np.array([start ** (i + 1) for i in range(H)], np.float32)
    lam = np.exp(-slopes.astype(np.float64)).astype(np.float32).astype(np.float64)
    lg = lam.reshape(G, H // G).repeat(HD, axis=1).T
    put("decay_chunk", lg ** P)
    put("diag", p[:, None] // HD == p[None, :] // HD)
    put("decay_q", (lg[:, :, None] ** (p + 1.0)[None, None, :]).reshape(P, G * P))
    put("decay_k", lam.repeat(HD)[None, :] ** (P - 1.0 - p)[:, None])
    diff = p[None, :] - p[:, None]
    mask = np.where(diff[:, None, :] >= 0, lam[None, :, None] ** np.maximum(diff, 0)[:, None, :], 0.0)
    return c, mask.reshape(P, H * P).astype(np.float32)


class Chain:

    def __init__(self, eng, sem):
        self.eng, self.sem, self.n = eng, sem, 0

    def __call__(self, ins):
        ins.then_inc(self.sem, 1)
        self.n += 1

    def settle(self):
        self.eng.wait_ge(self.sem, self.n)


def build(nc, x, w_qkvT, b_qkv, b_qkT, w_outT, b_out, Wr, br, w1, b1T, w2, b2, Wp1, bp1, Wp2, bp2, cst, dmask,
          xn_dram, sums_dram, out):
    ctx = ExitStack()
    with ctx:
        def sb(name, shape, dt=F32):
            return ctx.enter_context(nc.sbuf_tensor(name, shape, dt))

        def sem(name):
            return ctx.enter_context(nc.semaphore(name))

        W1 = sb("W1", [P, (E + 1) * SLOT])
        W2 = sb("W2", [P, (E + 1) * SLOT])
        w1h = W1[:, :].bitcast(F16)
        w2h = W2[:, :].bitcast(F16)
        X = sb("X", [P, T, D])
        C = sb("C", [P, CONST_N])
        Wr_s = sb("Wr_s", [P, KC, E])
        Wr_h = sb("Wr_h", [P, KC, 2, E], F16)
        rscale = sb("rscale", [P, 2])
        back = sb("back", [P, 1])
        br_s = sb("br_s", [P, E])
        b1_s = sb("b1_s", [P, E * IC])
        b1s = sb("b1s", [P, E * IC])
        Wp1_s = sb("Wp1_s", [P, KC, P])
        bp1_s = sb("bp1_s", [P, 1])
        Wp2_s = sb("Wp2_s", [P, 1])
        Wp2_b = sb("Wp2_b", [P, P])
        bp2_s = sb("bp2_s", [P, 1])
        tri_h = sb("tri_h", [P, P], BF16)
        ones_h = sb("ones_h", [P, P], BF16)
        iota_h = sb("iota_h", [P, P], BF16)
        ones = sb("ones", [P, P])
        eps = sb("eps", [P, 1])
        ss = sb("ss", [P, E * 2])
        ssb = sb("ssb", [P, E * 2])
        dsc = sb("dsc", [P, E])
        n2 = sb("n2", [P, E * 2])
        ibits = sb("ibits", [P, E * 2], I32)
        ihalf = sb("ihalf", [P, E * 2], I32)
        iscl = sb("iscl", [P, E, 4], I32)
        zeros = sb("zeros", [P, P])
        wscale = sb("wscale", [P, E, 4])
        wsc = sb("wsc", [P, E])
        wexp = sb("wexp", [P, E])
        cntm = sb("cntm", [P, E])[:, :]
        eob = sb("eob", [P, NB], I32)
        token = sb("token", [P, NT], I32)
        place = sb("place", [P, NT], I32)
        tok_q = sb("tok_q", [P, 2 * W], I32)
        place_q = sb("place_q", [P, 2 * W], I32)
        mv = sb("mv", [P, T, 2])
        rstd = sb("rstd", [P, T])
        stats_next = sb("stats_next", [P, 6])
        mv_next = sb("mv_next", [P, 2])
        nmr = sb("nmr", [P, T])
        gate = sb("gate", [P, B])
        pooled = sb("pooled", [P, KC * B])
        phid = sb("phid", [P, B])

        def const(name):
            o, n = CONST[name]
            return C[:, o:o + n]

        ident = const("ident")

        AR = 12600
        A = sb("A", [P, AR])
        top = {"at": 0}

        def carve(n, dt=F32, at=None):
            if at is not None:
                top["at"] = at
            words = n if dt in (F32, I32, U32) else (n + 1) // 2
            o = top["at"]
            top["at"] = o + words
            assert o + words <= AR, (o + words, AR)
            ap = A[:, o:o + words]
            return ap if dt == F32 else ap.bitcast(dt)

        b2w = carve(E * D, at=0)
        bufs_at = top["at"]
        XG = [carve(W * D) for _ in range(2)]
        XH = [carve(W * D, F16).rearrange("p (k t) -> p k t", k=KC) for _ in range(2)]
        XL = [carve(W * D, F16).rearrange("p (k t) -> p k t", k=KC) for _ in range(2)]
        HF = [carve(W * I) for _ in range(2)]
        HH = [carve(W * I, F16) for _ in range(2)]
        HL = [carve(W * I, F16) for _ in range(2)]
        YO = [carve(W * D) for _ in range(2)]
        temps_at = ASSIGN * NT
        xn_at = temps_at + T * D
        XN = carve(T * D, at=xn_at).rearrange("p (i d) -> p i d", i=T)
        O = XN
        junk = (W1[:, 0:SLOT // 2].bitcast(BF16), carve(SLOT, BF16))
        XTH = [carve(2 * D, F16, at=q * 2 * D).rearrange("p (m c) -> p m c", m=2 * KC) for q in range(AHEAD)]
        XTL = [carve(2 * D, F16, at=(q * 2 + 1) * D).rearrange("p (m c) -> p m c", m=2 * KC) for q in range(AHEAD)]
        OHB = carve(ASSIGN * 2 * NT, BF16, at=0).rearrange("p (a n) -> p a n", a=ASSIGN)
        BSUM = A[:, bufs_at:bufs_at + B * D]
        OHA = carve(ASSIGN * P, BF16, at=xn_at).rearrange("p (a n) -> p a n", a=ASSIGN)
        OHR = [carve(GROUP * NT, BF16).rearrange("p (a n) -> p a n", a=GROUP) for _ in range(2)]
        r3 = "p (i e) -> p i e"
        stats = sb("stats", [P, T, 6])
        carve(T * 6, at=temps_at)
        CB = A[:, top["at"]:top["at"] + NB * E]
        LG = carve(T * E).rearrange(r3, i=T)
        V8 = carve(T * 8).rearrange(r3, i=T)
        I8 = carve(T * 8, U32).rearrange(r3, i=T)
        DX = carve(T * (E + K)).rearrange(r3, i=T)
        EX = carve(T * (E + K)).rearrange(r3, i=T)
        Z = carve(T)
        RZ = carve(T)
        P3 = carve(T * K).rearrange(r3, i=T)
        D3 = carve(T * K).rearrange(r3, i=T)
        E3 = carve(T * K).rearrange(r3, i=T)
        S3 = Z
        RS3 = RZ
        EW = carve(T * K).rearrange(r3, i=T)
        IF = carve(T * K).rearrange(r3, i=T)
        OH = carve(ASSIGN * E)
        OHv = OH.rearrange("p (i k e) -> p i k e", i=T, k=K)
        OW = carve(ASSIGN * E)
        OWv = OW.rearrange("p (i k e) -> p i k e", i=T, k=K)
        M = carve(T * E, BF16)
        EWS = carve(T * E)
        TOT = carve(E * T)
        INC = carve(E * T)
        EXC = carve(E * T)
        POS = carve(T * E)
        CMP = OW[:, 0:E * (T // W)]
        NBK = sb("NBK", [P, E])[:, :]
        BINC = carve(E)
        BEX = carve(E)
        DF = carve(ASSIGN)
        DI = carve(ASSIGN, I32)
        DBI = carve(ASSIGN, I32)
        DMI = carve(ASSIGN, I32)
        DB = carve(ASSIGN, BF16)
        DM = carve(ASSIGN, BF16)
        EOF = carve(NB)
        RF = carve(NT)
        BIG = carve(NT)
        PF = carve(NT)
        assert top["at"] <= xn_at, (top["at"], xn_at)

        dmask_s = carve(H * P, at=0).rearrange("p (g r s c) -> p g r s c", g=G, r=4, s=2)
        XNa = [carve(D) for _ in range(2)]
        XTa = [carve(D).rearrange("p (k c) -> p k c", k=KC) for _ in range(2)]
        QR = carve(D).rearrange("p (g c) -> p g c", g=G)
        QE = carve(D).rearrange("p (g c) -> p g c", g=G)
        QO = carve(D).rearrange("p (g c) -> p g c", g=G)
        QD = carve(D).rearrange("p (g c) -> p g c", g=G)
        KT = carve(D).rearrange("p (g c) -> p g c", g=G)
        KD = carve(D)
        V2 = carve(H * 2 * HD)
        V2w = V2.rearrange("p (q s n) -> p q s n", s=2, n=2 * HD)
        V2m = V2.rearrange("p (q m d) -> p q m d", m=4, d=HD)
        S = carve(B * G * P).rearrange("p (b g e) -> p b g e", b=B, g=G)
        AT = carve(D)
        assert top["at"] <= xn_at
        PM = [carve(D * 4).rearrange("p (r s c) -> p r s c", r=4, s=2) for _ in range(G)]
        TMP = carve(G * P).rearrange("p (g e) -> p g e", g=G)
        extra1 = W1[:, E * SLOT:(E + 1) * SLOT]
        extra2 = W2[:, E * SLOT:(E + 1) * SLOT]
        wqk_s = extra1[:, 0:KC * 2 * D].rearrange("p (k n) -> p k n", k=KC)
        bo_s = extra1[:, KC * 2 * D:KC * 2 * D + D]
        wv_s = extra2[:, 0:KC * D].rearrange("p (k n) -> p k n", k=KC)
        wo_s = extra2[:, KC * D:2 * KC * D].rearrange("p (k n) -> p k n", k=KC)
        bv_s = extra2[:, 2 * KC * D:2 * KC * D + D]
        bqk_s = sb("bqk_s", [P, 2 * G])

        PS = ctx.enter_context(nc.psum_tensor("PS", [P, 8, 512], F32))
        bank = [PS[:, i, :] for i in range(8)]

        x_in = [sem(f"x_in{j}") for j in range(NC)]
        small_in = sem("small_in")
        w_in = [sem(f"w_in{e}") for e in range(E)]
        set_up = sem("set_up")
        squares = sem("squares")
        normed = sem("normed")
        wr_normed = sem("wr_normed")
        wr_ready = sem("wr_ready")
        xt_high = sem("xt_high")
        scaled = sem("scaled")
        scale_steps = sem("scale_steps")
        w_hi = sem("w_hi")
        w_lo = sem("w_lo")
        dve_steps = sem("dve_steps")
        var_ready = sem("var_ready")
        sd_ready = sem("sd_ready")
        rstd_ready = sem("rstd_ready")
        xn_dve = sem("xn_dve")
        xn_act = sem("xn_act")
        xn_stored = sem("xn_stored")
        xt_psum = sem("xt_psum")
        xt_copied = sem("xt_copied")
        logits_ready = sem("logits_ready")
        diffs_ready = sem("diffs_ready")
        exps_ready = sem("exps_ready")
        member_ready = sem("member_ready")
        weight_ready = sem("weight_ready")
        counted = sem("counted")
        onehot_ready = sem("onehot_ready")
        table_psum = sem("table_psum")
        table_ready = sem("table_ready")
        b2_in = sem("b2_in")
        w_ready = sem("w_ready")
        b2w_ready = sem("b2w_ready")
        gathered = [sem(f"gathered{q}") for q in range(2)]
        idx_copied = sem("idx_copied")
        pool_held = sem("pool_held")
        dve_held = sem("dve_held")
        transposed = sem("transposed")
        xh_ready = sem("xh_ready")
        xl_ready = sem("xl_ready")
        layer1 = sem("layer1")
        relu_done = sem("relu_done")
        hh_ready = sem("hh_ready")
        hl_ready = sem("hl_ready")
        layer2 = sem("layer2")
        y_ready = sem("y_ready")
        y_sent = [sem(f"y_sent{q}") for q in range(2)]
        sums_in = [sem(f"sums_in{c}") for c in range(NC)]
        chunks_added = sem("chunks_added")
        zeros_ready = sem("zeros_ready")
        sums_cleared = [sem(f"sums_cleared{f}") for f in range(2)]
        raw_ready = sem("raw_ready")
        rows_marked = sem("rows_marked")
        tiles_marked = sem("tiles_marked")
        pool_psum = sem("pool_psum")
        pool_ready = sem("pool_ready")
        hid_psum = sem("hid_psum")
        hid_ready = sem("hid_ready")
        phi_psum = sem("phi_psum")
        phi_exp = sem("phi_exp")
        x_out = sem("x_out")
        x_new = sem("x_new")

        attn_w_in = sem("attn_w_in")
        dmask_in = sem("dmask_in")
        a_xn = sem("a_xn")
        a_xb = sem("a_xb")
        a_tp = sem("a_tp")
        a_xt = sem("a_xt")
        a_proj = sem("a_proj")
        a_qk = sem("a_qk")
        a_q = sem("a_q")
        a_qd = sem("a_qd")
        a_kv = sem("a_kv")
        a_ve = sem("a_ve")
        a_kd = sem("a_kd")
        a_sc = sem("a_sc")
        a_p = sem("a_p")
        a_st = sem("a_st")
        a_s = sem("a_s")
        a_s0 = sem("a_s0")
        a_tmp = sem("a_tmp")
        a_pv = sem("a_pv")
        a_at = sem("a_at")
        a_out = sem("a_out")
        a_x = sem("a_x")
        a_bn = sem("a_bn")
        a_stat = sem("a_stat")

        FREE = 2
        TURNS = ((NB + 1) // 2, NB // 2)
        CLEARS = 6
        UNROLL = 3

        block = ctx.enter_context(nc.Block())
        x_t = x.rearrange("b (c p) d -> p c b d", p=P)
        out_t = out.rearrange("b (c p) d -> p c b d", p=P)
        Xc = X[:, :, :].rearrange("p (c b) d -> p c b d", b=B)
        xn_t = xn_dram.rearrange("(i p) d -> p i d", p=P)
        sums_t = [s[0:TOKENS, :].rearrange("(i p) d -> p i d", p=P) for s in sums_dram]
        calls = (0, 1)

        def bcast_row(ap, n):
            return ap.rearrange("(a n) -> a n", a=1).to_broadcast([P, n])

        @block.sync
        def _(sp):
            for j in range(NC):
                sp.dma_start(Xc[:, j], x_t[:, j]).then_inc(x_in[j], 16)
                if j == 1:
                    sp.dma_start(C[:, :], cst).then_inc(small_in, 16)
            sp.dma_start(Wr_s[:, :, :], Wr.rearrange("(k p) e -> p k e", p=P)).then_inc(small_in, 16)
            sp.dma_start(br_s[:, :], bcast_row(br, E)).then_inc(small_in, 16)
            sp.dma_start(b1_s[:, :], b1T).then_inc(small_in, 16)
            sp.dma_start(Wp2_s[:, :], Wp2).then_inc(small_in, 16)
            sp.dma_start(bp2_s[:, :], bcast_row(bp2, 1)).then_inc(small_in, 16)
            sp.dma_start(bp1_s[:, :], bp1.rearrange("(p a) -> p a", a=1)).then_inc(small_in, 16)
            sp.dma_start(Wp1_s[:, :, :], Wp1.rearrange("(k p) j -> p k j", p=P)).then_inc(small_in, 16)
            def store_rows(f):
                for g in range(4):
                    sp.wait_ge(xn_dve, 8 * f + 2 * (g + 1))
                    sp.wait_ge(xn_act, 8 * f + 2 * (g + 1))
                    sp.dma_start(xn_t[:, 4 * g:4 * g + 4, :], XN[:, 4 * g:4 * g + 4, :]).then_inc(xn_stored, 16)

            for e in range(E):
                if e == E // 2:
                    store_rows(0)
                sp.dma_start(W1[:, (e + 1) * SLOT:(e + 2) * SLOT].rearrange("p (k i) -> p k i", k=KC),
                             w1[e].rearrange("(k p) i -> p k i", p=P)).then_inc(w_in[e], 16)
                sp.dma_start(W2[:, (e + 1) * SLOT:(e + 2) * SLOT].rearrange("p (c h) -> p c h", c=IC),
                             w2[e].rearrange("(c p) h -> p c h", p=P)).then_inc(w_in[e], 16)
            def clear_sums(f, piece, pieces):
                rows = sums_dram[f].rearrange("(p r) (h d) -> p (r h) d", p=P, d=P)
                n = rows.shape[1] // pieces
                sp.dma_start(rows[:, n * piece:n * (piece + 1)], zeros[:, :].unsqueeze(1).to_broadcast([P, n, P])
                             ).then_inc(sums_cleared[f], 16)

            def load_between_blocks():
                sp.wait_ge(w_lo, 4 + 4 * E)
                step = 0

                def after_a_block():
                    nonlocal step
                    step += 1
                    sp.wait_ge(y_sent[0], 16 * W * step)

                for k in range(KC):
                    rows = w_qkvT[k * P:(k + 1) * P, :]
                    after_a_block()
                    sp.dma_start(wqk_s[:, k, :], rows[:, 0:2 * D]).then_inc(attn_w_in, 16)
                    after_a_block()
                    sp.dma_start(wv_s[:, k, :], rows[:, 2 * D:3 * D]).then_inc(attn_w_in, 16)
                    sp.dma_start(wo_s[:, k, :], w_outT[k * P:(k + 1) * P, :]).then_inc(attn_w_in, 16)
                sp.dma_start(bo_s, bcast_row(b_out, D)).then_inc(attn_w_in, 16)
                sp.dma_start(bv_s, bcast_row(b_qkv[2 * D:3 * D], D)).then_inc(attn_w_in, 16)
                sp.dma_start(bqk_s[:, :], b_qkT).then_inc(attn_w_in, 16)
                for piece in range(CLEARS):
                    after_a_block()
                    clear_sums(1, piece, CLEARS)

            sp.wait_ge(zeros_ready, 1)
            clear_sums(0, 0, 1)
            for f in calls:
                if f == 1:
                    store_rows(1)
                sp.wait_ge(table_psum, f + 1)
                sp.dma_start(b2w, b2.rearrange("(a e) h -> a (e h)", a=1).to_broadcast([P, E * D])).then_inc(b2_in, 16)
                if f == 0:
                    load_between_blocks()
                for q in range(2):
                    sp.wait_ge(y_sent[q], 16 * W * TURNS[q] * (f + 1))
                for c in range(NC):
                    tiles = slice(c * B, (c + 1) * B)
                    sp.dma_start(O[:, tiles, :], sums_t[f][:, tiles, :]).then_inc(sums_in[c], 16)
                if f == 0:
                    sp.wait_ge(x_new, B)
                    sp.dma_start(dmask_s, dmask).then_inc(dmask_in, 16)
            for b in range(B):
                sp.wait_ge(x_new, 2 * B + b + 1)
                sp.dma_start(out_t[:, :, b], Xc[:, :, b]).then_inc(x_out, 16)
            sp.wait_ge(x_out, 16 * B)

        def scale_of(e, n):
            return wscale[:, bass.ds(e, 1), n:n + 1].rearrange("p a b -> p (a b)")

        @block.gpsimd
        def _(pool):
            def gather(f, b, q):
                pool.wait_ge(transposed, f * NB + b + 1)
                pool.sem_inc(pool_held, 1)
                nc.gpsimd.tensor_copy(tok_q[:, W * q:W * q + W], token[:, bass.ds(b * W, W)]).then_inc(idx_copied, 1)
                pool.wait_ge(idx_copied, idx(f, b, 0))
                pool.sem_inc(pool_held, 1)
                for u in range(W):
                    nc.gpsimd.indirect_dma_start(
                        XG[q][:, u * D:(u + 1) * D], None, xn_dram[:, :],
                        bass.IndirectOffsetOnAxis(ap=tok_q[:, W * q + u:W * q + u + 1], axis=0)
                    ).then_inc(gathered[q], 16)

            def scatter(f, b, q):
                if not isinstance(b, int) or b >= 1:
                    pool.wait_ge(y_sent[1 - q], landed(f, b, q))
                    pool.sem_inc(pool_held, 1)
                pool.wait_ge(y_ready, FREE + f * NB + b + 1)
                pool.sem_inc(pool_held, 1)
                nc.gpsimd.tensor_copy(place_q[:, W * q:W * q + W], place[:, bass.ds(b * W, W)]).then_inc(idx_copied, 1)
                pool.wait_ge(idx_copied, idx(f, b, 1))
                pool.sem_inc(pool_held, 1)
                for u in range(W):
                    nc.gpsimd.indirect_dma_start(
                        sums_dram[f][:, :],
                        bass.IndirectOffsetOnAxis(ap=place_q[:, W * q + u:W * q + u + 1], axis=0),
                        YO[q][:, u * D:(u + 1) * D], None, compute_op=ALU.add).then_inc(y_sent[q], 16)

            def landed(f, b, q):
                base = 16 * W * f * TURNS[1 - q]
                return (b + q) // 2 * 16 * W + base if isinstance(b, int) else (b + q) * (8 * W) + base

            def weigh_b2(f, start, stop_):
                pool.wait_ge(b2_in, 16 * (f + 1))
                pool.wait_ge(w_ready, f + 1)
                v = b2w.rearrange("p (e h) -> p e h", e=E)[:, start:stop_]
                nc.gpsimd.tensor_tensor(v, v, wexp[:, start:stop_].unsqueeze(2).to_broadcast([P, stop_ - start, D]),
                                        ALU.mult).then_inc(b2w_ready, 1)

            LAG = 4

            def idx(f, b, kind):
                if kind == 0:
                    if isinstance(b, int) and b < LAG:
                        return 2 * NB * f + b + 1
                    return b * 2 + (2 * NB * f - LAG + 1)
                if isinstance(b, int) and b >= NB - LAG:
                    return 2 * NB * f + NB + b + 1
                return b * 2 + (2 * NB * f + LAG + 2)

            pool.wait_ge(small_in, 16 * 8)
            for f in calls:
                for g in range(ASSIGN // GROUP):
                    pool.wait_ge(raw_ready, 4 * f + g + 1)
                    nc.gpsimd.tensor_tensor(
                        OHB[:, g * GROUP:(g + 1) * GROUP, NT:2 * NT], OHR[g % 2],
                        const("tile_mark")[:, g * GROUP:(g + 1) * GROUP].unsqueeze(2).to_broadcast([P, GROUP, NT]),
                        ALU.mult).then_inc(tiles_marked, 1)
                pool.wait_ge(sums_cleared[f], 16 * (1, CLEARS)[f])
                pool.wait_ge(table_ready, f + 1)
                pool.wait_ge(xn_stored, 64 * (f + 1))
                for b in range(LAG):
                    if f == 0 and b == 2:
                        weigh_b2(0, 0, E)
                    if f == 1 and b >= 2:
                        weigh_b2(1, E // 2 * (b - 2), E // 2 * (b - 1))
                    gather(f, b, b % 2)
                for q in range(2):
                    gather(f, LAG + q, q)
                    scatter(f, q, q)
                with pool.Fori(1, (NB - LAG) // 2) as j:
                    for q in range(2):
                        gather(f, j * 2 + (LAG + q), q)
                        scatter(f, j * 2 + q, q)
                gather(f, NB - 1, 0)
                for b in range(NB - LAG - 1, NB):
                    scatter(f, b, b % 2)
                if f == 0:
                    pool.wait_ge(x_new, B)
                    nc.gpsimd.memset(V2, 0.0)
                    nc.gpsimd.memset(S, 0.0).then_inc(a_s0, 1)
                    pool.wait_ge(x_new, 2 * B)
                    pool.wait_ge(attn_w_in, 16 * 9)
                    with pool.Fori(0, T) as t:
                        pool.wait_ge(a_xn, t + 1)
                        pool.sem_inc(pool_held, 1)
                        xi = X[:, bass.ds(t, 1), :].rearrange("p a d -> p (a d)")
                        nc.gpsimd.tensor_tensor(xi, xi, bo_s, ALU.add).then_inc(a_xb, 1)

        TB = bank[6].rearrange("p (k t) -> p k t", k=KC)

        def hidden(q, c):
            return bank[3 * q + c // 2][:, c % 2 * W * P:(c % 2 + 1) * W * P]

        @block.scalar
        def _(act):
            def square_sum(e, n):
                if n == 0:
                    act.wait_ge(w_in[e], 32)
                if e or n:
                    act.wait_ge(squares, 2 * e + n)
                raw = (W1, W2)[n]
                nc.scalar.activation(junk[e >= E // 2], raw[:, (e + 1) * SLOT:(e + 2) * SLOT], ACT.Square,
                                     accum_out=ss[:, 2 * e + n:2 * e + n + 1]).then_inc(squares, 1)

            def high_parts(e):
                for n, (raw, half) in enumerate(((W1, w1h), (W2, w2h))):
                    act.wait_ge(w_lo, e * 4 + (2 * n + 1))
                    nc.scalar.mul(half[:, bass.ds(e * (2 * SLOT), SLOT)], raw[:, bass.ds(e * SLOT + SLOT, SLOT)],
                                  scale_of(e, n)).then_inc(w_hi, 1)

            def deviation(n, first=0, end=T):
                act.wait_ge(var_ready, n + 1)
                nc.scalar.activation(rstd[:, first:end], nmr[:, first:end], ACT.Sqrt).then_inc(sd_ready, 1)
                act.wait_ge(rstd_ready, n + 1)

            def deviation_ahead(t):
                act.wait_ge(var_ready, t + 3)
                nc.scalar.activation(rstd[:, bass.ds(t + B, 1)], nmr[:, bass.ds(t + B, 1)],
                                     ACT.Sqrt).then_inc(sd_ready, 1)

            def attention():
                deviation(1, 0, B)
                act.wait_ge(attn_w_in, 16 * 9)

                def normalise(t, b, ahead=True):
                    if ahead:
                        act.wait_ge(rstd_ready, t - (B - 3))
                    act.wait_ge(a_tp, t + 1)
                    nc.scalar.activation(XNa[b % 2], X[:, bass.ds(t, 1), :].rearrange("p a d -> p (a d)"),
                                         ACT.Identity, bias=nmr[:, bass.ds(t, 1)],
                                         scale=rstd[:, bass.ds(t, 1)]).then_inc(a_xn, 1)

                def columns(t, b):
                    act.wait_ge(a_tp, t + 3)
                    act.wait_ge(a_kv, t + 1)
                    nc.scalar.copy(XTa[b % 2], bank[4][:, 0:D].rearrange("p (k c) -> p k c", k=KC)).then_inc(a_xt, 1)

                def queries_keys(t):
                    act.wait_ge(a_proj, t + 1)
                    act.wait_ge(a_sc, t * 2 + 1)
                    act.wait_ge(a_qd, t + 1)
                    for n, dst in ((0, QR[:, 0]), (2, KT[:, 0]), (1, QR[:, 1]), (3, KT[:, 1])):
                        nc.scalar.activation(dst, bank[4][:, n * P:(n + 1) * P], ACT.Identity,
                                             bias=bqk_s[:, n:n + 1]).then_inc(a_qk, 1)

                def rows_out(t):
                    act.wait_ge(a_pv, t * 2 + 4)
                    act.wait_ge(a_out, t + 1)
                    nc.scalar.copy(AT, bank[6][:, 0:D]).then_inc(a_at, 1)

                def tile(t, b, last=False):
                    if not (last and b == B - 1):
                        columns(t + 1, b + 1)
                    if not (last and b >= B - 2):
                        normalise(t + 2, b)
                    if not (last and b == B - 1):
                        queries_keys(t + 1)
                    if not last:
                        deviation_ahead(t)
                    rows_out(t)

                normalise(0, 0, ahead=False)
                normalise(1, 1, ahead=False)
                columns(0, 0)
                queries_keys(0)
                with act.Fori(0, NC - 1) as c:
                    for b in range(B):
                        tile(c * B + b, b)
                for b in range(B):
                    tile((NC - 1) * B + b, b, last=True)

            def routing(f):
                deviation((T - B + 2) * f)
                for i in range(1, T, 2):
                    nc.scalar.activation(XN[:, i, :], X[:, i, :], ACT.Identity, bias=nmr[:, i:i + 1],
                                         scale=rstd[:, i:i + 1]).then_inc(xn_act, 1)
                if f == 0:
                    for m in range(E):
                        square_sum(m // 2, m % 2)
                for n in range(2):
                    act.wait_ge(diffs_ready, 2 * f + n + 1)
                    src, dst = ((DX, EX), (D3, E3))[n]
                    nc.scalar.activation(dst, src, ACT.Exp).then_inc(exps_ready, 1)
                if f == 0:
                    for m in range(2):
                        square_sum(6, m)
                act.wait_ge(small_in, 16 * 8)
                for g in range(ASSIGN // GROUP):
                    act.wait_ge(raw_ready, 4 * f + g + 1)
                    nc.scalar.activation(OHB[:, g * GROUP:(g + 1) * GROUP, 0:NT], OHR[g % 2], ACT.Identity,
                                         scale=const("row")).then_inc(rows_marked, 1)
                if f == 0:
                    for m in range(2 * 7, 2 * 9):
                        square_sum(m // 2, m % 2)
                    act.wait_ge(scaled, 1)
                    for e in range(E // 2):
                        high_parts(e)
                        square_sum(9 + e // 2, e % 2)
                    act.wait_ge(scaled, 2)
                    with act.Fori(E // 2 // UNROLL, E // UNROLL) as j:
                        for u in range(UNROLL):
                            high_parts(j * UNROLL + u)

            def blocks(f):
                def high(b, q):
                    act.wait_ge(transposed, FREE + f * NB + b + 1)
                    act.wait_ge(layer1, f * NB + b + 1)
                    nc.scalar.mul(XH[q], TB, X_SCALE).then_inc(xh_ready, 1)

                def relu(b, q):
                    e = act.value_load(eob[0:1, bass.ds(b, 1)], min_val=0, max_val=E - 1)
                    act.wait_ge(layer1, FREE + f * NB + b + 1)
                    act.wait_ge(hl_ready, f * NB + b + 1)
                    for c in range(IC):
                        ins = nc.scalar.activation(HF[q][:, c * W * P:(c + 1) * W * P], hidden(q, c),
                                                   ACT.Relu, bias=b1s[:, bass.ds(e * IC + c, 1)],
                                                   scale=H_SHIFT)
                    ins.then_inc(relu_done, 1)

                high(0, 0)
                with act.Fori(0, (NB - 1) // 2) as j:
                    for q in range(2):
                        high(j * 2 + (q + 1), 1 - q)
                        relu(j * 2 + q, q)
                relu(NB - 1, 0)

            def combine(f):
                act.wait_ge(hid_psum, f + 1)
                nc.scalar.activation(phid[:, :], bank[2][:, 0:B], ACT.Relu, bias=bp1_s[:, :]).then_inc(hid_ready, 1)
                act.wait_ge(phi_psum, f + 1)
                nc.scalar.activation(gate[:, :], bank[3][:, 0:B], ACT.Exp, bias=bp2_s[:, :],
                                     scale=-1.0).then_inc(phi_exp, 1)

            act.sem_inc(relu_done, FREE)
            act.sem_inc(a_at, 1)
            act.sem_inc(a_qk, 1)
            for f in calls:
                routing(f)
                blocks(f)
                combine(f)
                if f == 0:
                    attention()

        @block.tensor
        def _(pe):
            def matmul(out_, l, r, start, stop_):
                return nc.tensor.matmul(out_, l, r, start=start, stop=stop_, skip_group_check=True)

            def norms(half):
                pe.wait_ge(squares, E * (half + 1))
                cols = slice(E * half, E * (half + 1))
                matmul(bank[6 + half][:, 0:E], ones[:, :], ss[:, cols], True, False)
                matmul(bank[6 + half][:, 0:E], ones[:, :], ssb[:, cols], False, True).then_inc(normed, 1)

            def routing(f):
                if f == 0:
                    matmul(bank[3][:, 0:KC * E], ones[:, :], b1s[:, 0:KC * E], True, True).then_inc(wr_normed, 1)
                for j in range(T // 2 + 2):
                    if f == 0 and j == 2:
                        pe.wait_ge(wr_ready, 1)
                    if j < T // 2:
                        pe.wait_ge(xn_dve, 8 * f + j + 1)
                        pe.wait_ge(xn_act, 8 * f + j + 1)
                        if j >= AHEAD:
                            pe.wait_ge(xt_copied, T // 2 * f + j - AHEAD + 1)
                        for u in range(2):
                            for k in range(KC):
                                ins = nc.tensor.transpose(
                                    bank[4 + j % AHEAD][:, (u * KC + k) * P:(u * KC + k + 1) * P],
                                    XN[:, 2 * j + u, k * P:(k + 1) * P], ident)
                        ins.then_inc(xt_psum, 1)
                    if j >= 2:
                        pe.wait_ge(xt_copied, T // 2 * f + j - 1)
                        for u in range(2):
                            at = (2 * (j - 2) + u) * 2 * E
                            for k in range(KC):
                                matmul(bank[0][:, at:at + 2 * E], XTH[(j - 2) % AHEAD][:, u * KC + k, :],
                                       Wr_h[:, k].rearrange("p n e -> p (n e)"), k == 0, False)
                                ins = matmul(bank[0][:, at:at + E], XTL[(j - 2) % AHEAD][:, u * KC + k, :],
                                             Wr_h[:, k, 0, :], False, k == KC - 1)
                        ins.then_inc(logits_ready, 1)
                pe.wait_ge(member_ready, f + 1)
                matmul(bank[1][:, 0:T * E], tri_h[:, :], M, True, True)
                matmul(bank[1][:, 256:256 + T * E], ones_h[:, :], M, True, True).then_inc(counted, 1)
                if f == 0:
                    norms(0)
                for g in range(4):
                    pe.wait_ge(onehot_ready, 4 * f + g + 1)
                    pe.wait_ge(rows_marked, 4 * f + g + 1)
                    pe.wait_ge(tiles_marked, 4 * f + g + 1)
                    for a in range(GROUP * g, GROUP * (g + 1)):
                        ins = matmul(bank[3][:, 0:2 * NT], OHA[:, a, :], OHB[:, a, :], a == 0, a == ASSIGN - 1)
                ins.then_inc(table_psum, 1)
                pe.wait_ge(weight_ready, f + 1)
                matmul(bank[2][:, 0:T * E], ones[:, :], EWS, True, True).then_inc(counted, 1)
                if f == 0:
                    norms(1)

            def blocks(f):
                def transposes(b, q):
                    pe.wait_ge(gathered[q], gcount(f, b, q))
                    pe.wait_ge(xl_ready, f * NB + b + 2)
                    for u in range(W):
                        for k in range(KC):
                            ins = nc.tensor.transpose(TB[:, k, u * P:(u + 1) * P],
                                                      XG[q][:, u * D + k * P:u * D + (k + 1) * P], ident)
                    ins.then_inc(transposed, 1)

                def first(b, q):
                    e = pe.value_load(eob[0:1, bass.ds(b, 1)], min_val=0, max_val=E - 1)
                    pe.wait_ge(xl_ready, FREE + f * NB + b + 1)
                    pe.wait_ge(relu_done, f * NB + b + 1)
                    for c in range(IC):
                        dst = hidden(q, c)
                        n = 0
                        for k in range(KC):
                            for part, src in ((0, XH), (0, XL), (1, XH)):
                                w = w1h[:, bass.ds(e * (2 * SLOT) + (part * SLOT + k * I + c * P), P)]
                                ins = matmul(dst, w, src[q][:, k, :], n == 0, n == 5)
                                n += 1
                    ins.then_inc(layer1, 1)

                def second(b, q):
                    e = pe.value_load(eob[0:1, bass.ds(b, 1)], min_val=0, max_val=E - 1)
                    pe.wait_ge(hl_ready, FREE + f * NB + b + 1)
                    pe.wait_ge(y_ready, f * NB + b + 2)
                    n = 0
                    for c in range(IC):
                        for part, src in ((0, HH), (0, HL), (1, HH)):
                            w = w2h[:, bass.ds(e * (2 * SLOT) + (part * SLOT + c * D), D)]
                            for u in range(W):
                                ins = matmul(bank[7][:, u * D:(u + 1) * D],
                                             src[q][:, (c * W + u) * P:(c * W + u + 1) * P], w,
                                             n == 0 and u == 0, n == 14)
                            n += 1
                    ins.then_inc(layer2, 1)

                transposes(0, 0)
                transposes(1, 1)
                if f == 0:
                    pe.wait_ge(w_lo, 4 + 4 * E)
                first(0, 0)
                with pe.Fori(0, (NB - 3) // 2) as j:
                    for u in range(2):
                        transposes(j * 2 + (u + 2), u)
                        first(j * 2 + (u + 1), 1 - u)
                        second(j * 2 + u, u)
                transposes(NB - 1, 0)
                first(NB - 2, 1)
                second(NB - 3, 0)
                first(NB - 1, 0)
                second(NB - 2, 1)
                second(NB - 1, 0)

            def gcount(f, b, q):
                base = 16 * W * (f * TURNS[q] + 1)
                return (b - q) // 2 * 16 * W + base if isinstance(b, int) else (b - q) * (8 * W) + base

            def combine(f):
                pe.wait_ge(chunks_added, (NC - 1) * (f + 1))
                for k in range(KC):
                    for b in range(B):
                        col = k * B + b
                        ins = matmul(bank[1][:, col:col + 1], BSUM[:, b * D + k * P:b * D + (k + 1) * P],
                                     ones[:, 0:1], True, True)
                ins.then_inc(pool_psum, 1)
                pe.wait_ge(pool_ready, f + 1)
                for k in range(KC):
                    ins = matmul(bank[2][:, 0:B], Wp1_s[:, k, :], pooled[:, k * B:(k + 1) * B], k == 0, k == KC - 1)
                ins.then_inc(hid_psum, 1)
                pe.wait_ge(hid_ready, f + 1)
                matmul(bank[3][:, 0:B], Wp2_b[:, :], phid[:, :], True, True).then_inc(phi_psum, 1)

            def attention():
                pe.wait_ge(attn_w_in, 16 * 9)

                def columns(t, b):
                    pe.wait_ge(a_xn, t + 1)
                    pe.wait_ge(a_qk, t * 4 + 1)
                    for k in range(KC):
                        ins = nc.tensor.transpose(bank[4][:, k * P:(k + 1) * P], XNa[b % 2][:, k * P:(k + 1) * P],
                                                  ident)
                    ins.then_inc(a_tp, 1)

                def queries_keys(t, b):
                    pe.wait_ge(a_xt, t + 1)
                    for n in range(4):
                        for k in range(KC):
                            ins = matmul(bank[4][:, n * P:(n + 1) * P], wqk_s[:, k, n * P:(n + 1) * P],
                                         XTa[b % 2][:, k, :], k == 0, k == KC - 1)
                    ins.then_inc(a_proj, 1)

                def values_keys(t, b):
                    pe.wait_ge(a_qk, t * 4 + 5)
                    pe.wait_ge(a_kd, t + 1)
                    for k in range(KC):
                        matmul(bank[5][:, 0:D], XTa[b % 2][:, k, :], wv_s[:, k, :], k == 0, k == KC - 1)
                    for g in range(G):
                        ins = nc.tensor.transpose(bank[5][:, D + g * P:D + (g + 1) * P], KT[:, g, :], ident)
                    ins.then_inc(a_kv, 1)

                def scores(t, g):
                    pe.wait_ge(a_qk, t * 4 + (2 * g + 3))
                    pe.wait_ge(a_q, t * 2 + (g + 1))
                    pe.wait_ge(a_p, t * 2 + (g + 1))
                    for s in range(2):
                        q = (QE, QO)[s]
                        for r in range(4):
                            rows = slice(32 * r, 32 * r + 32)
                            ins = matmul(bank[r][:, s * P:(s + 1) * P], KT[rows, g, :], q[rows, g, :], True, True)
                    ins.then_inc(a_sc, 1)

                def from_state(t, b):
                    pe.wait_ge(a_qd, t + 2)
                    pe.wait_ge(a_s, t + 1)
                    pe.wait_ge(a_at, t + 1)
                    for g in range(G):
                        matmul(bank[6][:, g * P:(g + 1) * P], S[:, b, g, :], QD[:, g, :], g == 0, False)

                def from_chunk(t, g):
                    pe.wait_ge(a_p, t * 2 + (g + 2))
                    if g == 0:
                        pe.wait_ge(a_ve, t + 1)
                    for s in range(2):
                        for r in range(4):
                            ins = matmul(bank[6][32 * r:32 * r + 32, g * P:(g + 1) * P], V2w[:, 4 * g + r, s, :],
                                         PM[g][:, r, s, :], False, g == G - 1 and s == 1)
                    ins.then_inc(a_pv, 1)

                def state(t):
                    pe.wait_ge(a_kd, t + 2)
                    pe.wait_ge(a_x, t + 1)
                    for g in range(G):
                        ins = matmul(bank[7][:, g * P:(g + 1) * P], KD[:, g * P:(g + 1) * P],
                                     V2m[:, 4 * g:4 * g + 4, 0:4:3, :], True, True)
                    ins.then_inc(a_st, 1)

                def out_proj(t):
                    pe.wait_ge(a_at, t + 2)
                    pe.wait_ge(a_s, t + 5)
                    for k in range(KC):
                        ins = matmul(bank[7][:, D:2 * D], AT[:, k * P:(k + 1) * P], wo_s[:, k, :],
                                     k == 0, k == KC - 1)
                    ins.then_inc(a_out, 1)

                def tile(t, b, last=False):
                    more = not (last and b == B - 1)
                    if more:
                        columns(t + 1, b + 1)
                    values_keys(t, b)
                    from_state(t, b)
                    scores(t, 1)
                    if more:
                        queries_keys(t + 1, b + 1)
                    from_chunk(t, 0)
                    state(t)
                    from_chunk(t, 1)
                    if more:
                        scores(t + 1, 0)
                    out_proj(t)

                columns(0, 0)
                queries_keys(0, 0)
                pe.wait_ge(a_s0, 1)
                scores(0, 0)
                with pe.Fori(0, NC - 1) as c:
                    for b in range(B):
                        tile(c * B + b, b)
                for b in range(B):
                    tile((NC - 1) * B + b, b, last=True)

            pe.sem_inc(a_tp, 2)
            pe.sem_inc(a_kv, 2)
            pe.sem_inc(a_sc, 1)
            pe.sem_inc(a_pv, 2)
            pe.sem_inc(a_out, 1)
            pe.sem_inc(transposed, FREE)
            pe.sem_inc(layer1, FREE)
            pe.sem_inc(layer2, FREE)
            pe.wait_ge(set_up, 1)
            for f in calls:
                routing(f)
                blocks(f)
                combine(f)
                if f == 0:
                    attention()

        @block.vector
        def _(dve):
            step = Chain(dve, dve_steps)

            def set_up_tables():
                v = nc.vector
                v.memset(zeros[:, :], 0.0).then_inc(zeros_ready, 1)
                v.memset(ssb[:, :], 0.0).then_inc(zeros_ready, 1)
                dve.wait_ge(zeros_ready, 2)
                dve.wait_ge(small_in, 16 * 8)
                v.memset(ones[:, :], 1.0)
                v.memset(ones_h[:, :], 1.0)
                v.tensor_copy(tri_h[:, :], const("tri"))
                v.tensor_copy(iota_h[:, :], const("iota_p"))
                v.memset(eps[:, :], EPS)
                v.tensor_scalar(bp2_s[:, :], bp2_s[:, :], -1.0, None, ALU.mult)
                step(v.tensor_tensor(b1s[:, :], b1_s[:, :], b1_s[:, :], ALU.mult))
                step(v.tensor_copy(Wp2_b[:, :], Wp2_s[:, :].to_broadcast([P, P])))
                step.settle()
                step(v.tensor_reduce(ssb[:, :].rearrange("p (e n) -> p e n", n=2)[:, :, 0],
                                     b1s[:, :].rearrange("p (e c) -> p e c", c=IC), AX.X, ALU.add))
                step.settle()
                wr = Wr_s[:, :, :].rearrange("p k e -> p (k e)")
                v.tensor_tensor(b1s[:, 0:KC * E], wr, wr, ALU.mult).then_inc(set_up, 1)

            def power_of_two(norm2, cols, scale, inverse):
                v = nc.vector
                step(v.tensor_scalar(n2[:, cols], norm2, 1e-30, None, ALU.max))
                step.settle()
                step(v.tensor_scalar(ibits[:, cols], n2[:, cols].bitcast(I32), 23, None, ALU.logical_shift_right))
                step.settle()
                step(v.tensor_scalar(ihalf[:, cols], ibits[:, cols], 1.0, None, ALU.add))
                step.settle()
                step(v.tensor_scalar(ibits[:, cols], ihalf[:, cols], 1, None, ALU.logical_shift_right))
                step.settle()
                half = ibits[:, cols] if cols.stop - cols.start == 1 else ibits[:, cols].rearrange(
                    "p (e n) -> p e n", n=2)
                step(v.tensor_scalar(scale, half, -1.0, 205.0, ALU.mult, ALU.add))
                step(v.tensor_scalar(inverse, half, 49.0, None, ALU.add))
                step.settle()

            def router_weights():
                v = nc.vector
                dve.wait_ge(wr_normed, 1)
                step(v.tensor_reduce(back[:, :], bank[3][:, 0:KC * E], AX.X, ALU.add))
                step.settle()
                bits = iscl[:, 0, :]
                power_of_two(back[:, :], slice(0, 1), bits[:, 0:1], bits[:, 1:2])
                step(v.tensor_scalar(rscale[:, :].bitcast(I32), bits[:, 0:2], 23, None, ALU.logical_shift_left))
                step.settle()
                step(v.tensor_scalar(back[:, :], rscale[:, 1:2], 1.0 / X_SCALE, None, ALU.mult))
                step(v.tensor_scalar(Wr_h[:, :, 0, :], Wr_s[:, :, :], rscale[:, 0:1], None, ALU.mult))
                step.settle()
                step(v.scalar_tensor_tensor(Wr_h[:, :, 1, :], Wr_s[:, :, :], rscale[:, 0:1], Wr_h[:, :, 0, :],
                                            ALU.mult, ALU.subtract))
                step.settle()
                dve.sem_inc(wr_ready, 1)

            def scales(half):
                v = nc.vector
                cols = slice(E * half, E * (half + 1))
                es = slice(E // 2 * half, E // 2 * (half + 1))
                dve.wait_ge(normed, half + 1)
                power_of_two(bank[6 + half][:, 0:E], cols, iscl[:, es, 0:2], iscl[:, es, 2:4])
                v.tensor_scalar(wscale[:, es, :].bitcast(I32), iscl[:, es, :], 23, None,
                                ALU.logical_shift_left).then_inc(scaled, 1)

            def low_parts(start, stop_):
                v = nc.vector
                with dve.Fori(start // UNROLL, stop_ // UNROLL) as j:
                    for u in range(UNROLL):
                        for n, (raw, cut) in enumerate(((W1, w1h), (W2, w2h))):
                            e = j * UNROLL + u
                            dve.wait_ge(w_hi, e * 2 + (n + 1))
                            dve.wait_ge(w_lo, e * 4 + (2 * n + 2))
                            for piece in range(2):
                                at = piece * (SLOT // 2)
                                v.scalar_tensor_tensor(cut[:, bass.ds(e * (2 * SLOT) + (SLOT + at), SLOT // 2)],
                                                       raw[:, bass.ds(e * SLOT + (SLOT + at), SLOT // 2)],
                                                       scale_of(e, n),
                                                       cut[:, bass.ds(e * (2 * SLOT) + at, SLOT // 2)],
                                                       ALU.mult, ALU.subtract).then_inc(w_lo, 1)

            def bias_scales():
                v = nc.vector
                dve.wait_ge(scaled, 2)
                b3 = "p (e c) -> p e c"
                step(v.scalar_tensor_tensor(b1s[:, :].rearrange(b3, c=IC), b1_s[:, :].rearrange(b3, c=IC),
                                            X_SCALE * H_SHIFT, wscale[:, :, 0:1].to_broadcast([P, E, IC]),
                                            ALU.mult, ALU.mult))
                step(v.scalar_tensor_tensor(dsc[:, :], wscale[:, :, 2], 1.0 / (X_SCALE * H_SHIFT),
                                            wscale[:, :, 3], ALU.mult, ALU.mult))
                dve.wait_ge(w_lo, 4 + 4 * E)
                step.settle()

            def row_stats(n, first, end, measured=None):
                v = nc.vector
                if measured is None:
                    measured = stats
                    for i in range(first, end):
                        if n == 0 and i % B == 0:
                            dve.wait_ge(x_in[i // B], 16)
                        step(v.bn_stats(stats[:, i, :], X[:, i, :]))
                    step.settle()
                for i in range(first, end):
                    step(v.bn_aggr(mv[:, i, :], measured[:, i, :]))
                step.settle()
                v.tensor_scalar(nmr[:, first:end], mv[:, first:end, 1], EPS, None, ALU.add).then_inc(var_ready, 1)
                if n == 0:
                    set_up_tables()
                dve.wait_ge(sd_ready, n + 1)
                step(v.reciprocal(rstd[:, first:end], rstd[:, first:end]))
                step.settle()
                v.scalar_tensor_tensor(nmr[:, first:end], mv[:, first:end, 0], -1.0, rstd[:, first:end], ALU.mult,
                                       ALU.mult).then_inc(rstd_ready, 1)
                dve.wait_ge(rstd_ready, n + 1)

            def routing(f):
                v = nc.vector
                if f == 0:
                    row_stats(0, 0, T)
                else:
                    row_stats(T - B + 2, 0, T, measured=stats)
                for i in range(0, T, 2):
                    v.tensor_scalar(XN[:, i, :], X[:, i, :], rstd[:, i:i + 1], nmr[:, i:i + 1],
                                    ALU.mult, ALU.add).then_inc(xn_dve, 1)
                for j in range(T // 2):
                    if f == 0 and j == 0:
                        router_weights()
                    dve.wait_ge(xt_psum, T // 2 * f + j + 1)
                    if j >= AHEAD:
                        dve.wait_ge(logits_ready, T // 2 * f + j - AHEAD + 1)
                    src = bank[4 + j % AHEAD].rearrange("p (m c) -> p m c", m=2 * KC)
                    v.tensor_scalar(XTH[j % AHEAD], src, X_SCALE, None, ALU.mult).then_inc(xt_high, 1)
                    dve.wait_ge(xt_high, T // 2 * f + j + 1)
                    v.scalar_tensor_tensor(XTL[j % AHEAD], src, X_SCALE, XTH[j % AHEAD], ALU.mult,
                                           ALU.subtract).then_inc(xt_copied, 1)
                dve.wait_ge(logits_ready, T // 2 * (f + 1))
                parts = bank[0][:, 0:T * 2 * E].rearrange("p (i n e) -> p i n e", i=T, n=2)
                step(v.scalar_tensor_tensor(LG, parts[:, :, 0, :], back[:, :],
                                            br_s[:, :].unsqueeze(1).to_broadcast([P, T, E]), ALU.mult, ALU.add))
                step.settle()
                step(v.scalar_tensor_tensor(LG, parts[:, :, 1, :], back[:, :], LG, ALU.mult, ALU.add))
                step.settle()
                for i in range(T):
                    step(v.max(V8[:, i, :], LG[:, i, :]))
                step.settle()
                for i in range(T):
                    step(v.max_index(I8[:, i, :], V8[:, i, :], LG[:, i, :]))
                top1 = V8[:, :, 0:1]
                v.tensor_tensor(DX[:, :, E:E + K], V8[:, :, 0:K], top1.to_broadcast([P, T, K]), ALU.subtract)
                v.tensor_tensor(DX[:, :, 0:E], LG, top1.to_broadcast([P, T, E]),
                                ALU.subtract).then_inc(diffs_ready, 1)
                step.settle()
                step(v.tensor_copy(IF, I8[:, :, 0:K]))
                step.settle()
                step(v.tensor_tensor(OHv, IF.unsqueeze(3).to_broadcast([P, T, K, E]),
                                     const("iota_e").unsqueeze(1).unsqueeze(1).to_broadcast([P, T, K, E]),
                                     ALU.is_equal))
                step.settle()
                with nc.allow_low_precision(reason="sums of zeros and at most one one"):
                    v.tensor_reduce(M, OHv.rearrange("p i k e -> p i e k"), AX.X, ALU.add).then_inc(member_ready, 1)
                dve.wait_ge(exps_ready, 2 * f + 1)
                step(v.tensor_reduce(Z, EX[:, :, 0:E], AX.X, ALU.add))
                step.settle()
                step(v.reciprocal(RZ, Z))
                step.settle()
                step(v.tensor_tensor(P3, EX[:, :, E:E + K], RZ.unsqueeze(2).to_broadcast([P, T, K]), ALU.mult))
                step.settle()
                v.tensor_tensor(D3, P3, P3[:, :, 0:1].to_broadcast([P, T, K]),
                                ALU.subtract).then_inc(diffs_ready, 1)
                dve.wait_ge(counted, 2 * f + 1)
                step(v.tensor_copy(TOT.rearrange("p (e i) -> p e i", e=E),
                                   bank[1][:, 256:256 + T * E].rearrange("p (i e) -> p e i", e=E)))
                step.settle()
                step(v.tensor_tensor_scan(INC, const("reset"), TOT, 0.0, ALU.mult, ALU.add))
                step.settle()
                cnt = INC.rearrange("p (e i) -> p e i", e=E)[:, :, T - 1:T]
                step(v.tensor_tensor(EXC, INC, TOT, ALU.subtract))
                step(v.tensor_tensor(CMP.rearrange("p (e i) -> p e i", e=E), cnt.to_broadcast([P, E, T // W]),
                                     const("steps").unsqueeze(1).to_broadcast([P, E, T // W]), ALU.is_gt))
                step.settle()
                step(v.tensor_reduce(NBK, CMP.rearrange("p (e i) -> p e i", e=E), AX.X, ALU.add))
                step.settle()
                step(v.tensor_tensor_scan(BINC, ones[:, 0:E], NBK, 0.0, ALU.mult, ALU.add))
                step.settle()
                step(v.tensor_tensor(BEX, BINC, NBK, ALU.subtract))
                step.settle()
                e3 = EXC.rearrange("p (e i) -> p e i", e=E)
                step(v.scalar_tensor_tensor(e3, BEX.unsqueeze(2).to_broadcast([P, E, T]), float(W * P), e3,
                                            ALU.mult, ALU.add))
                step.settle()
                step(v.tensor_tensor(POS.rearrange(r3, i=T), bank[1][:, 0:T * E].rearrange(r3, i=T),
                                     EXC.rearrange("p (e i) -> p i e", e=E), ALU.add))
                step.settle()
                step(v.tensor_tensor(OWv, OHv, POS.rearrange(r3, i=T).unsqueeze(2).to_broadcast([P, T, K, E]),
                                     ALU.mult))
                step.settle()
                step(v.tensor_reduce(DF, OW.rearrange("p (a e) -> p a e", e=E), AX.X, ALU.add))
                step.settle()
                step(v.tensor_copy(DI, DF))
                step.settle()
                step(v.tensor_scalar(DBI, DI, 7, None, ALU.logical_shift_right))
                step(v.tensor_scalar(DMI, DI, P - 1, None, ALU.bitwise_and))
                step.settle()
                step(v.tensor_copy(DB, DBI))
                step(v.tensor_copy(DM, DMI))
                step.settle()
                dve.wait_ge(xn_stored, 64 * (f + 1))
                dve.wait_ge(xt_psum, T // 2 * (f + 1))
                for g in range(ASSIGN // GROUP):
                    pairs = slice(g * GROUP, (g + 1) * GROUP)
                    if g >= 2:
                        dve.wait_ge(rows_marked, 4 * f + g - 1)
                        dve.wait_ge(tiles_marked, 4 * f + g - 1)
                    v.tensor_tensor(OHR[g % 2], iota_h[:, 0:NT].unsqueeze(1).to_broadcast([P, GROUP, NT]),
                                    DB[:, pairs].unsqueeze(2).to_broadcast([P, GROUP, NT]),
                                    ALU.is_equal).then_inc(raw_ready, 1)
                    v.tensor_tensor(OHA[:, pairs, :], iota_h[:, :].unsqueeze(1).to_broadcast([P, GROUP, P]),
                                    DM[:, pairs].unsqueeze(2).to_broadcast([P, GROUP, P]),
                                    ALU.is_equal).then_inc(onehot_ready, 1)
                dve.wait_ge(exps_ready, 2 * f + 2)
                step(v.tensor_reduce(S3, E3, AX.X, ALU.add))
                step.settle()
                step(v.reciprocal(RS3, S3))
                step.settle()
                step(v.tensor_tensor(EW, E3, RS3.unsqueeze(2).to_broadcast([P, T, K]), ALU.mult))
                step.settle()
                step(v.tensor_tensor(OWv, OHv, EW.unsqueeze(3).to_broadcast([P, T, K, E]), ALU.mult))
                step.settle()
                v.tensor_reduce(EWS.rearrange(r3, i=T), OWv.rearrange("p i k e -> p i e k"), AX.X,
                                ALU.add).then_inc(weight_ready, 1)
                step(v.tensor_tensor(CB.rearrange("p (b e) -> p b e", e=E),
                                     const("iota_b")[:, 0:NB].unsqueeze(2).to_broadcast([P, NB, E]),
                                     BINC.unsqueeze(1).to_broadcast([P, NB, E]), ALU.is_ge))
                step.settle()
                step(v.tensor_reduce(EOF, CB.rearrange("p (b e) -> p b e", e=E), AX.X, ALU.add))
                step.settle()
                step(v.tensor_scalar(eob[:, :], EOF, float(E - 1), None, ALU.min))
                if f == 0:
                    scales(0)
                dve.wait_ge(table_psum, f + 1)
                step(v.tensor_copy(RF, bank[3][:, NT:2 * NT]))
                step.settle()
                step(v.scalar_tensor_tensor(BIG, RF, 0.0, const("pad_place"), ALU.is_equal, ALU.mult))
                step(v.scalar_tensor_tensor(PF, RF, float(P), bank[3][:, 0:NT], ALU.mult, ALU.add))
                step.settle()
                step(v.scalar_tensor_tensor(place[:, :], PF, float(-P), BIG, ALU.add, ALU.add))
                step.settle()
                v.tensor_scalar(token[:, :], place[:, :], T * P - 1, None, ALU.bitwise_and).then_inc(table_ready, 1)
                dve.wait_ge(counted, 2 * f + 2)
                step(v.tensor_reduce(wexp[:, :], bank[2][:, 0:T * E].rearrange("p (i e) -> p e i", e=E), AX.X,
                                     ALU.add))
                step(v.tensor_scalar(cntm, cnt.rearrange("p e i -> p (e i)"), 1.0, None, ALU.max))
                step.settle()
                step(v.reciprocal(cntm, cntm))
                step.settle()
                v.tensor_tensor(wexp[:, :], wexp[:, :], cntm, ALU.mult).then_inc(w_ready, 1)

            def blocks(f):
                v = nc.vector
                dve.wait_ge(w_ready, f + 1)
                step(v.tensor_tensor(wsc[:, :], wexp[:, :], dsc[:, :], ALU.mult))
                step.settle()

                def low(b, q):
                    dve.wait_ge(xh_ready, f * NB + b + 1)
                    v.scalar_tensor_tensor(XL[q], TB, X_SCALE, XH[q], ALU.mult,
                                           ALU.subtract).then_inc(xl_ready, 1)

                def split(b, q):
                    dve.wait_ge(relu_done, FREE + f * NB + b + 1)
                    dve.wait_ge(layer2, f * NB + b + 1)
                    v.tensor_copy(HH[q], HF[q]).then_inc(hh_ready, 1)
                    dve.wait_ge(hh_ready, f * NB + b + 1)
                    v.tensor_tensor(HL[q], HF[q], HH[q], ALU.subtract).then_inc(hl_ready, 1)

                def weigh(b, q):
                    e = dve.value_load(eob[0:1, bass.ds(b, 1)], min_val=0, max_val=E - 1)
                    dve.wait_ge(layer2, FREE + f * NB + b + 1)
                    if not isinstance(b, int) or b >= 2:
                        dve.wait_ge(y_sent[q], sent(f, b, q))
                    for u in range(W):
                        ins = v.scalar_tensor_tensor(YO[q][:, u * D:(u + 1) * D], bank[7][:, u * D:(u + 1) * D],
                                                     wsc[:, bass.ds(e, 1)], b2w[:, bass.ds(e * D, D)],
                                                     ALU.mult, ALU.add)
                    ins.then_inc(y_ready, 1)

                low(0, 0)
                low(1, 1)
                split(0, 0)
                for u in range(2):
                    low(u + 2, u)
                    split(u + 1, 1 - u)
                    if u == 0:
                        dve.wait_ge(b2w_ready, (1, 3)[f])
                    weigh(u, u)
                with dve.Fori(1, (NB - 3) // 2) as j:
                    for u in range(2):
                        low(j * 2 + (u + 2), u)
                        split(j * 2 + (u + 1), 1 - u)
                        weigh(j * 2 + u, u)
                low(NB - 1, 0)
                split(NB - 2, 1)
                weigh(NB - 3, 0)
                split(NB - 1, 0)
                weigh(NB - 2, 1)
                weigh(NB - 1, 0)

            def sent(f, b, q):
                base = 16 * W * f * TURNS[q]
                return (b - q) // 2 * 16 * W + base if isinstance(b, int) else (b - q) * (8 * W) + base

            def combine(f):
                v = nc.vector
                Oc = O.rearrange("p (c b) d -> p c (b d)", c=NC)
                for c in range(1, NC):
                    if c == 1:
                        dve.wait_ge(sums_in[0], 16 * (f + 1))
                    dve.wait_ge(sums_in[c], 16 * (f + 1))
                    if c > 1:
                        dve.wait_ge(chunks_added, (NC - 1) * f + c - 1)
                    v.tensor_tensor(BSUM, Oc[:, 0] if c == 1 else BSUM, Oc[:, c], ALU.add).then_inc(chunks_added, 1)
                dve.wait_ge(pool_psum, f + 1)
                v.tensor_scalar(pooled[:, :], bank[1][:, 0:KC * B], 1.0 / N, None, ALU.mult).then_inc(pool_ready, 1)
                dve.wait_ge(phi_exp, f + 1)
                step(v.tensor_scalar(gate[:, :], gate[:, :], 1.0, None, ALU.add))
                step.settle()
                step(v.reciprocal(gate[:, :], gate[:, :]))
                step.settle()
                step(v.tensor_scalar(gate[:, :], gate[:, :], 0.7, None, ALU.is_gt))
                step.settle()
                step(v.tensor_scalar(gate[:, :], gate[:, :], -0.4, 0.5, ALU.mult, ALU.add))
                step.settle()
                Ob = O.rearrange("p (c b) d -> p c b d", b=B)

                def updated(chunks, count):
                    for b in range(B):
                        v.scalar_tensor_tensor(Xc[:, chunks, b], Ob[:, chunks, b], gate[:, b:b + 1], Xc[:, chunks, b],
                                               ALU.mult, ALU.add).then_inc(x_new, 1)
                    dve.wait_ge(x_new, count)

                if f == 0:
                    updated(slice(0, 1), B)
                    row_stats(1, 0, B)
                    updated(slice(1, NC), 2 * B)
                else:
                    updated(slice(0, NC), 3 * B)

            def attention():
                v = nc.vector
                dve.wait_ge(a_s0, 1)
                dve.wait_ge(dmask_in, 16)

                def queries(t):
                    for g in range(G):
                        dve.wait_ge(a_qk, t * 4 + (2 * g + 2))
                        v.tensor_scalar(QE[:, g], QR[:, g], const("even"), None, ALU.mult)
                        v.tensor_scalar(QO[:, g], QR[:, g], const("odd"), None, ALU.mult).then_inc(a_q, 1)
                    v.tensor_tensor(QD, QR, const("decay_q").rearrange("p (g c) -> p g c", g=G),
                                    ALU.mult).then_inc(a_qd, 1)

                def masked(t, g):
                    dve.wait_ge(a_sc, t * 2 + (g + 2))
                    dve.wait_ge(a_pv, t * 2 + (g + 1))
                    v.tensor_tensor(PM[g].rearrange("p r s c -> p r (s c)"), PS[:, 0:4, 0:2 * P],
                                    dmask_s[:, g].rearrange("p r s c -> p r (s c)"), ALU.mult).then_inc(a_p, 1)

                def values_keys(t):
                    dve.wait_ge(a_kv, t + 3)
                    dve.wait_ge(a_pv, t * 2 + 2)
                    v.tensor_tensor(V2m[:, :, 0:4:3, :], bank[5][:, 0:D].rearrange("p (q s d) -> p q s d", s=2, d=HD),
                                    bv_s.rearrange("p (q s d) -> p q s d", s=2, d=HD), ALU.add).then_inc(a_ve, 1)
                    v.tensor_tensor(KD, bank[5][:, D:2 * D], const("decay_k"), ALU.mult).then_inc(a_kd, 1)

                def state(t, b):
                    dve.wait_ge(a_st, t + 1)
                    v.tensor_tensor(TMP, bank[7][:, 0:G * P].rearrange("p (g e) -> p g e", g=G),
                                    const("diag").unsqueeze(1).to_broadcast([P, G, P]), ALU.mult).then_inc(a_tmp, 1)
                    dve.wait_ge(a_tmp, t + 1)
                    for g in range(G):
                        ins = v.scalar_tensor_tensor(S[:, b, g, :], S[:, b, g, :], const("decay_chunk")[:, g:g + 1],
                                                     TMP[:, g, :], ALU.mult, ALU.add)
                    ins.then_inc(a_s, 1)

                def residual(t):
                    dve.wait_ge(a_xb, t + 1)
                    dve.wait_ge(a_out, t + 2)
                    xi = X[:, bass.ds(t, 1), :].rearrange("p a d -> p (a d)")
                    v.tensor_tensor(xi, bank[7][:, D:2 * D], xi, ALU.add).then_inc(a_x, 1)
                    dve.wait_ge(a_x, t + 2)
                    v.bn_stats(stats[:, bass.ds(t, 1), :].rearrange("p a s -> p (a s)"), xi).then_inc(a_bn, 1)

                def stats_ahead(t):
                    col = bass.ds(t + B, 1)
                    flat = "p a s -> p (a s)"
                    v.bn_stats(stats_next[:, :], X[:, col, :].rearrange(flat)).then_inc(a_stat, 1)
                    dve.wait_ge(a_stat, t * 3 + 1)
                    dve.sem_inc(dve_held, 1)
                    v.bn_aggr(mv_next[:, :], stats_next[:, :]).then_inc(a_stat, 1)
                    dve.wait_ge(a_stat, t * 3 + 2)
                    v.tensor_scalar(nmr[:, col], mv_next[:, 1:2], EPS, None, ALU.add).then_inc(var_ready, 1)

                def scales_ahead(t):
                    col = bass.ds(t + B, 1)
                    dve.wait_ge(sd_ready, t + 3)
                    v.reciprocal(rstd[:, col], rstd[:, col]).then_inc(a_stat, 1)
                    dve.wait_ge(a_stat, t * 3 + 3)
                    v.scalar_tensor_tensor(nmr[:, col], mv_next[:, 0:1], -1.0,
                                           rstd[:, col], ALU.mult, ALU.mult).then_inc(rstd_ready, 1)

                def tile(t, b, last=False):
                    values_keys(t)
                    if not last:
                        stats_ahead(t)
                    masked(t, 1)
                    if not (last and b == B - 1):
                        queries(t + 1)
                    state(t, b)
                    if not (last and b == B - 1):
                        masked(t + 1, 0)
                    if not last:
                        scales_ahead(t)
                    residual(t)

                queries(0)
                masked(0, 0)
                with dve.Fori(0, NC - 1) as c:
                    for b in range(B):
                        tile(c * B + b, b)
                for b in range(B):
                    tile((NC - 1) * B + b, b, last=True)
                dve.wait_ge(a_bn, T)

            dve.sem_inc(a_p, 1)
            dve.sem_inc(a_kd, 1)
            dve.sem_inc(a_qd, 1)
            dve.sem_inc(a_s, 4)
            dve.sem_inc(a_x, 1)
            dve.sem_inc(w_lo, 4)
            dve.sem_inc(xl_ready, FREE)
            dve.sem_inc(hl_ready, FREE)
            dve.sem_inc(y_ready, FREE)
            for f in calls:
                routing(f)
                if f == 0:
                    low_parts(0, E // 2)
                    scales(1)
                    low_parts(E // 2, E)
                    bias_scales()
                blocks(f)
                combine(f)
                if f == 0:
                    attention()


def kernel(L0_attn_x, L0_attn_w_qkv, L0_attn_b_qkv, L0_attn_w_out, L0_attn_b_out, L0_ffn_Wr, L0_ffn_br,
           L0_ffn_w1, L0_ffn_b1, L0_ffn_w2, L0_ffn_b2, L0_ffn_Wp1, L0_ffn_bp1, L0_ffn_Wp2, L0_ffn_bp2):
    import concourse.bacc as bacc
    from concourse.bass_utils import run_bass_kernel_spmd

    nc, arrays = program(dict(
        x=L0_attn_x, w_qkv=L0_attn_w_qkv, b_qkv=L0_attn_b_qkv, w_out=L0_attn_w_out, b_out=L0_attn_b_out,
        Wr=L0_ffn_Wr, br=L0_ffn_br, w1=L0_ffn_w1, b1=L0_ffn_b1, w2=L0_ffn_w2, b2=L0_ffn_b2,
        Wp1=L0_ffn_Wp1, bp1=L0_ffn_bp1, Wp2=L0_ffn_Wp2, bp2=L0_ffn_bp2), bacc)
    r = run_bass_kernel_spmd(nc, [arrays], core_ids=[0])
    return r.results[0]["out"]


def program(a, bacc):
    a = {k: np.asarray(v) for k, v in a.items()}
    cst, dmask = constants()
    arrays = {
        "x": a["x"], "w_qkvT": a["w_qkv"].T, "b_qkv": a["b_qkv"],
        "b_qkT": a["b_qkv"][:2 * D].reshape(2 * G, P).T, "w_outT": a["w_out"].T, "b_out": a["b_out"],
        "Wr": a["Wr"], "br": a["br"], "w1": a["w1"],
        "b1T": a["b1"].reshape(E, IC, P).transpose(2, 0, 1).reshape(P, E * IC),
        "w2": a["w2"], "b2": a["b2"], "Wp1": a["Wp1"], "bp1": a["bp1"], "Wp2": a["Wp2"], "bp2": a["bp2"],
        "cst": cst, "dmask": dmask,
    }
    arrays = {k: np.ascontiguousarray(v) for k, v in arrays.items()}
    nc = bacc.Bacc("TRN2", target_bir_lowering=False, num_devices=1)
    args = [nc.dram_tensor(k, v.shape, mybir.dt.from_np(v.dtype), kind="ExternalInput").ap()
            for k, v in arrays.items()]
    xn_dram = nc.dram_tensor("xn_rows", (T * P, D), F32, kind="Internal").ap()
    sums_dram = [nc.dram_tensor(f"expert_sums{f}", (TOKENS + SPARE, D), F32, kind="Internal").ap() for f in range(2)]
    out = nc.dram_tensor("out", (B, N, D), F32, kind="ExternalOutput").ap()
    build(nc, *args, xn_dram, sums_dram, out)
    return nc, arrays
```
